# Optimizing a Trainium2 kernel written in Bass

```python
import numpy as np
import jax
import jax.numpy as jnp

def _softmax(x, axis=-1):
    return jax.nn.softmax(x, axis=axis)

def _gelu(x):
    return jax.nn.gelu(x, approximate=True)

def _silu(x):
    return jax.nn.silu(x)

def _sigmoid(x):
    return jax.nn.sigmoid(x)

def _layernorm(x, axis=-1, eps=1e-05):
    m = jnp.mean(x, axis=axis, keepdims=True)
    v = jnp.var(x, axis=axis, keepdims=True)
    return (x - m) / jnp.sqrt(v + eps)

def _scatter_add(tgt, idx, src, axis=0):
    return tgt.at[idx].add(src)

def _segment_sum(src, seg, n):
    return jax.ops.segment_sum(src, seg, n)
kernel_name = 'mk_adaln_attn_ffn_d1_seqx_r8_e2ea29'

def setup_inputs(seed: int=0):
    np.random.seed(seed)
    _w = jnp.asarray

    def _rec_inputs():
        import jax
        import jax.numpy as jnp
        _rk = jax.random.key(seed)
        x = 7.22e-05 + 1 * jax.random.normal(jax.random.fold_in(_rk, 1), (8, 128, 128), jnp.float32)
        _lenS = 128 - jax.random.randint(jax.random.fold_in(_rk, 7), (8,), 0, max(1, 128 // 4) + 1, jnp.int32)
        _lenS2 = 128 - jax.random.randint(jax.random.fold_in(_rk, 8), (8,), 0, max(1, 128 // 4) + 1, jnp.int32)
        fside_BxSxS_0 = 4.13588e-05 + 0.999923 * jax.random.normal(jax.random.fold_in(_rk, 11), (8, 128, 128), jnp.float32)
        itok_B_18_1004 = jax.random.randint(jax.random.fold_in(_rk, 12), (8,), 18, 1005, jnp.int32)
        condB_tauraws = -5.74692 + 0.777674 * jax.random.normal(jax.random.fold_in(_rk, 13), (8,), jnp.float32)
        cond_256 = -0.000235209 + 0.019331 * jax.random.normal(jax.random.fold_in(_rk, 14), (8, 32), jnp.float32)
        condB_bn2 = jnp.zeros((8,), jnp.float32)
        cond_1024 = -4.10585e-05 + 0.0199478 * jax.random.normal(jax.random.fold_in(_rk, 16), (8, 128), jnp.float32)
        return (x, fside_BxSxS_0, itok_B_18_1004, condB_tauraws, cond_256, condB_bn2, cond_1024)
    x, fside_BxSxS_0, itok_B_18_1004, condB_tauraws, cond_256, condB_bn2, cond_1024 = _rec_inputs()

    def _L0_cond_setup():
        import jax, jax.numpy as jnp
        import numpy as np
        B, L1, L2, DIN, DOUT, H = (8, 128, 128, 128, 128, 16)
        DH = DOUT // H
        SCALE = 1.0 / np.sqrt(DH).astype(np.float32)
        key = jax.random.key(seed)
        ks = jax.random.split(key, 13)
        s = 0.02
        return {'seq1': jax.random.normal(ks[0], (B, L1, DIN), jnp.float32), 'seq2': jax.random.normal(ks[1], (B, L2, DIN), jnp.float32), 'seq_len1': jax.random.randint(ks[2], (B,), 1, L1 + 1, jnp.int32), 'Wq': jax.random.normal(ks[3], (DIN, DOUT), jnp.float32) * s, 'bq': jnp.zeros((DOUT,), jnp.float32), 'Wk': jax.random.normal(ks[4], (DIN, DOUT), jnp.float32) * s, 'bk': jnp.zeros((DOUT,), jnp.float32), 'Wv': jax.random.normal(ks[5], (DIN, DOUT), jnp.float32) * s, 'bv': jnp.zeros((DOUT,), jnp.float32), 'Wo': jax.random.normal(ks[6], (DOUT, DOUT), jnp.float32) * s, 'bo': jnp.zeros((DOUT,), jnp.float32), 'b_prev': jax.random.normal(ks[7], (1, 1, DIN), jnp.float32) * s, 'b_self': jax.random.normal(ks[8], (1, 1, DIN), jnp.float32) * s}
    _L0_cond_all = _L0_cond_setup()
    _L0_cond_in = {k: v for k, v in _L0_cond_all.items() if k in ('Wq', 'bq', 'Wk', 'bk', 'Wv', 'bv', 'Wo', 'bo', 'b_prev', 'b_self')}
    del _L0_cond_all

    def _L0_attn_setup():
        import jax, jax.numpy as jnp
        import numpy as np
        import math
        DIM = 128
        WINDOW = 16
        NUM_HEADS = 16
        HEAD_DIM = DIM // NUM_HEADS
        SCALE = math.sqrt(HEAD_DIM)
        LN_EPS = 1e-05

        def _gather_window(z, W):
            B, T, H, C = z.shape
            t = jnp.arange(T)[:, None]
            w = jnp.arange(W)[None, :]
            idx = t - 1 - w
            valid = idx >= 0
            idxc = jnp.clip(idx, 0, T - 1)
            nb = z[:, idxc]
            nb = jnp.where(valid[None, :, :, None, None], nb, jnp.zeros((), z.dtype))
            return nb.transpose(0, 1, 3, 2, 4)
        key = jax.random.key(seed)
        k0, k1, k2, k3 = jax.random.split(key, 4)
        B, T, D = (2, 512, DIM)
        x = jax.random.normal(k0, (B, T, D), dtype=jnp.float32)
        wq = jax.random.normal(k1, (D, D), dtype=jnp.float32) * 0.02
        wkv = jax.random.normal(k2, (2 * D, D), dtype=jnp.float32) * 0.02
        wo = jax.random.normal(k3, (D, D), dtype=jnp.float32) * 0.02
        gamma = jnp.ones((D,), dtype=jnp.float32)
        beta = jnp.zeros((D,), dtype=jnp.float32)
        return {'x': x, 'wq': wq, 'wkv': wkv, 'wo': wo, 'gamma': gamma, 'beta': beta}
    _L0_attn_all = _L0_attn_setup()
    _L0_attn_in = {k: v for k, v in _L0_attn_all.items() if k in ('wq', 'wkv', 'wo', 'gamma', 'beta')}
    del _L0_attn_all

    def _L0_cond2_setup():
        import jax, jax.numpy as jnp
        import numpy as np
        import math
        B, T, E, D = (4, 256, 128, 4)

        def _tau_init(t):
            a = 0.1 ** (1.0 / max(t - 1, 1))
            tt = -math.log(max(a, 1e-10))
            return math.log(math.exp(tt) - 1 + 1e-10)

        def causal_ema(b, tau_raw):
            alpha = jnp.exp(-jax.nn.softplus(tau_raw)).astype(b.dtype)

            def step(h, bt):
                h = alpha * h + bt
                return (h, h)
            h0 = jnp.zeros((b.shape[0], b.shape[2]), b.dtype)
            _, hs = jax.lax.scan(step, h0, jnp.swapaxes(b, 0, 1))
            return jnp.swapaxes(hs, 0, 1)
        key = jax.random.key(seed)
        ks = jax.random.split(key, 10)
        s = 0.02
        return {'x': jax.random.normal(ks[0], (B, T, E), jnp.float32), 'tau_ctx': jnp.float32(_tau_init(max(T // 2, 4))), 'tau_raws': jnp.array([_tau_init(max(T // 2 ** i, 2)) for i in range(D)], jnp.float32), 'Wg': jax.random.normal(ks[1], (E, 2 * E), jnp.float32) * s, 'bg': jnp.full((E,), -0.5, jnp.float32), 'Wn1': jax.random.normal(ks[2], (E // 4, E), jnp.float32) * s, 'bn1': jnp.zeros((E // 4,), jnp.float32), 'Wn2': jax.random.normal(ks[3], (D, E // 4), jnp.float32) * s, 'bn2': jnp.zeros((D,), jnp.float32), 'blend': jax.random.normal(ks[4], (D, E), jnp.float32) * s, 'Wsoma': jax.random.normal(ks[5], (E, E), jnp.float32) * s, 'bsoma': jnp.zeros((E,), jnp.float32), 'Wtemp': jax.random.normal(ks[6], (E, E), jnp.float32) * s, 'btemp': jnp.zeros((E,), jnp.float32), 'Wout': jax.random.normal(ks[7], (E, E), jnp.float32) * s, 'gamma': jnp.ones((E,), jnp.float32), 'beta': jnp.zeros((E,), jnp.float32)}
    _L0_cond2_all = _L0_cond2_setup()
    _L0_cond2_in = {k: v for k, v in _L0_cond2_all.items() if k in ('tau_ctx', 'Wg', 'bg', 'Wn1', 'bn1', 'Wsoma', 'bsoma', 'Wtemp', 'btemp', 'Wout', 'gamma', 'beta')}
    del _L0_cond2_all

    def _L0_ffn_setup():
        import jax, jax.numpy as jnp
        import numpy as np
        B, S, D, F, E = (4, 256, 128, 512, 8)
        key = jax.random.key(seed)
        ks = jax.random.split(key, 7)
        s1 = 1.0 / np.sqrt(D)
        s2 = 1.0 / np.sqrt(F)
        x = jax.random.normal(ks[0], (B, S, D), dtype=jnp.float32)
        W1 = jax.random.uniform(ks[1], (E, D, F), jnp.float32, -s1, s1)
        b1 = jax.random.uniform(ks[2], (E, F), jnp.float32, -s1, s1)
        W2 = jax.random.uniform(ks[3], (E, F, D), jnp.float32, -s2, s2)
        b2 = jax.random.uniform(ks[4], (E, D), jnp.float32, -s2, s2)
        Wr = jax.random.uniform(ks[5], (D, E), jnp.float32, -s1, s1)
        br = jax.random.uniform(ks[6], (E,), jnp.float32, -s1, s1)
        return {'x': x, 'W1': W1, 'b1': b1, 'W2': W2, 'b2': b2, 'Wr': Wr, 'br': br}
    _L0_ffn_all = _L0_ffn_setup()
    _L0_ffn_in = {k: v for k, v in _L0_ffn_all.items() if k in ('W1', 'b1', 'W2', 'b2', 'Wr', 'br')}
    del _L0_ffn_all
    return {'x': x, 'fside_BxSxS_0': fside_BxSxS_0, 'itok_B_18_1004': itok_B_18_1004, 'condB_tauraws': condB_tauraws, 'cond_256': cond_256, 'condB_bn2': condB_bn2, 'cond_1024': cond_1024, 'L0_cond_Wq': _L0_cond_in['Wq'], 'L0_cond_bq': _L0_cond_in['bq'], 'L0_cond_Wk': _L0_cond_in['Wk'], 'L0_cond_bk': _L0_cond_in['bk'], 'L0_cond_Wv': _L0_cond_in['Wv'], 'L0_cond_bv': _L0_cond_in['bv'], 'L0_cond_Wo': _L0_cond_in['Wo'], 'L0_cond_bo': _L0_cond_in['bo'], 'L0_cond_b_prev': _L0_cond_in['b_prev'], 'L0_cond_b_self': _L0_cond_in['b_self'], 'L0_attn_wq': _L0_attn_in['wq'], 'L0_attn_wkv': _L0_attn_in['wkv'], 'L0_attn_wo': _L0_attn_in['wo'], 'L0_attn_gamma': _L0_attn_in['gamma'], 'L0_attn_beta': _L0_attn_in['beta'], 'L0_cond2_tau_ctx': _L0_cond2_in['tau_ctx'], 'L0_cond2_Wg': _L0_cond2_in['Wg'], 'L0_cond2_bg': _L0_cond2_in['bg'], 'L0_cond2_Wn1': _L0_cond2_in['Wn1'], 'L0_cond2_bn1': _L0_cond2_in['bn1'], 'L0_cond2_Wsoma': _L0_cond2_in['Wsoma'], 'L0_cond2_bsoma': _L0_cond2_in['bsoma'], 'L0_cond2_Wtemp': _L0_cond2_in['Wtemp'], 'L0_cond2_btemp': _L0_cond2_in['btemp'], 'L0_cond2_Wout': _L0_cond2_in['Wout'], 'L0_cond2_gamma': _L0_cond2_in['gamma'], 'L0_cond2_beta': _L0_cond2_in['beta'], 'L0_ffn_W1': _L0_ffn_in['W1'], 'L0_ffn_b1': _L0_ffn_in['b1'], 'L0_ffn_W2': _L0_ffn_in['W2'], 'L0_ffn_b2': _L0_ffn_in['b2'], 'L0_ffn_Wr': _L0_ffn_in['Wr'], 'L0_ffn_br': _L0_ffn_in['br']}

def reference(x, fside_BxSxS_0, itok_B_18_1004, condB_tauraws, cond_256, condB_bn2, cond_1024, L0_cond_Wq, L0_cond_bq, L0_cond_Wk, L0_cond_bk, L0_cond_Wv, L0_cond_bv, L0_cond_Wo, L0_cond_bo, L0_cond_b_prev, L0_cond_b_self, L0_attn_wq, L0_attn_wkv, L0_attn_wo, L0_attn_gamma, L0_attn_beta, L0_cond2_tau_ctx, L0_cond2_Wg, L0_cond2_bg, L0_cond2_Wn1, L0_cond2_bn1, L0_cond2_Wsoma, L0_cond2_bsoma, L0_cond2_Wtemp, L0_cond2_btemp, L0_cond2_Wout, L0_cond2_gamma, L0_cond2_beta, L0_ffn_W1, L0_ffn_b1, L0_ffn_W2, L0_ffn_b2, L0_ffn_Wr, L0_ffn_br):
    import jax
    import jax.numpy as jnp

    def _L0_cond_ref(seq1, seq2, seq_len1, Wq, bq, Wk, bk, Wv, bv, Wo, bo, b_prev, b_self):
        import jax, jax.numpy as jnp
        import numpy as np
        B, L1, L2, DIN, DOUT, H = (8, 128, 128, 128, 128, 16)
        DH = DOUT // H
        SCALE = 1.0 / np.sqrt(DH).astype(np.float32)
        b, l1, _ = seq1.shape
        l2 = seq2.shape[1]
        query = seq2 + b_self
        key = jnp.concatenate([seq1 + b_prev, seq2 + b_self], 1)
        value = jnp.concatenate([seq1, seq2], 1)
        q = (query @ Wq + bq).reshape(b, l2, H, DH).transpose(0, 2, 1, 3)
        k = (key @ Wk + bk).reshape(b, l1 + l2, H, DH).transpose(0, 2, 1, 3)
        v = (value @ Wv + bv).reshape(b, l1 + l2, H, DH).transpose(0, 2, 1, 3)
        score_prev = jnp.einsum('bhqd,bhkd->bhqk', q, k[:, :, :l1]) * SCALE
        score_self = (q * k[:, :, l1:]).sum(-1, keepdims=True) * SCALE
        mask = jnp.arange(l1)[None, :] < seq_len1[:, None]
        score_prev = jnp.where(mask[:, None, None, :], score_prev, -jnp.inf)
        score = jnp.concatenate([score_prev, score_self], -1)
        weights = jax.nn.softmax(score, axis=-1)
        attn = jnp.einsum('bhqk,bhkd->bhqd', weights[..., :-1], v[:, :, :l1])
        attn = attn + weights[..., -1:] * v[:, :, l1:]
        attn = attn.transpose(0, 2, 1, 3).reshape(b, l2, H * DH)
        return attn @ Wo + bo

    def _L0_attn_ref(x, wq, wkv, wo, gamma, beta):
        import jax, jax.numpy as jnp
        import numpy as np
        import math
        DIM = 128
        WINDOW = 16
        NUM_HEADS = 16
        HEAD_DIM = DIM // NUM_HEADS
        SCALE = math.sqrt(HEAD_DIM)
        LN_EPS = 1e-05

        def _gather_window(z, W):
            B, T, H, C = z.shape
            t = jnp.arange(T)[:, None]
            w = jnp.arange(W)[None, :]
            idx = t - 1 - w
            valid = idx >= 0
            idxc = jnp.clip(idx, 0, T - 1)
            nb = z[:, idxc]
            nb = jnp.where(valid[None, :, :, None, None], nb, jnp.zeros((), z.dtype))
            return nb.transpose(0, 1, 3, 2, 4)
        B, T, D = x.shape
        H, HD, W = (NUM_HEADS, HEAD_DIM, WINDOW)
        q = (x @ wq.T).reshape(B, T, H, HD)
        kv = (x @ wkv.T).reshape(B, T, H, 2 * HD)
        nb_kv = _gather_window(kv, W)
        nb_k, nb_v = (nb_kv[..., :HD], nb_kv[..., HD:])
        tau = jax.nn.sigmoid(jnp.einsum('bthd,bthwd->bthw', q, nb_k) / SCALE)
        msg = jnp.einsum('bthw,bthwd->bthd', tau, nb_v)
        y = x + msg.reshape(B, T, D) @ wo.T
        mu = jnp.mean(y, axis=-1, keepdims=True)
        var = jnp.mean((y - mu) ** 2, axis=-1, keepdims=True)
        out = (y - mu) * jax.lax.rsqrt(var + LN_EPS) * gamma + beta
        return out

    def _L0_cond2_ref(x, tau_ctx, tau_raws, Wg, bg, Wn1, bn1, Wn2, bn2, blend, Wsoma, bsoma, Wtemp, btemp, Wout, gamma, beta):
        import jax, jax.numpy as jnp
        import numpy as np
        import math
        B, T, E, D = (4, 256, 128, 4)

        def _tau_init(t):
            a = 0.1 ** (1.0 / max(t - 1, 1))
            tt = -math.log(max(a, 1e-10))
            return math.log(math.exp(tt) - 1 + 1e-10)

        def causal_ema(b, tau_raw):
            alpha = jnp.exp(-jax.nn.softplus(tau_raw)).astype(b.dtype)

            def step(h, bt):
                h = alpha * h + bt
                return (h, h)
            h0 = jnp.zeros((b.shape[0], b.shape[2]), b.dtype)
            _, hs = jax.lax.scan(step, h0, jnp.swapaxes(b, 0, 1))
            return jnp.swapaxes(hs, 0, 1)
        ctx = causal_ema(x, tau_ctx)
        gate_in = jnp.concatenate([x, ctx], axis=-1)
        wg = jax.nn.sigmoid(jnp.einsum('btc,ec->bte', gate_in, Wg) + bg)
        gated = x * wg
        h1 = jax.nn.gelu(jnp.einsum('btc,hc->bth', x, Wn1) + bn1, approximate=False)
        mod = 0.5 + jax.nn.sigmoid(jnp.einsum('bth,dh->btd', h1, Wn2) + bn2)
        traces = jax.vmap(lambda tau, m: causal_ema(gated * m[..., None], tau))(tau_raws, jnp.moveaxis(mod, -1, 0))
        blend_w = jax.nn.softmax(blend, axis=0)
        temporal = jnp.einsum('dbtc,dc->btc', traces, blend_w)
        gate = jax.nn.sigmoid(jnp.einsum('btc,ec->bte', temporal, Wtemp) + btemp)
        soma = jax.nn.gelu(jnp.einsum('btc,ec->bte', x, Wsoma) + bsoma, approximate=False)
        out = jnp.einsum('btc,ec->bte', soma * gate, Wout)
        mu = out.mean(-1, keepdims=True)
        var = out.var(-1, keepdims=True)
        return (out - mu) / jnp.sqrt(var + 1e-05) * gamma + beta

    def _L0_ffn_ref(x, W1, b1, W2, b2, Wr, br):
        import jax, jax.numpy as jnp
        import numpy as np
        B, S, D, F, E = (4, 256, 128, 512, 8)
        b, s, d = x.shape
        e = Wr.shape[1]
        logits = x @ Wr + br
        idx = jnp.argmax(logits, axis=-1)
        probs = jax.nn.softmax(logits, axis=-1)
        gates = jnp.take_along_axis(probs, idx[..., None], axis=-1)[..., 0]
        xf = x.reshape(-1, d)
        idxf = idx.reshape(-1)
        gf = gates.reshape(-1)
        out = jnp.zeros_like(xf)
        for ei in range(e):
            h = jax.nn.gelu(xf @ W1[ei] + b1[ei], approximate=False)
            y = h @ W2[ei] + b2[ei]
            mask = (idxf == ei).astype(xf.dtype)
            out = out + y * (gf * mask)[:, None]
        return out.reshape(b, s, d)
    x = x + _L0_attn_ref(_L0_cond_ref(x, fside_BxSxS_0, itok_B_18_1004, L0_cond_Wq, L0_cond_bq, L0_cond_Wk, L0_cond_bk, L0_cond_Wv, L0_cond_bv, L0_cond_Wo, L0_cond_bo, L0_cond_b_prev, L0_cond_b_self), L0_attn_wq, L0_attn_wkv, L0_attn_wo, L0_attn_gamma, L0_attn_beta)
    x = x + _L0_ffn_ref(_L0_cond2_ref(x, L0_cond2_tau_ctx, condB_tauraws, L0_cond2_Wg, L0_cond2_bg, L0_cond2_Wn1, L0_cond2_bn1, cond_256, condB_bn2, cond_1024, L0_cond2_Wsoma, L0_cond2_bsoma, L0_cond2_Wtemp, L0_cond2_btemp, L0_cond2_Wout, L0_cond2_gamma, L0_cond2_beta), L0_ffn_W1, L0_ffn_b1, L0_ffn_W2, L0_ffn_b2, L0_ffn_Wr, L0_ffn_br)
    return x

_drawn_inputs = setup_inputs


def setup_inputs(seed=0):
    import zlib

    import numpy as np

    out = dict(_drawn_inputs(seed))
    spreads = {'condB_bn2': (0.0, 2.0),
     'L0_cond_bq': (0.0, 0.8),
     'L0_cond_bk': (0.0, 2.0),
     'L0_cond_bv': (0.0, 0.1),
     'L0_cond_bo': (0.0, 0.1),
     'L0_attn_gamma': (1.0, 0.2),
     'L0_attn_beta': (0.0, 0.1),
     'L0_cond2_bg': (-0.5, 0.6),
     'L0_cond2_bn1': (0.0, 2.0),
     'L0_cond2_bsoma': (0.0, 0.312),
     'L0_cond2_btemp': (0.0, 0.8),
     'L0_cond2_gamma': (1.0, 0.6),
     'L0_cond2_beta': (0.0, 0.8)}
    factors = {'fside_BxSxS_0': 8.0,
     'condB_tauraws': 8.0,
     'cond_256': 28.911,
     'cond_1024': 40.853,
     'L0_cond_Wq': 8.0,
     'L0_cond_Wk': 8.0,
     'L0_cond_b_prev': 8.0,
     'L0_cond_b_self': 8.0,
     'L0_attn_wq': 200.0,
     'L0_cond2_Wn1': 28.112,
     'L0_ffn_b1': 8.0,
     'L0_ffn_b2': 8.0,
     'L0_ffn_br': 4.618}
    for name, (base, spread) in spreads.items():
        noise = np.random.default_rng([zlib.crc32(name.encode()), seed]).standard_normal(out[name].shape)
        drawn = base * np.exp(spread * noise) if base else spread * noise
        out[name] = jnp.asarray(drawn.astype(out[name].dtype))
    for name, factor in factors.items():
        out[name] = (out[name] * factor).astype(out[name].dtype)
    return out
```

```python
from contextlib import ExitStack

import concourse.bass as bass
from concourse import mybir

ALU = mybir.AluOpType
ACT = mybir.ActivationFunctionType
AX = mybir.AxisListType
F32 = mybir.dt.float32
BF16 = mybir.dt.bfloat16
I32 = mybir.dt.int32
U32 = mybir.dt.uint32


def fused_layer(nc, A, out):
    NB, T, D = A["x"].shape
    H = 16
    DH = D // H
    G = H // 4
    HALF = NB // 2
    HT = HALF * T
    NT = NB * T
    WINDOW = 16
    NE, _, FF = A["L0_ffn_W1"].shape
    FC = FF // 128
    ND = A["cond_1024"].shape[0]
    NH1 = A["cond_256"].shape[1]
    TILES = NT // 128 + NE - 1
    SCALE = float(DH) ** -0.5
    MASKED = -1.0e30
    EPS = 1e-5
    Q_RUNS = ((0, 1, 3), (0, 1, 2), (0, 1, 1))
    K_RUNS = ((0, 0, 3), (1, 0, 2), (2, 0, 1))
    NSLOT = 6
    NPROD = NSLOT * DH
    KROWS = 96
    R0 = KROWS - NPROD
    RMASK = R0 - 1

    ctx = ExitStack()
    with ctx:
        sb = lambda name, shape, dt=F32: ctx.enter_context(nc.sbuf_tensor("t_" + name, shape, dt))
        sem = lambda name: ctx.enter_context(nc.semaphore(name))
        dram = lambda name, shape, dt=F32: nc.dram_tensor(name, shape, dt).ap()

        ident = sb("ident", [128, 128])
        identb = sb("identb", [128, 128], BF16)
        bandb = sb("bandb", [128, 128], BF16)
        onesb = sb("onesb", [128, 128], BF16)
        ones_row = sb("ones_row", [1, NT], BF16)
        mask_row = sb("mask_row", [1, NB, T], BF16)
        pos_row = sb("pos_row", [1, NB, T])
        len_i = sb("len_i", [1, NB], I32)
        len_f = sb("len_f", [1, NB])
        wqkv = sb("wqkv", [128, 3, D])
        wo = sb("wo", [128, D])
        bqkv_bc = sb("bqkv_bc", [128, 3, D])
        bo_bc = sb("bo_bc", [128, D])
        cols = sb("cols", [128, 12])
        BQ, BK, BPREV, BSELF, BO, BSOMA, BTEMP, BN1 = range(8)
        ecols = sb("ecols", [128, 2])

        x_tok = sb("x_tok", [128, NB, D])
        s2_tok = sb("s2_tok", [128, NB, D])
        xT = sb("xT", [128, NT])
        s2T = sb("s2T", [128, NT])
        qf = sb("qf", [128, 2, HT])
        parts = sb("parts", [128, 2, 3, HT], BF16)
        rest = sb("rest", [128, 2, HT])
        Qs_all = sb("Qs", [128, 2, H, HT], BF16)
        Ks_all = sb("Ks", [128, 2, H, HT], BF16)
        Qs, Ks = Qs_all[0:KROWS], Ks_all[0:KROWS]
        w_dh = sb("w_dh", [128, 2, D])
        b_dh = sb("b_dh", [1, 2, D])
        tokA = sb("tokA", [128, NB, 3, D])
        v_pad = sb("v_pad", [128, NB, H, 32])
        prod = sb("prod", [128, HALF, D])
        s_self = sb("s_self", [128, NB, H])
        mx = sb("mx", [128, NB, H])
        negm = sb("negm", [128, NB, H], BF16)
        sshift = sb("sshift", [128, NB, H])
        w_self = sb("w_self", [128, NB, H])
        P = sb("P", [128, 3, 512])
        pv_sb = sb("pv_sb", [128, 2, 512])
        den = sb("den", [128, 2, H])
        rden = sb("rden", [128, 2, H])
        wv = sb("wv", [128, 2, D])
        attn = sb("attn", [128, 2, D])
        attnT = sb("attnT", [128, NT])

        w_raw = sb("w_raw", [128, 3, D])
        wo_raw = sb("wo_raw", [128, D])
        wo_rp = sb("wo_rp", [128, H, 32])
        wB = sb("wB", [128, 3, D])
        woT = sb("woT", [128, G, D])
        y0T = sb("y0T", [128, NT])
        x1 = sb("x1", [128, NB, D])
        stats = sb("stats", [128, NB, 6])
        mv = sb("mv", [128, NB, 2])
        rstd = sb("rstd", [128, NB])
        mhalf = sb("mhalf", [128, NB])
        gamma1 = sb("gamma1", [128, D])
        beta1 = sb("beta1", [128, D])
        wc_raw = sb("wc_raw", [128, 5, D])
        wn1_raw = sb("wn1_raw", [NH1, D])
        wn2_raw = sb("wn2_raw", [ND, NH1])
        wC = sb("wC", [128, 6, D])
        wn1T = sb("wn1T", [128, NH1])
        wn2T = sb("wn2T", [NH1, ND])
        bg_bc = sb("bg_bc", [128, D])
        bn2_bc = sb("bn2_bc", [128, ND])
        blend = sb("blend", [128, ND, D])
        bl_small = sb("bl_small", [128, 2, D])
        tau = sb("tau", [128, ND + 1])
        tau2 = sb("tau2", [128, ND + 1])
        diff = sb("diff", [128, 128])
        ema = sb("ema", [128, ND + 1, 128])
        gamma2 = sb("gamma2", [128, D])
        beta2 = sb("beta2", [128, D])
        x1T = xT
        ctxT = s2T
        mod = sb("mod", [128, NB, ND])
        tempT = attnT
        somaT = y0T
        wr = sb("wr", [128, NE])
        br_bc = sb("br_bc", [128, NE])
        b_rest = sb("b_rest", [NE, FF + D])
        b_parts = sb("b_parts", [NE, 3, FF + D], BF16)
        lg = sb("lg", [128, NB, NE])
        lgm = sb("lgm", [128, NB])
        em8 = sb("em8", [128, NE])
        cand = sb("cand", [128, NB, NE])
        emin = sb("emin", [128, NB])
        onehot = sb("onehot", [128, NB, NE])
        onehotb = sb("onehotb", [128, 2 * NB, NE], BF16)
        gexp = sb("gexp", [128, NB, NE])
        gate = sb("gate", [128, NB])
        gsum = sb("gsum", [128, NB])
        trib = sb("trib", [128, 128], BF16)
        k128 = sb("k128", [128, NB])
        cmp = sb("cmp", [128, NE, NB])
        tiles_e = sb("tiles_e", [128, NE])
        tri8 = sb("tri8", [128, NE, NE])
        incl = sb("incl", [128, NE])
        excl = sb("excl", [128, NE])
        slotf = sb("slotf", [128, NB])
        slot = sb("slot", [128, NB], U32)
        tile_no = sb("tile_no", [1, TILES])
        tmap_c = sb("tmap_c", [1, TILES, NE])
        tmap_f = sb("tmap_f", [1, TILES])
        tmap = sb("tmap", [1, TILES], I32)
        zsT = sb("zsT", [128, 2, 128])
        zero_tile = sb("zero_tile", [128, D])

        flat = lambda buf, pattern: buf[:].rearrange(pattern)
        q_room = flat(Qs_all, "p a h t -> p (a h t)").bitcast(F32)
        k_room = flat(Ks_all, "p a h t -> p (a h t)").bitcast(F32)
        v_room = flat(v_pad, "p b h e -> p (b h e)")
        t_room = flat(tokA, "p b a c -> p (b a c)")
        cut3 = lambda room, at, n, m: room[:, at:at + n * m].rearrange("p (n m) -> p n m", n=n)
        Gb = q_room[:, 0:2 * ND * D].rearrange("p (k d c) -> p k d c", k=2, d=ND)
        at = 2 * ND * D
        gateT, zT, h1T = (q_room[:, at + i * NT:at + (i + 1) * NT] for i in range(3))
        h1T = h1T[0:NH1]
        at += 3 * NT
        o_sb, yg = (cut3(q_room, at + i * NB * D, NB, D) for i in range(2))
        hs = cut3(q_room, at + 2 * NB * D, 2, FF)
        W1 = cut3(k_room, 0, NE, FF)
        W2 = k_room[:, NE * FF:NE * (FF + FC * D)].rearrange("p (e k d) -> p e k d", e=NE, k=FC)
        zs = cut3(v_room, 0, TILES, D)
        hsT = cut3(v_room, TILES * D, 2, FF)
        wgate = cut3(v_room, TILES * D + 2 * FF, NB, D)
        b_rows = t_room.bitcast(BF16)[0:KROWS, 0:NE * (FF + D)].rearrange("p (e f) -> p e f", e=NE)
        b_raw = flat(s2_tok, "p b c -> p (b c)")[0:NE, 0:FF + D]
        z = s2_tok
        xb = x_tok
        ys = zs

        b_dram = dram("b_dram", (3, NE, FF + D), BF16)
        z_dram = dram("z_dram", (TILES * 128, D))
        y_dram = dram("y_dram", (TILES * 128, D))

        scr_parts = dram("scr_parts", (2, 2, 2, NSLOT, 128, HT), BF16)

        ps = [ctx.enter_context(nc.psum_tensor(f"ps{i}", [128, 512], F32)) for i in range(8)]
        S1B, S2B, PVB, MB = ps[0:2], ps[2:4], ps[4:6], ps[6:8]

        order = ["trS2_0", "trX_0", "bcols", "bbc", "qT_0", "kT_0"]
        order += [f"tok_{b}" for b in range(4)] + [f"vp_{b}" for b in range(4)]
        order += ["trS2_1", "trX_1", "qT_1", "kT_1"]
        order += [f"tok_{b}" for b in range(4, 8)] + [f"vp_{b}" for b in range(4, 8)]
        for i in range(NB + 2):
            order += {1: ["wB"], 2: ["wO"], 3: ["wC1"], 4: ["wC2"]}.get(i, [])
            if i == HALF + 2:
                order += ["bq_0", "bk_0"]
            if i >= 2:
                order += [f"pvtr_{i-2}", f"attnT_{i-2}"]
            if i == HALF + 1:
                order += ["y0T_0"]
            if i == HALF + 2:
                order += [f"bv_{b}" for b in range(HALF)]
        order += ["y0T_1", "bq_1", "bk_1"] + [f"bv_{b}" for b in range(HALF, NB)]
        order += [f"y_{b}" for b in range(NB)]
        for stage in ("x1T", "ctxT", "gate", "h1", "mod", "soma", "tg", "o", "zT", "lg"):
            order += [f"{stage}_0", f"{stage}_1"]
        order += ["rank"]
        job = {name: n for n, name in enumerate(order)}
        misc_full = [sem("misc_full0"), sem("misc_full1")]
        misc_read = [sem("misc_read0"), sem("misc_read1")]
        bank_of = lambda name: MB[job[name] % 2]

        def job_wait_free(eng, name):
            n = job[name]
            if n >= 2:
                eng.wait_ge(misc_read[n % 2], n // 2)

        def job_full(ins, name):
            ins.then_inc(misc_full[job[name] % 2], 1)

        def job_wait_full(eng, name):
            eng.wait_ge(misc_full[job[name] % 2], job[name] // 2 + 1)

        def job_read(ins, name):
            ins.then_inc(misc_read[job[name] % 2], 1)

        def job_wait_read(eng, name):
            eng.wait_ge(misc_read[job[name] % 2], job[name] // 2 + 1)

        ld_s2, ld_x, ld_wa, ld_cols, ld_len = sem("ld_s2"), sem("ld_x"), sem("ld_wa"), sem("ld_cols"), sem("ld_len")
        consts_ready = sem("consts_ready")
        vpad_zero = sem("vpad_zero")
        row_ready = sem("row_ready")
        ecols_ready = sem("ecols_ready")
        split_ready = sem("split_ready")
        parts_out = [sem("parts_out_q"), sem("parts_out_k")]
        stack_in = [sem(f"stack_in{i}") for i in range(2)]
        rows_in = sem("rows_in")
        s1_full, s1_read = sem("s1_full"), sem("s1_read")
        s2_full, s2_read = sem("s2_full"), sem("s2_read")
        pv_full, pv_read = sem("pv_full"), sem("pv_read")
        pv_done = sem("pv_done")
        negm_ready = sem("negm_ready")
        wself_ready = sem("wself_ready")
        sshift_ready = sem("sshift_ready")
        attn_ready = sem("attn_ready")
        tok_ready = sem("tok_ready")
        dve_step = sem("dve_step")
        pool_step = sem("pool_step")
        stack_zero = sem("stack_zero")
        wdh_ready = sem("wdh_ready")
        pool_pos = sem("pool_pos")
        rest_ready = sem("rest_ready")
        mid_ready = sem("mid_ready")
        mask_row_ready = sem("mask_row_ready")
        act_step = sem("act_step")
        out_sem = sem("out_sem")

        ld_wb, ld_wcr, ld_c, ld_f, ld_brow = sem("ld_wb"), sem("ld_wcr"), sem("ld_c"), sem("ld_f"), sem("ld_brow")
        ld_tau, ld_braw, ld_g1, ld_blend = sem("ld_tau"), sem("ld_braw"), sem("ld_g1"), sem("ld_blend")
        sb_full, sb_read = sem("sb_full"), sem("sb_read")
        wo_padded = sem("wo_padded")
        mv_ready, rstd_ready = sem("mv_ready"), sem("rstd_ready")
        x1_ready, xb_ready = sem("x1_ready"), sem("xb_ready")
        band_ready = sem("band_ready")
        ema_ready, tau_ready, diff_ready, ema_exp = sem("ema_ready"), sem("tau_ready"), sem("diff_ready"), sem("ema_exp")
        tau_abs, tau_exp = sem("tau_abs"), sem("tau_exp")
        blend_sub, blend_exp, blend_ready = sem("blend_sub"), sem("blend_exp"), sem("blend_ready")
        gate_sig, gated_ready = sem("gate_sig"), sem("gated_ready")
        mod_sig, mod_ready = sem("mod_sig"), sem("mod_ready")
        Gd_ready, Gp_ready, G_used, ema_full, ema_read = sem("Gd_ready"), sem("Gp_ready"), sem("G_used"), sem("ema_full"), sem("ema_read")
        sg_ready, z_ready = sem("sg_ready"), sem("z_ready")
        lgm_sub, gexp_ready, onehot_ready, slot_ready, tmap_ready = sem("lgm_sub"), sem("gexp_ready"), sem("onehot_ready"), sem("slot_ready"), sem("tmap_ready")
        b_split, b_out = sem("b_split"), sem("b_out")
        z_zeroed, z_out = sem("z_zeroed"), sem("z_out")
        zs_in = [sem(f"zs_in{i}") for i in range(3)]
        brow_zero, tile_zero = sem("brow_zero"), sem("tile_zero")
        a_full, a_read = sem("zT_full"), sem("zT_read")
        h_full, h_read = sem("h_full"), sem("h_read")
        t_full, t_read = sem("hT_full"), sem("hT_read")
        y_full, y_read = sem("y_full"), sem("y_read")
        y_out, yg_in, res_ready = sem("y_out"), [sem("yg_in0"), sem("yg_in1")], sem("res_ready")
        rank_consts = sem("rank_consts")

        half_of = lambda b: b // HALF
        bc_mid = lambda ap, n: ap.unsqueeze(1).broadcast_to([ap.shape[0], n, ap.shape[1]])
        bc_last = lambda ap, n: ap.unsqueeze(2).broadcast_to([ap.shape[0], ap.shape[1], n])

        block = ctx.enter_context(nc.Block())

        @block.sync
        def _(sp):
            col = lambda a: a.rearrange("(p o) -> p o", o=1)
            sp.dma_start(s2_tok[:], A["fside_BxSxS_0"].rearrange("b s c -> s b c")).then_inc(ld_s2, 16)
            sp.dma_start(x_tok[:], A["x"].rearrange("b s c -> s b c")).then_inc(ld_x, 16)
            for i, n in enumerate(("q", "k", "v")):
                sp.dma_start(wqkv[:, i, :], A[f"L0_cond_W{n}"]).then_inc(ld_wa, 16)
                sp.dma_start(bqkv_bc[:, i, :], A[f"L0_cond_b{n}"].partition_broadcast(128)).then_inc(ld_wa, 16)
            sp.dma_start(cols[:, BPREV:BPREV + 1], A["L0_cond_b_prev"].rearrange("a b c -> c (a b)")).then_inc(ld_cols, 16)
            sp.dma_start(cols[:, BSELF:BSELF + 1], A["L0_cond_b_self"].rearrange("a b c -> c (a b)")).then_inc(ld_cols, 16)
            sp.dma_start(len_i[:], A["itok_B_18_1004"].rearrange("(o b) -> o b", o=1)).then_inc(ld_len, 16)
            sp.dma_start(wo[:], A["L0_cond_Wo"]).then_inc(ld_wb, 16)
            sp.dma_start(w_raw[:, 0, :], A["L0_attn_wq"]).then_inc(ld_wb, 16)
            sp.dma_start(w_raw[:, 1:3, :], A["L0_attn_wkv"].rearrange("(a p) c -> p a c", a=2)).then_inc(ld_wb, 16)
            sp.dma_start(wo_raw[:], A["L0_attn_wo"]).then_inc(ld_wb, 16)
            sp.dma_start(bo_bc[:], A["L0_cond_bo"].partition_broadcast(128)).then_inc(ld_wb, 16)
            sp.dma_start(cols[:, BO:BO + 1], col(A["L0_cond_bo"])).then_inc(ld_wb, 16)
            sp.dma_start(tau[:, 0:1], A["L0_cond2_tau_ctx"].partition_broadcast(128)).then_inc(ld_tau, 16)
            sp.dma_start(tau[:, 1:], A["condB_tauraws"].partition_broadcast(128)).then_inc(ld_tau, 16)
            sp.dma_start(blend[:], A["cond_1024"].partition_broadcast(128)).then_inc(ld_blend, 16)
            sp.wait_ge(row_ready, 1)
            sp.wait_ge(mask_row_ready, 1)
            for half in range(2):
                sp.wait_ge(stack_zero, 2 * half + 2)
                row = mask_row[:, half * HALF:half * HALF + HALF, :].rearrange("o b t -> o (b t)")
                sp.dma_start(Ks[RMASK:R0, half], bc_mid(row, H)).then_inc(rows_in, 16)
                sp.dma_start(Qs[RMASK:R0, half], bc_mid(ones_row[:, 0:HT], H)).then_inc(rows_in, 16)

            def stack_up(att, half):
                for which, (stack, runs) in enumerate(((Qs, Q_RUNS), (Ks, K_RUNS))):
                    n = 4 * att + 2 * half + which
                    sp.wait_ge(split_ready, n + 1)
                    slot = 0
                    for first, step, count in runs:
                        src = parts[:, which, first:first + count, :] if step else \
                            bc_mid(parts[:, which, first, :], count)
                        sp.dma_start(scr_parts[att, half, which, slot:slot + count].rearrange("s p t -> p s t"), src)\
                            .then_inc(parts_out[which], 16)
                        slot += count
                for which, stack in enumerate((Qs, Ks)):
                    sp.wait_ge(parts_out[which], 16 * 3 * (2 * att + half + 1))
                    sp.dma_start(stack[R0:KROWS, half],
                                 scr_parts[att, half, which].rearrange("s (d h) t -> (s d) h t", h=H))\
                        .then_inc(stack_in[half], 16)

            stack_up(0, 0)
            stack_up(0, 1)
            job_wait_read(sp, "trS2_1")
            sp.dma_start(b_raw[:, 0:FF], A["L0_ffn_b1"]).then_inc(ld_braw, 16)
            sp.dma_start(b_raw[:, FF:], A["L0_ffn_b2"]).then_inc(ld_braw, 16)
            sp.dma_start(gamma1[:], A["L0_attn_gamma"].partition_broadcast(128)).then_inc(ld_g1, 16)
            sp.dma_start(beta1[:], A["L0_attn_beta"].partition_broadcast(128)).then_inc(ld_g1, 16)
            sp.dma_start(wc_raw[:, 0:2, :], A["L0_cond2_Wg"].rearrange("e (a c) -> e a c", a=2)).then_inc(ld_wcr, 16)
            for i, n in enumerate(("Wsoma", "Wtemp", "Wout")):
                sp.dma_start(wc_raw[:, 2 + i, :], A[f"L0_cond2_{n}"]).then_inc(ld_wcr, 16)
            sp.dma_start(wn1_raw[:], A["L0_cond2_Wn1"]).then_inc(ld_wcr, 16)
            sp.dma_start(wn2_raw[:], A["cond_256"]).then_inc(ld_wcr, 16)
            for dst, n in ((bg_bc, "L0_cond2_bg"), (bn2_bc, "condB_bn2"), (gamma2, "L0_cond2_gamma"),
                           (beta2, "L0_cond2_beta"), (br_bc, "L0_ffn_br")):
                sp.dma_start(dst[:], A[n].partition_broadcast(128)).then_inc(ld_c, 16)
            sp.dma_start(cols[:, BSOMA:BSOMA + 1], col(A["L0_cond2_bsoma"])).then_inc(ld_c, 16)
            sp.dma_start(cols[:, BTEMP:BTEMP + 1], col(A["L0_cond2_btemp"])).then_inc(ld_c, 16)
            sp.dma_start(cols[0:NH1, BN1:BN1 + 1], col(A["L0_cond2_bn1"])).then_inc(ld_c, 16)
            sp.dma_start(wr[:], A["L0_ffn_Wr"]).then_inc(ld_c, 16)
            sp.wait_ge(tile_zero, 1)
            sp.dma_start(z_dram.rearrange("(i p) c -> p i c", p=128), bc_mid(zero_tile[:], TILES)).then_inc(z_zeroed, 16)
            sp.wait_ge(b_split, 3)
            sp.dma_start(b_dram.rearrange("q e f -> e q f"), b_parts[:]).then_inc(b_out, 16)
            for half in range(2):
                sp.wait_ge(s2_full, G * HALF * (half + 1))
                sp.dma_start(Qs[RMASK:R0, half], bc_mid(ones_row[:, HT:2 * HT], H)).then_inc(stack_in[half], 16)
                stack_up(1, half)
            sp.wait_ge(b_out, 16)
            sp.wait_ge(brow_zero, 1)
            sp.dma_start(b_rows[0:3], b_dram).then_inc(ld_brow, 16)
            sp.wait_ge(sb_full, G * NB)
            sp.dma_start(W1[:], A["L0_ffn_W1"].rearrange("e d f -> d e f")).then_inc(ld_f, 16)
            sp.dma_start(W2[:], A["L0_ffn_W2"].rearrange("e (k p) d -> p e k d", p=128)).then_inc(ld_f, 16)
            sp.wait_ge(z_out, 16 * NB)
            third = TILES // 3
            for k in range(3):
                sp.dma_start(zs[:, k * third:(k + 1) * third, :],
                             z_dram[k * third * 128:(k + 1) * third * 128].rearrange("(i p) c -> p i c", p=128))\
                    .then_inc(zs_in[k], 16)
            for k in range(3):
                sp.wait_ge(y_read, (k + 1) * third)
                sp.dma_start(y_dram[k * third * 128:(k + 1) * third * 128].rearrange("(i p) c -> p i c", p=128),
                             ys[:, k * third:(k + 1) * third, :]).then_inc(y_out, 16)
            for half in range(2):
                bs = slice(half * HALF, half * HALF + HALF)
                sp.wait_ge(res_ready, half + 1)
                sp.dma_start(out[bs].rearrange("b s c -> s b c"), yg[:, bs, :]).then_inc(out_sem, 16)
            sp.wait_ge(out_sem, 32)

        @block.gpsimd
        def _(pool):
            steps = [0]

            def link(ins):
                steps[0] += 1
                ins.then_inc(pool_step, 1)
                pool.wait_ge(pool_step, steps[0])

            link(pool.memset(ident[:], 1.0))
            zero_rows = lambda stack, half: pool.memset(stack[0:64, half].bitcast(F32), 0.0).then_inc(stack_zero, 1)
            pool.affine_select(ident[:], ident[:], pattern=[[1, 128]], compare_op=ALU.is_equal, fill=0.0,
                               base=0, channel_multiplier=-1).then_inc(consts_ready, 1)
            link(pool.memset(ones_row[:, HT:2 * HT], 0.0))
            pool.memset(ones_row[:, 0:HT], 1.0).then_inc(row_ready, 1)
            pool.iota(pos_row[:], pattern=[[0, NB], [1, T]], base=0, channel_multiplier=0,
                      allow_small_or_imprecise_dtypes=True).then_inc(pool_pos, 1)
            pool.wait_ge(consts_ready, 1)
            pool.tensor_copy(identb[:], ident[:]).then_inc(consts_ready, 1)
            zero_rows(Qs, 0)
            zero_rows(Ks, 0)
            pool.memset(v_pad[:, 0:HALF], 0.0).then_inc(vpad_zero, 1)
            zero_rows(Qs, 1)
            zero_rows(Ks, 1)
            pool.memset(v_pad[:, HALF:NB], 0.0).then_inc(vpad_zero, 1)
            link(pool.iota(diff[:], pattern=[[1, 128]], base=0, channel_multiplier=-1,
                           allow_small_or_imprecise_dtypes=True))
            pool.tensor_scalar(diff[:], diff[:], 0.0, None, ALU.max).then_inc(diff_ready, 1)
            pool.memset(zero_tile[:], 0.0).then_inc(tile_zero, 1)
            link(pool.memset(wo_rp[:], 0.0))
            pool.wait_ge(ld_wb, 16 * 6)
            pool.tensor_copy(wo_rp[:, :, 0:DH], wo_raw[:].rearrange("p (h d) -> p h d", d=DH)).then_inc(wo_padded, 1)
            link(pool.memset(bandb[:], 0.0))
            link(pool.affine_select(bandb[:], bandb[:], pattern=[[1, 128]], compare_op=ALU.is_ge,
                                    fill=MASKED, base=-1, channel_multiplier=-1))
            pool.affine_select(bandb[:], bandb[:], pattern=[[-1, 128]], compare_op=ALU.is_ge,
                               fill=MASKED, base=WINDOW, channel_multiplier=1).then_inc(band_ready, 1)
            pool.wait_ge(ema_exp, 1)
            pool.affine_select(ema[:], ema[:], pattern=[[0, ND + 1], [1, 128]], compare_op=ALU.is_ge,
                               fill=0.0, base=0, channel_multiplier=-1).then_inc(ema_ready, 1)
            pool.wait_ge(ld_g1, 32)
            job_wait_full(pool, "trX_1")
            pool.tensor_tensor(xb[:], x_tok[:], bc_mid(beta1[:], NB), ALU.add).then_inc(xb_ready, 1)
            link(pool.memset(onehotb[:, 0:NB], 0.0))
            link(pool.memset(onesb[:], 1.0))
            link(pool.affine_select(trib[:], onesb[:], pattern=[[1, 128]], compare_op=ALU.is_gt, fill=0.0,
                                    base=0, channel_multiplier=-1))
            link(pool.iota(em8[:], pattern=[[1, NE]], base=-NE, channel_multiplier=0,
                           allow_small_or_imprecise_dtypes=True))
            link(pool.iota(k128[:], pattern=[[128, NB]], base=0, channel_multiplier=0,
                           allow_small_or_imprecise_dtypes=True))
            link(pool.iota(tile_no[:], pattern=[[1, TILES]], base=0, channel_multiplier=0,
                           allow_small_or_imprecise_dtypes=True))
            link(pool.memset(tri8[:], 1.0))
            pool.affine_select(tri8[:], tri8[:], pattern=[[1, NE], [-1, NE]], compare_op=ALU.is_ge, fill=0.0,
                               base=0, channel_multiplier=0).then_inc(rank_consts, 1)
            link(pool.memset(mhalf[:], -0.5))
            pool.wait_ge(attn_ready, NB)
            pool.memset(b_rows[:], 0.0).then_inc(brow_zero, 1)

            def inverse_std(n, bs):
                pool.wait_ge(mv_ready, n + 1)
                if n >= 2:
                    pool.wait_ge(z_ready if n == 3 else x1_ready, 1 if n == 3 else 2)
                link(pool.tensor_scalar(rstd[:, bs], mv[:, bs, 1], EPS, None, ALU.add))
                pool.tensor_tensor(rstd[:, bs], rstd[:, bs], mhalf[:, bs], ALU.pow).then_inc(rstd_ready, 1)

            inverse_std(0, slice(0, HALF))
            inverse_std(1, slice(HALF, NB))

            PD = 2
            for b in range(NB):
                k = b % 2
                ds = slice(ND - PD, ND)
                pool.wait_ge(gated_ready, half_of(b) + 1)
                pool.wait_ge(mod_ready, half_of(b) + 1)
                pool.wait_ge(blend_ready, 1)
                if b >= 2:
                    pool.wait_ge(G_used, b - 1)
                link(pool.tensor_tensor(Gb[:, k, ds, :], bc_mid(wgate[:, b, :], PD), blend[:, ds, :], ALU.mult))
                pool.tensor_tensor(Gb[:, k, ds, :], Gb[:, k, ds, :], bc_last(mod[:, b, ds], D), ALU.mult)\
                    .then_inc(Gp_ready, 1)

            inverse_std(2, slice(0, HALF))
            inverse_std(3, slice(HALF, NB))

            pool.wait_ge(slot_ready, 1)
            pool.wait_ge(z_ready, 2)
            pool.wait_ge(z_zeroed, 16)
            for b in range(NB):
                pool.indirect_dma_start(out=z_dram, out_offset=bass.IndirectOffsetOnAxis(slot[:, b:b + 1], 0),
                                        in_=z[:, b, :], in_offset=None).then_inc(z_out, 16)
            pool.wait_ge(y_out, 48)
            for b in range(NB):
                pool.indirect_dma_start(out=yg[:, b, :], out_offset=None, in_=y_dram,
                                        in_offset=bass.IndirectOffsetOnAxis(slot[:, b:b + 1], 0))\
                    .then_inc(yg_in[half_of(b)], 16)

        @block.tensor
        def _(pe):
            def transposes(name, src, count, wait=None):
                job_wait_free(pe, name)
                for i in range(count):
                    m = pe.transpose(bank_of(name)[:, i * 128:(i + 1) * 128], src(i), ident[:])
                job_full(m, name)

            def dense(name, lhsT, rhs, cols_, start=True):
                job_wait_free(pe, name)
                m = pe.matmul(bank_of(name)[:, 0:cols_], lhsT, rhs, start=True, stop=True)
                job_full(m, name)

            def project(half):
                cs = slice(half * HT, half * HT + HT)
                if half == 0:
                    pe.wait_ge(consts_ready, 1)
                    pe.wait_ge(ld_s2, 16)
                transposes(f"trS2_{half}", lambda i: s2_tok[:, half * HALF + i, :], 4)
                if half == 0:
                    pe.wait_ge(ld_x, 16)
                transposes(f"trX_{half}", lambda i: x_tok[:, half * HALF + i, :], 4)
                if half == 0:
                    pe.wait_ge(ld_wa, 16 * 6)
                    pe.wait_ge(ld_cols, 16 * 2)
                    job_wait_free(pe, "bcols")
                    pe.wait_ge(wdh_ready, 4)
                    for i, added in enumerate((BSELF, BPREV)):
                        o = bank_of("bcols")[:, i:i + 1]
                        pe.matmul(o, w_dh[:, i, :], cols[:, added:added + 1], start=True, stop=False)
                        m = pe.matmul(o, b_dh[:, i, :], ident[0:1, 0:1],
                                      start=False, stop=True)
                    job_full(m, "bcols")
                    dense("bbc", cols[:, BSELF:BSELF + 1].broadcast_to([128, 128]),
                          wqkv[:, 0:2, :].rearrange("p a b -> p (a b)"), 2 * D)
                job_wait_read(pe, f"trS2_{half}")
                dense(f"qT_{half}", w_dh[:, 0, :], s2T[:, cs], HT)
                job_wait_read(pe, f"trX_{half}")
                dense(f"kT_{half}", w_dh[:, 1, :], xT[:, cs], HT)
                for b in range(half * HALF, half * HALF + HALF):
                    dense(f"tok_{b}", s2T[:, b * T:(b + 1) * T], wqkv[:].rearrange("p a b -> p (a b)"), 3 * D)
                for b in range(half * HALF, half * HALF + HALF):
                    dense(f"vp_{b}", xT[:, b * T:(b + 1) * T], wqkv[:, 2, :], D)

            def stacked(stack, b, h):
                return stack[:, half_of(b), h, (b % HALF) * T:(b % HALF + 1) * T]

            def scores_max(b, g):
                u = b * G + g
                if u == 0:
                    pe.wait_ge(rows_in, 16 * 4)
                if b % HALF == 0 and g == 0:
                    pe.wait_ge(stack_in[half_of(b)], 16 * 2)
                if u >= 2:
                    pe.wait_ge(s1_read, u - 1)
                for j in range(4):
                    h = 4 * g + j
                    m = pe.matmul(S1B[u % 2][:, j * T:(j + 1) * T], stacked(Qs, b, h), stacked(Ks, b, h),
                                  start=True, stop=True)
                m.then_inc(s1_full, 1)

            def scores(b, g):
                u = b * G + g
                pe.wait_ge(negm_ready, b + 1)
                if u >= 2:
                    pe.wait_ge(s2_read, u - 1)
                for j in range(4):
                    h = 4 * g + j
                    o = S2B[u % 2][:, j * T:(j + 1) * T]
                    pe.matmul(o, stacked(Ks, b, h), stacked(Qs, b, h), start=True, stop=False)
                    m = pe.matmul(o, negm[:, b, h:h + 1].broadcast_to([128, 128]), identb[:], start=False, stop=True)
                m.then_inc(s2_full, 1)

            def values(b, g):
                u = b * G + g
                pe.wait_ge(s2_read, u + 1)
                if g == 0:
                    job_wait_read(pe, f"vp_{b}")
                    if b >= 2:
                        pe.wait_ge(pv_read, b - 1)
                for j in range(4):
                    m = pe.matmul(PVB[b % 2][32 * j:32 * j + 32, g * T:(g + 1) * T], v_pad[:, b, 4 * g + j, :],
                                  P[:, u % 3, j * T:(j + 1) * T], start=True, stop=True)
                m.then_inc(pv_done, 1)

            def wide(name, lhsT, rhs):
                dense(name, lhsT, rhs, HT)

            def project_window_y(half):
                job_wait_read(pe, f"attnT_{half * HALF + HALF - 1}")
                wide(f"y0T_{half}", wo[:], attnT[:, half * HT:half * HT + HT])

            def project_window_qk(half):
                job_wait_read(pe, "wB")
                job_wait_read(pe, f"y0T_{half}")
                wide(f"bq_{half}", wB[:, 0, :], y0T[:, half * HT:half * HT + HT])
                wide(f"bk_{half}", wB[:, 1, :], y0T[:, half * HT:half * HT + HT])

            def project_window_v(half):
                for b in range(half * HALF, half * HALF + HALF):
                    dense(f"bv_{b}", y0T[:, b * T:(b + 1) * T], wB[:, 2, :], D)

            def weight_job(i):
                if i == 1:
                    pe.wait_ge(ld_wb, 16 * 6)
                    transposes("wB", lambda k: w_raw[:, k, :], 3)
                if i == 2:
                    pe.wait_ge(wo_padded, 1)
                    transposes("wO", lambda k: wo_rp[:, 4 * k:4 * k + 4, :].rearrange("p a b -> p (a b)"), 4)
                if i == 3:
                    pe.wait_ge(ld_wcr, 16 * 6)
                    transposes("wC1", lambda k: wc_raw[:, k, :], 4)
                if i == 4:
                    job_wait_free(pe, "wC2")
                    bank = bank_of("wC2")
                    pe.transpose(bank[:, 0:128], wc_raw[:, 4, :], ident[:])
                    pe.transpose(bank[:, 128:128 + NH1], wn1_raw[:], ident[0:NH1, 0:NH1])
                    job_full(pe.transpose(bank[0:NH1, 160:160 + ND], wn2_raw[:], ident[0:ND, 0:ND]), "wC2")

            project(0)
            project(1)
            for i in range(NB + 2):
                for g in range(G):
                    if i < NB:
                        scores_max(i, g)
                    if g == 0 and 2 <= i:
                        values(i - 2, G - 1)
                    if g == 0:
                        weight_job(i)
                        if i == HALF + 2:
                            project_window_qk(0)
                    if 1 <= i <= NB:
                        scores(i - 1, g)
                    if g >= 1 and 1 <= i <= NB:
                        values(i - 1, g - 1)
                    if g == 1 and i >= 2:
                        pe.wait_ge(pv_read, i - 1)
                        transposes(f"pvtr_{i-2}", lambda k: pv_sb[:, i % 2, k * 128:(k + 1) * 128], 4)
                    if g == 3 and i >= 2:
                        pe.wait_ge(attn_ready, i - 1)
                        transposes(f"attnT_{i-2}", lambda k: attn[:, i % 2, :], 1)
                        if i == HALF + 1:
                            project_window_y(0)
                        if i == HALF + 2:
                            project_window_v(0)
            project_window_y(1)
            project_window_qk(1)
            project_window_v(1)

            def window_scores(b, g):
                u = b * G + g
                if u == 0:
                    pe.wait_ge(s1_read, G * NB)
                    pe.wait_ge(s2_read, G * NB)
                    pe.wait_ge(band_ready, 1)
                if b % HALF == 0 and g == 0:
                    pe.wait_ge(stack_in[half_of(b)], 16 * 5)
                if u >= 4:
                    pe.wait_ge(sb_read, u - 3)
                bank = ps[u % 4]
                for j in range(4):
                    h = 4 * g + j
                    pe.matmul(bank[:, j * T:(j + 1) * T], stacked(Ks, b, h), stacked(Qs, b, h), start=True, stop=False)
                    m = pe.matmul(bank[:, j * T:(j + 1) * T], identb[:], bandb[:], start=False, stop=True)
                m.then_inc(sb_full, 1)

            def window_values(b, g):
                u = b * G + g
                pe.wait_ge(sb_read, u + 1)
                if g == 0:
                    job_wait_read(pe, f"bv_{b}")
                    pe.wait_ge(pv_read, NB + b - 1)
                for j in range(4):
                    m = pe.matmul(PVB[b % 2][32 * j:32 * j + 32, g * T:(g + 1) * T], v_pad[:, b, 4 * g + j, :],
                                  P[:, u % 3, j * T:(j + 1) * T], start=True, stop=True)
                m.then_inc(pv_done, 1)

            def window_out(b):
                pe.wait_ge(pv_read, NB + b + 1)
                if b == 0:
                    job_wait_read(pe, "wO")
                name = f"y_{b}"
                job_wait_free(pe, name)
                o = bank_of(name)[:, 0:D]
                pe.matmul(o, attnT[:, b * T:(b + 1) * T], wo[:], start=True, stop=False)
                for g in range(G):
                    m = pe.matmul(o, pv_sb[:, b % 2, g * T:(g + 1) * T], woT[:, g, :], start=False, stop=(g == G - 1))
                job_full(m, name)

            for u in range(G * NB + 2):
                if u < G * NB:
                    window_scores(u // G, u % G)
                if u >= 2:
                    window_values((u - 2) // G, (u - 2) % G)
                if u >= 8 and u % G == 0:
                    window_out(u // G - 2)
            window_out(NB - 1)

            def by_batch(name, half, lhsT, rhs, n):
                job_wait_free(pe, name)
                for i in range(HALF):
                    b = half * HALF + i
                    for k in range(len(lhsT)):
                        m = pe.matmul(bank_of(name)[:, i * n:(i + 1) * n], lhsT[k](b), rhs[k], start=(k == 0),
                                      stop=(k == len(lhsT) - 1))
                job_full(m, name)

            tok = lambda src: lambda b: src[:, b * T:(b + 1) * T]
            for half in range(2):
                pe.wait_ge(x1_ready, half + 1)
                transposes(f"x1T_{half}", lambda i: x1[:, half * HALF + i, :], 4)
            pe.wait_ge(ema_ready, 1)
            for half in range(2):
                by_batch(f"ctxT_{half}", half, [lambda b: x1[:, b, :]], [ema[:, 0, :]], T)
            job_wait_read(pe, "wC1")
            for half in range(2):
                job_wait_read(pe, f"x1T_{half}")
                job_wait_read(pe, f"ctxT_{half}")
                by_batch(f"gate_{half}", half, [tok(x1T), tok(ctxT)], [wC[:, 0, :], wC[:, 1, :]], D)
            job_wait_read(pe, "wC2")
            for half in range(2):
                name = f"h1_{half}"
                job_wait_free(pe, name)
                job_full(pe.matmul(bank_of(name)[0:NH1, :], wn1T[:], x1T[:, half * HT:half * HT + HT],
                                   start=True, stop=True), name)
            for half in range(2):
                job_wait_read(pe, f"h1_{half}")
                by_batch(f"mod_{half}", half, [tok(h1T)], [wn2T[:]], ND)
            for half in range(2):
                wide(f"soma_{half}", wC[:, 2, :], x1T[:, half * HT:half * HT + HT])
            for b in range(NB):
                pe.wait_ge(Gd_ready, b + 1)
                pe.wait_ge(Gp_ready, b + 1)
                if b == 0:
                    pe.wait_ge(sb_read, G * NB)
                for d in range(ND):
                    m = pe.matmul(ps[half_of(b)][:, (b % HALF) * T:(b % HALF + 1) * T], Gb[:, b % 2, d, :],
                                  ema[:, 1 + d, :], start=(d == 0), stop=(d == ND - 1))
                m.then_inc(G_used, 1)
            for half in range(2):
                pe.wait_ge(ema_read, half + 1)
                wide(f"tg_{half}", wC[:, 3, :], tempT[:, half * HT:half * HT + HT])
            for half in range(2):
                pe.wait_ge(sg_ready, half + 1)
                by_batch(f"o_{half}", half, [tok(gateT)], [wC[:, 4, :]], D)
            for half in range(2):
                pe.wait_ge(z_ready, half + 1)
                transposes(f"zT_{half}", lambda i: z[:, half * HALF + i, :], 4)
            for half in range(2):
                job_wait_read(pe, f"zT_{half}")
                if half == 0:
                    pe.wait_ge(ld_c, 16 * 9)
                by_batch(f"lg_{half}", half, [tok(zT)], [wr[:]], NE)

            pe.wait_ge(onehot_ready, 1)
            pe.wait_ge(rank_consts, 1)
            job_wait_free(pe, "rank")
            bank = bank_of("rank")
            oh = onehotb[:].rearrange("p b e -> p (b e)")
            W = NB * NE
            pe.matmul(bank[:, 0:W], trib[:], oh[:, W:2 * W], start=True, stop=False)
            for k in range(1, NB):
                pe.matmul(bank[:, 0:W], onesb[:], oh[:, W - k * NE:2 * W - k * NE], start=False, stop=(k == NB - 1))
            for b in range(NB):
                m = pe.matmul(bank[:, W:W + NE], onesb[:], oh[:, W + b * NE:W + (b + 1) * NE], start=(b == 0),
                              stop=(b == NB - 1))
            job_full(m, "rank")

            pe.wait_ge(tmap_ready, 1)
            pe.wait_ge(ld_f, 32)
            pe.wait_ge(ld_brow, 16)
            pe.wait_ge(ema_read, 2)
            job_wait_read(pe, "rank")
            expert = {}
            for i in range(TILES + 3):
                if i < TILES:
                    pe.wait_ge(zs_in[i // (TILES // 3)], 16)
                    if i >= 2:
                        pe.wait_ge(a_read, i - 1)
                    pe.transpose(ps[4 + i % 2][:, 0:128], zs[:, i, :], ident[:]).then_inc(a_full, 1)
                if 1 <= i <= TILES:
                    n = i - 1
                    e = pe.value_load(tmap[0:1, n:n + 1], min_val=0, max_val=NE - 1)
                    expert[n] = e
                    pe.wait_ge(a_read, n + 1)
                    if n >= 2:
                        pe.wait_ge(h_read, n - 1)
                    pe.matmul(ps[n % 2][:, :], zsT[:, n % 2, :], W1[:, bass.ds(e, 1), :].rearrange("p a f -> p (a f)"),
                              start=True, stop=False)
                    pe.matmul(ps[n % 2][:, :], onesb[0:KROWS, :], b_rows[:, bass.ds(e, 1), 0:FF].rearrange("p a f -> p (a f)"),
                              start=False, stop=True).then_inc(h_full, 1)
                if 2 <= i <= TILES + 1:
                    n = i - 2
                    pe.wait_ge(h_read, n + 1)
                    if n >= 2:
                        pe.wait_ge(t_read, n - 1)
                    for c in range(FC):
                        m = pe.transpose(ps[2 + n % 2][:, c * 128:(c + 1) * 128], hs[:, n % 2, c * 128:(c + 1) * 128],
                                         ident[:])
                    m.then_inc(t_full, 1)
                if i >= 3:
                    n = i - 3
                    e = expert[n]
                    pe.wait_ge(t_read, n + 1)
                    if n >= 2:
                        pe.wait_ge(y_read, n - 1)
                    o = ps[6 + n % 2][:, 0:D]
                    for c in range(FC):
                        pe.matmul(o, hsT[:, n % 2, c * 128:(c + 1) * 128],
                                  W2[:, bass.ds(e, 1), c, :].rearrange("p a f -> p (a f)"), start=(c == 0), stop=False)
                    pe.matmul(o, onesb[0:KROWS, :], b_rows[:, bass.ds(e, 1), FF:].rearrange("p a f -> p (a f)"),
                              start=False, stop=True).then_inc(y_full, 1)

        @block.scalar
        def _(act):
            act.wait_ge(tau_abs, 1)
            act.activation(tau2[:], tau2[:], ACT.Exp, scale=-1.0).then_inc(tau_exp, 1)
            act.wait_ge(tau_exp, 1)
            act.activation(tau2[:], tau2[:], ACT.Ln, bias=1.0).then_inc(tau_exp, 1)
            act.wait_ge(tau_ready, 1)
            act.wait_ge(diff_ready, 1)
            for d in range(ND + 1):
                m = act.activation(ema[:, d, :], diff[:], ACT.Exp, scale=tau2[:, d:d + 1])
            m.then_inc(ema_exp, 1)

            def split_high(name, which, n, bias=None):
                job_wait_full(act, name)
                if n:
                    act.wait_ge(parts_out[which], 16 * 3 * n)
                bank = bank_of(name)
                add = {} if bias is None else {"bias": bias}
                act.activation(qf[:, which, :], bank[:, 0:HT], ACT.Identity, **add).then_inc(act_step, 1)
                job_read(act.activation(parts[:, which, 0, :], bank[:, 0:HT], ACT.Identity, **add), name)

            def split_middle(which, n):
                act.wait_ge(rest_ready, 2 * n + which + 1)
                act.copy(parts[:, which, 1, :], rest[:, which, :]).then_inc(mid_ready, 1)

            job_wait_read(act, "bcols")
            for half in range(2):
                split_high(f"qT_{half}", 0, half, ecols[:, 0:1])
                split_high(f"kT_{half}", 1, half, ecols[:, 1:2])
                split_middle(0, half)
                split_middle(1, half)

            def weights_of(u):
                act.wait_ge(s2_full, u + 1)
                if u >= 3:
                    act.wait_ge(pv_done, u - 2)
                act.activation(P[:, u % 3, :], S2B[u % 2][:, :], ACT.Exp, scale=SCALE).then_inc(s2_read, 1)

            def evac_y0T(half):
                name = f"y0T_{half}"
                job_wait_full(act, name)
                if half == 0:
                    act.wait_ge(ld_wb, 16 * 6)
                job_read(act.activation(y0T[:, half * HT:half * HT + HT], bank_of(name)[:, :], ACT.Identity,
                                        bias=cols[:, BO:BO + 1]), name)

            def split_window(half):
                split_high(f"bq_{half}", 0, 2 + half)
                split_high(f"bk_{half}", 1, 2 + half)
                split_middle(0, 2 + half)
                split_middle(1, 2 + half)

            def window_pv(b):
                act.wait_ge(pv_done, G * (NB + b + 1))
                if b >= 2:
                    job_wait_full(act, f"y_{b-2}")
                else:
                    job_wait_full(act, f"pvtr_{NB-2+b}")
                act.copy(pv_sb[:, b % 2, :], PVB[b % 2][:, :]).then_inc(pv_read, 1)

            act.wait_ge(blend_sub, 1)
            act.activation(blend[:], blend[:], ACT.Exp).then_inc(blend_exp, 1)
            for i in range(NB + 2):
                if 1 <= i <= NB:
                    act.wait_ge(sshift_ready, i)
                    act.activation(w_self[:, i - 1, :], sshift[:, i - 1, :], ACT.Exp, scale=SCALE)\
                        .then_inc(wself_ready, 1)
                for g in range(G):
                    if 1 <= i <= NB:
                        weights_of((i - 1) * G + g)
                    if g == 0 and 2 <= i:
                        b = i - 2
                        act.wait_ge(pv_done, G * (b + 1))
                        if b >= 2:
                            job_wait_full(act, f"pvtr_{b-2}")
                        act.copy(pv_sb[:, b % 2, :], PVB[b % 2][:, :]).then_inc(pv_read, 1)
                    if g == 3 and 2 <= i:
                        b = i - 2
                        job_wait_full(act, f"attnT_{b}")
                        job_read(act.copy(attnT[:, b * T:(b + 1) * T], bank_of(f"attnT_{b}")[:, 0:T]), f"attnT_{b}")
                        if i == HALF + 1:
                            evac_y0T(0)
                    if g == 1 and i == HALF + 2:
                        split_window(0)
            evac_y0T(1)
            split_window(1)

            for u in range(G * NB + 2):
                if u < G * NB:
                    act.wait_ge(sb_full, u + 1)
                    act.wait_ge(pv_done, G * NB + u - 2)
                    act.activation(P[:, u % 3, :], ps[u % 4][:, :], ACT.Sigmoid, scale=SCALE).then_inc(sb_read, 1)
                if u >= 5 and (u - 5) % G == 0:
                    window_pv((u - 5) // G)

            def evac(name, dst, rows=128):
                job_wait_full(act, name)
                job_read(act.copy(dst, bank_of(name)[0:rows, 0:HT]), name)

            cut = lambda buf, half: buf[:, half * HT:half * HT + HT]
            for half in range(2):
                evac(f"x1T_{half}", cut(x1T, half))
            for half in range(2):
                evac(f"ctxT_{half}", cut(ctxT, half))
            act.wait_ge(ld_c, 16 * 9)
            for half in range(2):
                name = f"h1_{half}"
                job_wait_full(act, name)
                job_read(act.activation(cut(h1T, half), bank_of(name)[0:NH1, :], ACT.Gelu,
                                        bias=cols[0:NH1, BN1:BN1 + 1]), name)
            for half in range(2):
                name = f"soma_{half}"
                job_wait_full(act, name)
                job_read(act.activation(cut(somaT, half), bank_of(name)[:, :], ACT.Gelu,
                                        bias=cols[:, BSOMA:BSOMA + 1]), name)
            for half in range(2):
                job_wait_read(act, f"gate_{half}")
                act.activation(wgate[:, half * HALF:half * HALF + HALF, :], wgate[:, half * HALF:half * HALF + HALF, :],
                               ACT.Sigmoid).then_inc(gate_sig, 1)
                job_wait_read(act, f"mod_{half}")
                act.activation(mod[:, half * HALF:half * HALF + HALF, :], mod[:, half * HALF:half * HALF + HALF, :],
                               ACT.Sigmoid).then_inc(mod_sig, 1)
            for half in range(2):
                act.wait_ge(G_used, HALF * (half + 1))
                act.copy(cut(tempT, half), ps[half][:, :]).then_inc(ema_read, 1)
            for half in range(2):
                name = f"tg_{half}"
                job_wait_full(act, name)
                job_read(act.activation(cut(gateT, half), bank_of(name)[:, :], ACT.Sigmoid,
                                        bias=cols[:, BTEMP:BTEMP + 1]), name)
            for half in range(2):
                evac(f"o_{half}", o_sb[:, half * HALF:half * HALF + HALF, :].rearrange("p b c -> p (b c)"))
            for half in range(2):
                evac(f"zT_{half}", cut(zT, half))
            act.wait_ge(lgm_sub, 1)
            act.activation(gexp[:], gexp[:], ACT.Exp).then_inc(gexp_ready, 1)

            for i in range(TILES + 1):
                if i < TILES:
                    act.wait_ge(a_full, i + 1)
                    if i >= 2:
                        act.wait_ge(h_full, i - 1)
                    act.copy(zsT[:, i % 2, :], ps[4 + i % 2][:, 0:128]).then_inc(a_read, 1)
                if i >= 1:
                    n = i - 1
                    act.wait_ge(h_full, n + 1)
                    if n >= 2:
                        act.wait_ge(t_full, n - 1)
                    act.activation(hs[:, n % 2, :], ps[n % 2][:, :], ACT.Gelu).then_inc(h_read, 1)

        @block.vector
        def _(dve):
            counts = {}

            def link(ins, s=dve_step):
                counts[id(s)] = counts.get(id(s), 0) + 1
                ins.then_inc(s, 1)
                dve.wait_ge(s, counts[id(s)])

            def link_job(ins, name):
                job_read(ins, name)
                job_wait_read(dve, name)

            dve.wait_ge(ld_len, 16)
            link(dve.tensor_copy(len_f[:], len_i[:]))
            dve.wait_ge(pool_pos, 1)
            link(dve.tensor_tensor(pos_row[:], pos_row[:], bc_last(len_f[:], T), ALU.is_ge))
            link(dve.tensor_scalar(mask_row[:], pos_row[:], MASKED, None, ALU.mult), mask_row_ready)

            dve.wait_ge(ld_tau, 32)
            link(dve.scalar_tensor_tensor(tau2[:], tau[:], -1.0, tau[:], ALU.mult, ALU.max), tau_abs)
            link(dve.tensor_scalar(tau[:], tau[:], 0.0, None, ALU.max))
            dve.wait_ge(tau_exp, 2)
            link(dve.scalar_tensor_tensor(tau2[:], tau[:], -1.0, tau2[:], ALU.mult, ALU.subtract), tau_ready)

            dve.wait_ge(ld_wa, 16 * 6)
            for i in range(2):
                link(dve.tensor_copy(w_dh[:, i, :].rearrange("p (d h) -> p d h", h=H),
                                     wqkv[:, i, :].rearrange("p (h d) -> p d h", d=DH)), wdh_ready)
                link(dve.tensor_copy(b_dh[:, i, :].rearrange("p (d h) -> p d h", h=H),
                                     bqkv_bc[0:1, i, :].rearrange("p (h d) -> p d h", d=DH)), wdh_ready)

            def evac_transposes(name, dst):
                job_wait_full(dve, name)
                link_job(dve.tensor_copy(dst, bank_of(name)[:, 0:HT]), name)

            def token_major(b):
                name = f"tok_{b}"
                job_wait_full(dve, name)
                link_job(dve.tensor_tensor(tokA[:, b].rearrange("p a b -> p (a b)"), bank_of(name)[:, 0:3 * D],
                                           bqkv_bc[:].rearrange("p a b -> p (a b)"), ALU.add), name)

            def v_prev(b):
                name = f"vp_{b}"
                job_wait_full(dve, name)
                dve.wait_ge(vpad_zero, half_of(b) + 1)
                link(dve.memset(v_pad[:, b, :, DH:DH + 1], 1.0))
                link_job(dve.tensor_tensor(v_pad[:, b, :, 0:DH],
                                           bank_of(name)[:, 0:D].rearrange("p (h d) -> p h d", d=DH),
                                           bqkv_bc[:, 2, :].rearrange("p (h d) -> p h d", d=DH), ALU.add), name)

            def split_rest(name, which, n):
                dve.wait_ge(act_step, 2 * n + which + 1)
                job_wait_read(dve, name)
                link(dve.tensor_tensor(rest[:, which, :], qf[:, which, :], parts[:, which, 0, :], ALU.subtract), rest_ready)

            def split_low(which, n):
                dve.wait_ge(mid_ready, 2 * n + which + 1)
                link(dve.tensor_tensor(parts[:, which, 2, :], rest[:, which, :], parts[:, which, 1, :], ALU.subtract),
                     split_ready)

            def split_both(names, n):
                split_rest(names[0], 0, n)
                split_rest(names[1], 1, n)
                split_low(0, n)
                split_low(1, n)

            for half in range(2):
                cs = slice(half * HT, half * HT + HT)
                evac_transposes(f"trS2_{half}", s2T[:, cs])
                evac_transposes(f"trX_{half}", xT[:, cs])
                if half == 0:
                    job_wait_full(dve, "bcols")
                    link_job(dve.tensor_copy(ecols[:], bank_of("bcols")[:, 0:2]), "bcols")
                    job_wait_full(dve, "bbc")
                    dve.wait_ge(ld_wa, 16 * 6)
                    qk_bc = bqkv_bc[:, 0:2, :].rearrange("p a b -> p (a b)")
                    link_job(dve.tensor_tensor(qk_bc, bank_of("bbc")[:, 0:2 * D], qk_bc, ALU.add), "bbc")
                split_both((f"qT_{half}", f"kT_{half}"), half)
                for b in range(half * HALF, half * HALF + HALF):
                    token_major(b)
                bs = slice(half * HALF, half * HALF + HALF)
                link(dve.tensor_tensor(prod[:], tokA[:, bs, 0, :], tokA[:, bs, 1, :], ALU.mult))
                link(dve.tensor_reduce(s_self[:, bs, :], prod[:].rearrange("p b (h d) -> p b h d", d=DH), AX.X, ALU.add))
                for b in range(half * HALF, half * HALF + HALF):
                    v_prev(b)

            def row_max(b, g):
                u = b * G + g
                dve.wait_ge(s1_full, u + 1)
                link(dve.tensor_reduce(mx[:, b, 4 * g:4 * g + 4], S1B[u % 2][:, :].rearrange("p (j t) -> p j t", j=4),
                                       AX.X, ALU.max), s1_read)

            def shift(b):
                link(dve.tensor_tensor(mx[:, b, :], mx[:, b, :], s_self[:, b, :], ALU.max))
                link(dve.tensor_scalar(negm[:, b, :], mx[:, b, :], -1.0, None, ALU.mult), negm_ready)
                link(dve.tensor_tensor(sshift[:, b, :], s_self[:, b, :], negm[:, b, :], ALU.add), sshift_ready)

            def normalise(b):
                name = f"pvtr_{b}"
                k = b % 2
                pvt = bank_of(name)[:, :].rearrange("p (h e) -> p h e", e=32)
                hd = lambda ap: ap.rearrange("p (h d) -> p h d", d=DH)
                dve.wait_ge(wself_ready, b + 1)
                link(dve.tensor_tensor(hd(wv[:, k, :]), hd(tokA[:, b, 2, :]), bc_last(w_self[:, b, :], DH), ALU.mult))
                job_wait_full(dve, name)
                link(dve.tensor_tensor(den[:, k, :], pvt[:, :, DH], w_self[:, b, :], ALU.add))
                link(dve.reciprocal(rden[:, k, :], den[:, k, :]))
                link_job(dve.tensor_tensor(hd(wv[:, k, :]), pvt[:, :, 0:DH], hd(wv[:, k, :]), ALU.add), name)
                link(dve.tensor_tensor(hd(attn[:, k, :]), hd(wv[:, k, :]), bc_last(rden[:, k, :], DH), ALU.mult), attn_ready)

            dve.wait_ge(ld_blend, 16)
            by_c = blend[:].rearrange("p d c -> p c d")
            link(dve.tensor_reduce(bl_small[:, 0, :], by_c, AX.X, ALU.max))
            link(dve.tensor_tensor(blend[:], blend[:], bc_mid(bl_small[:, 0, :], ND), ALU.subtract), blend_sub)

            def weight_copies(i):
                if i == 1:
                    job_wait_full(dve, "wB")
                    bank = bank_of("wB")
                    hd, dh = "p (h d) -> p h d", "p (d h) -> p h d"
                    kv = bank[:, 128:384].rearrange("p (h e) -> p h e", e=2 * DH)
                    link(dve.tensor_copy(wB[:, 0, :].rearrange(dh, d=DH), bank[:, 0:128].rearrange(hd, d=DH)))
                    link(dve.tensor_copy(wB[:, 1, :].rearrange(dh, d=DH), kv[:, :, 0:DH]))
                    link_job(dve.tensor_copy(wB[:, 2, :].rearrange(hd, d=DH), kv[:, :, DH:]), "wB")
                if i == 2:
                    job_wait_full(dve, "wO")
                    link_job(dve.tensor_copy(woT[:].rearrange("p g c -> p (g c)"), bank_of("wO")[:, :]), "wO")
                    dve.wait_ge(blend_exp, 1)
                    link(dve.tensor_reduce(bl_small[:, 0, :], by_c, AX.X, ALU.add))
                    link(dve.reciprocal(bl_small[:, 1, :], bl_small[:, 0, :]))
                    link(dve.tensor_tensor(blend[:], blend[:], bc_mid(bl_small[:, 1, :], ND), ALU.mult), blend_ready)
                if i == 3:
                    job_wait_full(dve, "wC1")
                    link_job(dve.tensor_copy(wC[:, 0:4, :].rearrange("p g c -> p (g c)"), bank_of("wC1")[:, :]), "wC1")
                if i == 4:
                    job_wait_full(dve, "wC2")
                    bank = bank_of("wC2")
                    link(dve.tensor_copy(wC[:, 4, :], bank[:, 0:128]))
                    link(dve.tensor_copy(wn1T[:], bank[:, 128:128 + NH1]))
                    link_job(dve.tensor_copy(wn2T[:], bank[0:NH1, 160:160 + ND]), "wC2")
                if i == 5:
                    dve.wait_ge(ld_braw, 32)
                    link(dve.tensor_copy(b_parts[:, 0, :], b_raw[:]), b_split)
                    link(dve.tensor_tensor(b_rest[:], b_raw[:], b_parts[:, 0, :], ALU.subtract))
                    link(dve.tensor_copy(b_parts[:, 1, :], b_rest[:]), b_split)
                    link(dve.tensor_tensor(b_parts[:, 2, :], b_rest[:], b_parts[:, 1, :], ALU.subtract), b_split)

            def window_v(half):
                for b in range(half * HALF, half * HALF + HALF):
                    name = f"bv_{b}"
                    job_wait_full(dve, name)
                    dve.wait_ge(pv_done, G * (b + 1))
                    link_job(dve.tensor_copy(v_pad[:, b, :, 0:DH],
                                             bank_of(name)[:, 0:D].rearrange("p (h d) -> p h d", d=DH)), name)

            for i in range(NB + 2):
                for g in range(G):
                    if i < NB:
                        row_max(i, g)
                    if g == 0:
                        weight_copies(i)
                        if i == HALF + 2:
                            split_both(("bq_0", "bk_0"), 2)
                    if g == 2 and i >= 2:
                        normalise(i - 2)
                    if g == 3 and i == HALF + 2:
                        window_v(0)
                if i < NB:
                    shift(i)
            split_both(("bq_1", "bk_1"), 3)
            window_v(1)

            def statistics(src, b, done):
                link(dve.bn_stats(stats[:, b, :], src))
                link(dve.bn_aggr(mv[:, b, :], stats[:, b, :]), *done)

            dve.wait_ge(ld_g1, 32)
            dve.wait_ge(xb_ready, 1)

            def norm_half(n, buf, half, gamma, addend, done):
                bs = slice(half * HALF, half * HALF + HALF)
                dve.wait_ge(rstd_ready, n + 1)
                for b in range(half * HALF, half * HALF + HALF):
                    link(dve.tensor_scalar(buf[:, b, :], buf[:, b, :], mv[:, b, 0:1], rstd[:, b:b + 1],
                                           ALU.subtract, ALU.mult))
                link(dve.tensor_tensor(buf[:, bs, :], buf[:, bs, :], bc_mid(gamma[:], HALF), ALU.mult))
                return bs

            for b in range(NB):
                name = f"y_{b}"
                job_wait_full(dve, name)
                link_job(dve.tensor_tensor(x1[:, b, :], bank_of(name)[:, 0:D], bo_bc[:], ALU.add), name)
                statistics(x1[:, b, :], b, (mv_ready,) if b % HALF == HALF - 1 else ())
                if b % HALF == HALF - 1:
                    half = half_of(b)
                    bs = norm_half(half, x1, half, gamma1, None, None)
                    link(dve.tensor_tensor(x1[:, bs, :], x1[:, bs, :], xb[:, bs, :], ALU.add), x1_ready)

            dve.wait_ge(ld_c, 16 * 9)
            for half in range(2):
                name = f"gate_{half}"
                bs = slice(half * HALF, half * HALF + HALF)
                job_wait_full(dve, name)
                job_read(dve.tensor_tensor(wgate[:, bs, :], bank_of(name)[:, :].rearrange("p (b c) -> p b c", b=HALF),
                                           bc_mid(bg_bc[:], HALF), ALU.add), name)
            for half in range(2):
                name = f"mod_{half}"
                bs = slice(half * HALF, half * HALF + HALF)
                job_wait_full(dve, name)
                link_job(dve.tensor_tensor(mod[:, bs, :], bank_of(name)[:, 0:HALF * ND].rearrange("p (b c) -> p b c", b=HALF),
                                           bc_mid(bn2_bc[:], HALF), ALU.add), name)
            for half in range(2):
                bs = slice(half * HALF, half * HALF + HALF)
                dve.wait_ge(gate_sig, half + 1)
                link(dve.tensor_tensor(wgate[:, bs, :], wgate[:, bs, :], x1[:, bs, :], ALU.mult), gated_ready)
                dve.wait_ge(mod_sig, half + 1)
                link(dve.tensor_scalar(mod[:, bs, :], mod[:, bs, :], 0.5, None, ALU.add), mod_ready)
                for b in range(half * HALF, half * HALF + HALF):
                    if b >= 2:
                        dve.wait_ge(G_used, b - 1)
                    for d in range(ND - 2):
                        m = dve.scalar_tensor_tensor(Gb[:, b % 2, d, :], wgate[:, b, :], mod[:, b, d:d + 1],
                                                     blend[:, d, :], ALU.mult, ALU.mult)
                    link(m, Gd_ready)
            for half in range(2):
                name = f"tg_{half}"
                cs = slice(half * HT, half * HT + HT)
                job_wait_read(dve, name)
                job_wait_read(dve, f"soma_{half}")
                link(dve.tensor_tensor(gateT[:, cs], gateT[:, cs], somaT[:, cs], ALU.mult), sg_ready)
            for half in range(2):
                job_wait_read(dve, f"o_{half}")
                for b in range(half * HALF, half * HALF + HALF):
                    statistics(o_sb[:, b, :], b, (mv_ready,) if b % HALF == HALF - 1 else ())
                bs = norm_half(2 + half, o_sb, half, gamma2, None, None)
                link(dve.tensor_tensor(z[:, bs, :], o_sb[:, bs, :], bc_mid(beta2[:], HALF), ALU.add), z_ready)

            for half in range(2):
                name = f"lg_{half}"
                bs = slice(half * HALF, half * HALF + HALF)
                job_wait_full(dve, name)
                link_job(dve.tensor_tensor(lg[:, bs, :], bank_of(name)[:, 0:HALF * NE].rearrange("p (b c) -> p b c", b=HALF),
                                           bc_mid(br_bc[:], HALF), ALU.add), name)
            dve.wait_ge(rank_consts, 1)
            link(dve.tensor_reduce(lgm[:], lg[:], AX.X, ALU.max))
            link(dve.tensor_tensor(cand[:], lg[:], bc_last(lgm[:], NE), ALU.is_equal))
            link(dve.tensor_tensor(cand[:], cand[:], bc_mid(em8[:], NB), ALU.mult))
            link(dve.tensor_reduce(emin[:], cand[:], AX.X, ALU.min))
            link(dve.tensor_tensor(onehotb[:, NB:], cand[:], bc_last(emin[:], NE), ALU.is_equal), onehot_ready)
            link(dve.tensor_tensor(onehot[:], cand[:], bc_last(emin[:], NE), ALU.is_equal))
            link(dve.tensor_tensor(gexp[:], lg[:], bc_last(lgm[:], NE), ALU.subtract), lgm_sub)
            job_wait_full(dve, "rank")
            bank = bank_of("rank")
            W = NB * NE
            link(dve.tensor_tensor(cmp[:], bc_last(bank[:, W:W + NE], NB), bc_mid(k128[:], NE), ALU.is_gt))
            link(dve.tensor_reduce(tiles_e[:], cmp[:], AX.X, ALU.add))
            link(dve.tensor_tensor(cmp[:], tri8[:], bc_mid(tiles_e[:], NE), ALU.mult))
            link(dve.tensor_reduce(incl[:], cmp[:], AX.X, ALU.add))
            link(dve.tensor_tensor(excl[:], incl[:], tiles_e[:], ALU.subtract))
            link_job(dve.scalar_tensor_tensor(cand[:], bc_mid(excl[:], NB), 128.0,
                                              bank[:, 0:W].rearrange("p (b e) -> p b e", e=NE), ALU.mult, ALU.add), "rank")
            link(dve.tensor_tensor(cand[:], cand[:], onehot[:], ALU.mult))
            link(dve.tensor_reduce(slotf[:], cand[:], AX.X, ALU.add))
            link(dve.tensor_copy(slot[:], slotf[:]), slot_ready)
            link(dve.tensor_tensor(tmap_c[:], bc_mid(incl[0:1, :], TILES), bc_last(tile_no[:], NE), ALU.is_le))
            link(dve.tensor_reduce(tmap_f[:], tmap_c[:], AX.X, ALU.add))
            link(dve.tensor_scalar(tmap_f[:], tmap_f[:], float(NE - 1), None, ALU.min))
            link(dve.tensor_copy(tmap[:], tmap_f[:]), tmap_ready)
            dve.wait_ge(gexp_ready, 1)
            link(dve.tensor_reduce(gsum[:], gexp[:], AX.X, ALU.add))
            link(dve.reciprocal(gate[:], gsum[:]))

            for i in range(2, TILES + 3):
                if i < TILES + 2:
                    n = i - 2
                    dve.wait_ge(t_full, n + 1)
                    if n >= 2:
                        dve.wait_ge(y_full, n - 1)
                    dve.tensor_copy(hsT[:, n % 2, :], ps[2 + n % 2][:, :]).then_inc(t_read, 1)
                if i >= 3:
                    n = i - 3
                    dve.wait_ge(y_full, n + 1)
                    dve.tensor_copy(ys[:, n, :], ps[6 + n % 2][:, 0:D]).then_inc(y_read, 1)
            for half in range(2):
                dve.wait_ge(yg_in[half], 16 * HALF)
                for b in range(half * HALF, half * HALF + HALF):
                    m = dve.scalar_tensor_tensor(yg[:, b, :], yg[:, b, :], gate[:, b:b + 1], x1[:, b, :], ALU.mult, ALU.add)
                link(m, res_ready)


_OUTS = [((8, 128, 128), "float32")]


def kernel(**inputs):
    import numpy as _np
    import concourse.bacc as _bacc
    from concourse import mybir as _mybir
    from concourse.bass_utils import run_bass_kernel_spmd as _run

    nc = _bacc.Bacc("TRN2", target_bir_lowering=False, num_devices=1)
    arrays, args = {}, {}
    for name, a in inputs.items():
        a = _np.ascontiguousarray(a)
        if a.ndim == 0:
            a = a.reshape(1)
        arrays[f"in_{name}_dram"] = a
        args[name] = nc.dram_tensor(f"in_{name}_dram", a.shape, _mybir.dt.from_np(a.dtype), kind="ExternalInput").ap()
    shape, dtype = _OUTS[0]
    o = nc.dram_tensor("out_0_dram", shape, _mybir.dt.from_np(_np.dtype(dtype)), kind="ExternalOutput").ap()
    fused_layer(nc, args, o)
    r = _run(nc, [arrays], core_ids=[0])
    return r.results[0]["out_0_dram"]
```

```python
from contextlib import ExitStack

import concourse.bass as bass
from concourse import mybir

ALU = mybir.AluOpType
ACT = mybir.ActivationFunctionType
AX = mybir.AxisListType
F32 = mybir.dt.float32
BF16 = mybir.dt.bfloat16
I32 = mybir.dt.int32
U32 = mybir.dt.uint32


def fused_layer(nc, A, out):
    NB, T, D = A["x"].shape
    H = 16
    DH = D // H
    G = H // 4
    HALF = NB // 2
    HT = HALF * T
    NT = NB * T
    WINDOW = 16
    NE, _, FF = A["L0_ffn_W1"].shape
    FC = FF // 128
    ND = A["cond_1024"].shape[0]
    NH1 = A["cond_256"].shape[1]
    TILES = NT // 128 + NE - 1
    SCALE = float(DH) ** -0.5
    MASKED = -1.0e30
    EPS = 1e-5
    PRODUCTS = ((0, 1, 2, 0, 1, 0), (0, 0, 0, 1, 1, 2))
    NSLOT = len(PRODUCTS[0])
    NPROD = NSLOT * DH
    KROWS = 96
    R0 = KROWS - NPROD
    RMASK = R0 - 1

    ctx = ExitStack()
    with ctx:
        sb = lambda name, shape, dt=F32: ctx.enter_context(nc.sbuf_tensor("t_" + name, shape, dt))
        sem = lambda name: ctx.enter_context(nc.semaphore(name))
        dram = lambda name, shape, dt=F32: nc.dram_tensor(name, shape, dt).ap()

        ident = sb("ident", [128, 128])
        identb = sb("identb", [128, 128], BF16)
        bandb = sb("bandb", [128, 128], BF16)
        onesb = sb("onesb", [128, 128], BF16)
        ones_row = sb("ones_row", [1, NT], BF16)
        mask_row = sb("mask_row", [1, NB, T], BF16)
        pos_row = sb("pos_row", [1, NB, T])
        len_i = sb("len_i", [1, NB], I32)
        len_f = sb("len_f", [1, NB])
        wqkv = sb("wqkv", [128, 3, D])
        wo = sb("wo", [128, D])
        bqkv_bc = sb("bqkv_bc", [128, 3, D])
        bo_bc = sb("bo_bc", [128, D])
        cols = sb("cols", [128, 12])
        BQ, BK, BPREV, BSELF, BO, BSOMA, BTEMP, BN1 = range(8)
        ecols = sb("ecols", [128, 2])

        x_tok = sb("x_tok", [128, NB, D])
        ROW = 2 * D + 2
        GATE, TOKEN = 2 * D, 2 * D + 1
        rows = sb("rows", [128, NB, ROW])
        z, x1 = rows[:, :, 0:D], rows[:, :, D:2 * D]
        s2_tok = rows[:].rearrange("p b c -> p (b c)")[:, 0:NB * D].rearrange("p (b c) -> p b c", b=NB)
        xT = sb("xT", [128, NT])
        s2T = sb("s2T", [128, NT])
        qf = sb("qf", [128, 2, HT])
        parts = sb("parts", [128, 2, 2, 3, HT], BF16)
        rest = sb("rest", [128, 2, HT])
        Qs_all = sb("Qs", [128, 2, H, HT], BF16)
        Ks_all = sb("Ks", [128, 2, H, HT], BF16)
        Qs, Ks = Qs_all[0:KROWS], Ks_all[0:KROWS]
        w_dh = sb("w_dh", [128, 2, D])
        b_dh = sb("b_dh", [1, 2, D])
        tokA = sb("tokA", [128, NB, 3, D])
        v_pad = sb("v_pad", [128, NB, H, 32])
        prod = sb("prod", [128, HALF, D])
        s_self = sb("s_self", [128, NB, H])
        mx = sb("mx", [128, NB, H])
        negm = sb("negm", [128, NB, H], BF16)
        sshift = sb("sshift", [128, NB, H])
        w_self = sb("w_self", [128, NB, H])
        P = sb("P", [128, 3, 512])
        pv_sb = sb("pv_sb", [128, 2, 512])
        den = sb("den", [128, 2, H])
        rden = sb("rden", [128, 2, H])
        wv = sb("wv", [128, 2, D])
        attn = sb("attn", [128, 2, D])
        attnT = sb("attnT", [128, NT])

        w_raw = sb("w_raw", [128, 3, D])
        wo_raw = sb("wo_raw", [128, D])
        wo_rp = sb("wo_rp", [128, H, 32])
        wB = sb("wB", [128, 3, D])
        woT = sb("woT", [128, G, D])
        y0T = sb("y0T", [128, NT])
        stats = sb("stats", [128, NB, 6])
        mv = sb("mv", [128, NB, 2])
        rstd = sb("rstd", [128, NB])
        mhalf = sb("mhalf", [128, NB])
        gamma1 = sb("gamma1", [128, D])
        beta1 = sb("beta1", [128, D])
        wc_raw = sb("wc_raw", [128, 5, D])
        wn1_raw = sb("wn1_raw", [NH1, D])
        wn2_raw = sb("wn2_raw", [ND, NH1])
        wC = sb("wC", [128, 6, D])
        wn1T = sb("wn1T", [128, NH1])
        wn2T = sb("wn2T", [NH1, ND])
        bg_bc = sb("bg_bc", [128, D])
        bn2_bc = sb("bn2_bc", [128, ND])
        blend = sb("blend", [128, ND, D])
        bl_small = sb("bl_small", [128, 2, D])
        tau = sb("tau", [128, ND + 1])
        tau2 = sb("tau2", [128, ND + 1])
        diff = sb("diff", [128, 128])
        ema = sb("ema", [128, ND + 1, 128])
        gamma2 = sb("gamma2", [128, D])
        beta2 = sb("beta2", [128, D])
        x1T = xT
        ctxT = s2T
        mod = sb("mod", [128, NB, ND])
        tempT = attnT
        somaT = y0T
        wr = sb("wr", [128, NE])
        br_bc = sb("br_bc", [128, NE])
        b_parts = sb("b_parts", [NE, 3, FF + D], BF16)
        lg = sb("lg", [128, NB, NE])
        lgm = sb("lgm", [128, NB])
        em8 = sb("em8", [128, NE])
        cand = sb("cand", [128, NB, NE])
        emin = sb("emin", [128, NB])
        onehotb = sb("onehotb", [128, 2 * NB, NE], BF16)
        gexp = sb("gexp", [128, NB, NE])
        gsum = sb("gsum", [128, NB])
        trib = sb("trib", [128, 128], BF16)
        k128 = sb("k128", [128, NB])
        cmp = sb("cmp", [128, NE, NB])
        tiles_e = sb("tiles_e", [128, NE])
        tri8 = sb("tri8", [128, NE, NE])
        incl = sb("incl", [128, NE])
        excl = sb("excl", [128, NE])
        slotf = sb("slotf", [128, NB])
        slot = sb("slot", [128, NB], U32)
        tile_no = sb("tile_no", [1, TILES])
        tmap_c = sb("tmap_c", [1, TILES, NE])
        tmap_f = sb("tmap_f", [1, TILES])
        tmap = sb("tmap", [1, TILES], I32)
        zsT = sb("zsT", [128, 2, 128])
        empty_row = sb("empty_row", [128, ROW])

        flat = lambda buf, pattern: buf[:].rearrange(pattern)
        q_room = flat(Qs_all, "p a h t -> p (a h t)").bitcast(F32)
        k_room = flat(Ks_all, "p a h t -> p (a h t)").bitcast(F32)
        v_room = flat(v_pad, "p b h e -> p (b h e)")
        t_room = flat(tokA, "p b a c -> p (b a c)")
        cut3 = lambda room, at, n, m: room[:, at:at + n * m].rearrange("p (n m) -> p n m", n=n)
        Gb = q_room[:, 0:2 * ND * D].rearrange("p (k d c) -> p k d c", k=2, d=ND)
        at = 2 * ND * D
        gateT, h1T, zT = (q_room[:, at + i * NT:at + (i + 1) * NT] for i in range(3))
        h1T = h1T[0:NH1]
        at += 3 * NT
        o_sb = cut3(q_room, at, NB, D)
        hs = cut3(q_room, at + NB * D, 2, FF)
        zs = cut3(q_room, 0, TILES, ROW)
        W1 = cut3(k_room, 0, NE, FF)
        W2 = k_room[:, NE * FF:NE * (FF + FC * D)].rearrange("p (e k d) -> p e k d", e=NE, k=FC)
        wgate = cut3(v_room, 0, NB, D)
        hsT = cut3(v_room, NB * D, 2, FF)
        ys = cut3(v_room, NB * D + 2 * FF, TILES, D)
        b_rows = t_room.bitcast(BF16)[0:KROWS, 0:NE * (FF + D)].rearrange("p (e f) -> p e f", e=NE)
        b_raw = flat(rows, "p b c -> p (b c)")[0:NE, 0:FF + D]
        b_rest = flat(rows, "p b c -> p (b c)")[0:NE, FF + D:2 * (FF + D)]
        xb = x_tok

        b_dram = dram("b_dram", (3, NE, FF + D), BF16)
        z_dram = dram("z_dram", (TILES * 128, ROW))

        ps = [ctx.enter_context(nc.psum_tensor(f"ps{i}", [128, 512], F32)) for i in range(8)]
        S1B, S2B, PVB = ps[0:2], ps[2:4], ps[4:6]

        UNITS = G * NB
        PD = 1
        LAG_SCORES, LAG_VALUES = 5, 6
        LAG_PVTR, LAG_OUT = 8, 11
        PROJECT_AT = HALF * G - 1 + LAG_OUT + 2

        order = [("trS2_0", 6), ("trX_0", 7), ("bcols", 0), ("bbc", 1), ("qT_0", 2), ("kT_0", 3), ("trS2_1", 4),
                 ("trX_1", 5), ("qT_1", 0), ("kT_1", 1)]
        order += [(f"tok_{b}", 6 + b % 2) for b in range(HALF)] + [("vp_0", 2)]
        alternating = [f"tok_{b}" for b in range(HALF, NB)] + ["vp_1"]
        for t in range(UNITS + LAG_OUT + 1):
            if t % G == 2:
                alternating += {1: ["wB"], 2: ["wO"], 3: ["wC1"], 4: ["wC2"]}.get(t // G, [])
            if t == PROJECT_AT:
                alternating += ["bq_0", "bk_0"]
            if t == PROJECT_AT + 3:
                alternating += ["bv_0"]
            for lag, names in ((LAG_PVTR, ("pvtr",)), (LAG_OUT, ("attnT",))):
                u = t - lag
                if 0 <= u < UNITS and u % G == G - 1:
                    alternating += [f"{name}_{u // G}" for name in names]
                    if lag == LAG_OUT and u // G == HALF - 1:
                        alternating += ["y0T_0"]
        alternating += ["y0T_1", "bq_1", "bk_1", "bv_1"]
        alternating += [f"y_{b}" for b in range(NB)]
        for half in "01":
            alternating += [f"{stage}_{half}" for stage in ("x1T", "ctxT", "h1", "gate", "soma", "mod")]
        alternating += ["tg_0", "o_0", "tg_1", "o_1", "zT_0", "lg_0", "zT_1", "lg_1", "rank"]
        order += [(name, 6 + n % 2) for n, name in enumerate(alternating)]
        job = {}
        served = [0] * 8
        for name, bank in order:
            job[name] = (bank, served[bank])
            served[bank] += 1
        misc_full = [sem(f"bank_full{i}") for i in range(8)]
        misc_read = [sem(f"bank_read{i}") for i in range(8)]
        bank_of = lambda name: ps[job[name][0]]

        def job_wait_free(eng, name):
            bank, n = job[name]
            if n:
                eng.wait_ge(misc_read[bank], n)

        def job_full(ins, name):
            ins.then_inc(misc_full[job[name][0]], 1)

        def job_wait_full(eng, name):
            eng.wait_ge(misc_full[job[name][0]], job[name][1] + 1)

        def job_read(ins, name):
            ins.then_inc(misc_read[job[name][0]], 1)

        def job_wait_read(eng, name):
            eng.wait_ge(misc_read[job[name][0]], job[name][1] + 1)

        ld_s2, ld_x, ld_wa, ld_cols, ld_len = sem("ld_s2"), sem("ld_x"), sem("ld_wa"), sem("ld_cols"), sem("ld_len")
        consts_ready = sem("consts_ready")
        vpad_zero = sem("vpad_zero")
        row_ready = sem("row_ready")
        ecols_ready = sem("ecols_ready")
        split_ready = sem("split_ready")
        high_ready = sem("high_ready")
        stack_in = [sem(f"stack_in{i}") for i in range(2)]
        rows_in = [sem("rows_in0"), sem("rows_in1")]
        s1_full, s1_read = sem("s1_full"), sem("s1_read")
        s2_full, s2_read = sem("s2_full"), sem("s2_read")
        pv_full, pv_read = sem("pv_full"), sem("pv_read")
        pv_done = sem("pv_done")
        negm_ready = sem("negm_ready")
        wself_ready = sem("wself_ready")
        sshift_ready = sem("sshift_ready")
        attn_ready = sem("attn_ready")
        norm_step = sem("norm_step")
        dve_step = sem("dve_step")
        pool_step = sem("pool_step")
        stack_zero = sem("stack_zero")
        wdh_ready = sem("wdh_ready")
        pool_pos = sem("pool_pos")
        rest_ready = sem("rest_ready")
        mid_ready = sem("mid_ready")
        mask_row_ready = sem("mask_row_ready")

        ld_wb, ld_wcr, ld_c, ld_f, ld_brow = sem("ld_wb"), sem("ld_wcr"), sem("ld_c"), sem("ld_f"), sem("ld_brow")
        ld_tau, ld_braw, ld_g1, ld_blend = sem("ld_tau"), sem("ld_braw"), sem("ld_g1"), sem("ld_blend")
        sb_full, sb_read = sem("sb_full"), sem("sb_read")
        wo_padded = sem("wo_padded")
        stats_ready = sem("stats_ready")
        mv_ready, rstd_ready = sem("mv_ready"), sem("rstd_ready")
        x1_ready, xb_ready = sem("x1_ready"), sem("xb_ready")
        band_ready = sem("band_ready")
        ema_ready, tau_ready, diff_ready, ema_exp = sem("ema_ready"), sem("tau_ready"), sem("diff_ready"), sem("ema_exp")
        tau_abs, tau_exp = sem("tau_abs"), sem("tau_exp")
        blend_sub, blend_exp, blend_ready = sem("blend_sub"), sem("blend_exp"), sem("blend_ready")
        gate_sig, gated_ready = sem("gate_sig"), sem("gated_ready")
        mod_sig, mod_ready = sem("mod_sig"), sem("mod_ready")
        Gd_ready, Gp_ready, G_used, ema_full, ema_read = sem("Gd_ready"), sem("Gp_ready"), sem("G_used"), sem("ema_full"), sem("ema_read")
        sg_ready, z_ready = sem("sg_ready"), sem("z_ready")
        lgm_sub, gexp_ready, onehot_ready, slot_ready, tmap_ready = sem("lgm_sub"), sem("gexp_ready"), sem("onehot_ready"), sem("slot_ready"), sem("tmap_ready")
        b_split, b_out = sem("b_split"), sem("b_out")
        z_zeroed, z_out = sem("z_zeroed"), sem("z_out")
        zs_in = [sem(f"zs_in{i}") for i in range(3)]
        brow_zero, tile_zero = sem("brow_zero"), sem("tile_zero")
        a_full, a_read = sem("zT_full"), sem("zT_read")
        h_full, h_read = sem("h_full"), sem("h_read")
        t_full, t_read = sem("hT_full"), sem("hT_read")
        y_full, y_read = sem("y_full"), sem("y_read")
        y_out, gate_ready, token_no = sem("y_out"), sem("gate_ready"), sem("token_no")
        rank_consts = sem("rank_consts")

        half_of = lambda b: b // HALF
        bc_mid = lambda ap, n: ap.unsqueeze(1).broadcast_to([ap.shape[0], n, ap.shape[1]])
        bc_last = lambda ap, n: ap.unsqueeze(2).broadcast_to([ap.shape[0], ap.shape[1], n])

        block = ctx.enter_context(nc.Block())

        @block.sync
        def _(sp):
            col = lambda a: a.rearrange("(p o) -> p o", o=1)
            sp.dma_start(s2_tok[:], A["fside_BxSxS_0"].rearrange("b s c -> s b c")).then_inc(ld_s2, 16)
            sp.dma_start(x_tok[:], A["x"].rearrange("b s c -> s b c")).then_inc(ld_x, 16)
            for i, n in enumerate(("q", "k", "v")):
                sp.dma_start(wqkv[:, i, :], A[f"L0_cond_W{n}"]).then_inc(ld_wa, 16)
                sp.dma_start(bqkv_bc[:, i, :], A[f"L0_cond_b{n}"].partition_broadcast(128)).then_inc(ld_wa, 16)
            sp.dma_start(cols[:, BPREV:BPREV + 1], A["L0_cond_b_prev"].rearrange("a b c -> c (a b)")).then_inc(ld_cols, 16)
            sp.dma_start(cols[:, BSELF:BSELF + 1], A["L0_cond_b_self"].rearrange("a b c -> c (a b)")).then_inc(ld_cols, 16)
            sp.dma_start(len_i[:], A["itok_B_18_1004"].rearrange("(o b) -> o b", o=1)).then_inc(ld_len, 16)
            sp.dma_start(wo[:], A["L0_cond_Wo"]).then_inc(ld_wb, 16)
            sp.dma_start(w_raw[:, 0, :], A["L0_attn_wq"]).then_inc(ld_wb, 16)
            sp.dma_start(w_raw[:, 1:3, :], A["L0_attn_wkv"].rearrange("(a p) c -> p a c", a=2)).then_inc(ld_wb, 16)
            sp.dma_start(wo_raw[:], A["L0_attn_wo"]).then_inc(ld_wb, 16)
            sp.dma_start(bo_bc[:], A["L0_cond_bo"].partition_broadcast(128)).then_inc(ld_wb, 16)
            sp.dma_start(cols[:, BO:BO + 1], col(A["L0_cond_bo"])).then_inc(ld_wb, 16)
            sp.dma_start(tau[:, 0:1], A["L0_cond2_tau_ctx"].partition_broadcast(128)).then_inc(ld_tau, 16)
            sp.dma_start(tau[:, 1:], A["condB_tauraws"].partition_broadcast(128)).then_inc(ld_tau, 16)
            sp.dma_start(blend[:], A["cond_1024"].partition_broadcast(128)).then_inc(ld_blend, 16)
            def constant_rows(half):
                row = mask_row[:, half * HALF:half * HALF + HALF, :].rearrange("o b t -> o (b t)")
                sp.dma_start(Ks[RMASK:R0, half], bc_mid(row, H)).then_inc(rows_in[half], 16)
                sp.dma_start(Qs[RMASK:R0, half], bc_mid(ones_row[:, 0:HT], H)).then_inc(rows_in[half], 16)

            def stack_up(att, half):
                n = 2 * att + half
                for part in range(3):
                    for which, stack in enumerate((Qs, Ks)):
                        sp.wait_ge((high_ready, mid_ready, split_ready)[part], 2 * n + which + 1)
                        for slot in range(NSLOT):
                            if PRODUCTS[which][slot] == part:
                                r0 = R0 + slot * DH
                                sp.dma_start(stack[r0:r0 + DH, half], parts[:, half, which, part, :])\
                                    .then_inc(stack_in[half], 16)

            sp.wait_ge(stack_zero, 2)
            stack_up(0, 0)
            sp.wait_ge(row_ready, 1)
            sp.wait_ge(mask_row_ready, 1)
            constant_rows(0)
            sp.wait_ge(stack_zero, 4)
            constant_rows(1)
            stack_up(0, 1)
            job_wait_read(sp, "trS2_1")
            sp.dma_start(b_raw[:, 0:FF], A["L0_ffn_b1"]).then_inc(ld_braw, 16)
            sp.dma_start(b_raw[:, FF:], A["L0_ffn_b2"]).then_inc(ld_braw, 16)
            sp.dma_start(gamma1[:], A["L0_attn_gamma"].partition_broadcast(128)).then_inc(ld_g1, 16)
            sp.dma_start(beta1[:], A["L0_attn_beta"].partition_broadcast(128)).then_inc(ld_g1, 16)
            sp.dma_start(wc_raw[:, 0:2, :], A["L0_cond2_Wg"].rearrange("e (a c) -> e a c", a=2)).then_inc(ld_wcr, 16)
            for i, n in enumerate(("Wsoma", "Wtemp", "Wout")):
                sp.dma_start(wc_raw[:, 2 + i, :], A[f"L0_cond2_{n}"]).then_inc(ld_wcr, 16)
            sp.dma_start(wn1_raw[:], A["L0_cond2_Wn1"]).then_inc(ld_wcr, 16)
            sp.dma_start(wn2_raw[:], A["cond_256"]).then_inc(ld_wcr, 16)
            for dst, n in ((bg_bc, "L0_cond2_bg"), (bn2_bc, "condB_bn2"), (gamma2, "L0_cond2_gamma"),
                           (beta2, "L0_cond2_beta"), (br_bc, "L0_ffn_br")):
                sp.dma_start(dst[:], A[n].partition_broadcast(128)).then_inc(ld_c, 16)
            sp.dma_start(cols[:, BSOMA:BSOMA + 1], col(A["L0_cond2_bsoma"])).then_inc(ld_c, 16)
            sp.dma_start(cols[:, BTEMP:BTEMP + 1], col(A["L0_cond2_btemp"])).then_inc(ld_c, 16)
            sp.dma_start(cols[0:NH1, BN1:BN1 + 1], col(A["L0_cond2_bn1"])).then_inc(ld_c, 16)
            sp.dma_start(wr[:], A["L0_ffn_Wr"]).then_inc(ld_c, 16)
            sp.wait_ge(tile_zero, 1)
            sp.dma_start(z_dram.rearrange("(i p) c -> p i c", p=128), bc_mid(empty_row[:], TILES)).then_inc(z_zeroed, 16)
            sp.wait_ge(b_split, 3)
            sp.dma_start(b_dram.rearrange("q e f -> e q f"), b_parts[:]).then_inc(b_out, 16)
            for half in range(2):
                sp.wait_ge(s2_full, G * HALF * (half + 1))
                sp.dma_start(Qs[RMASK:R0, half], bc_mid(ones_row[:, HT:2 * HT], H)).then_inc(stack_in[half], 16)
                stack_up(1, half)
            sp.wait_ge(b_out, 16)
            sp.wait_ge(brow_zero, 1)
            sp.dma_start(b_rows[0:3], b_dram).then_inc(ld_brow, 16)
            sp.wait_ge(sb_full, G * NB)
            sp.dma_start(W1[:], A["L0_ffn_W1"].rearrange("e d f -> d e f")).then_inc(ld_f, 16)
            sp.dma_start(W2[:], A["L0_ffn_W2"].rearrange("e (k p) d -> p e k d", p=128)).then_inc(ld_f, 16)
            sp.wait_ge(z_out, 16 * NB)
            third = TILES // 3
            for k in range(3):
                sp.dma_start(zs[:, k * third:(k + 1) * third, :],
                             z_dram[k * third * 128:(k + 1) * third * 128].rearrange("(i p) c -> p i c", p=128))\
                    .then_inc(zs_in[k], 16)

        @block.gpsimd
        def _(pool):
            steps = [0]

            def link(ins):
                steps[0] += 1
                ins.then_inc(pool_step, 1)
                pool.wait_ge(pool_step, steps[0])

            link(pool.memset(ident[:], 1.0))
            zero_rows = lambda stack, half: pool.memset(stack[0:64, half].bitcast(F32), 0.0).then_inc(stack_zero, 1)
            pool.affine_select(ident[:], ident[:], pattern=[[1, 128]], compare_op=ALU.is_equal, fill=0.0,
                               base=0, channel_multiplier=-1).then_inc(consts_ready, 1)
            link(pool.memset(ones_row[:, HT:2 * HT], 0.0))
            pool.memset(ones_row[:, 0:HT], 1.0).then_inc(row_ready, 1)
            pool.iota(pos_row[:], pattern=[[0, NB], [1, T]], base=0, channel_multiplier=0,
                      allow_small_or_imprecise_dtypes=True).then_inc(pool_pos, 1)
            pool.wait_ge(consts_ready, 1)
            pool.tensor_copy(identb[:], ident[:]).then_inc(consts_ready, 1)
            zero_rows(Qs, 0)
            zero_rows(Ks, 0)
            def zero_values(half):
                bs = slice(half * HALF, half * HALF + HALF)
                link(pool.memset(v_pad[:, bs], 0.0))
                pool.memset(v_pad[:, bs, :, DH:DH + 1], 1.0).then_inc(vpad_zero, 1)

            zero_values(0)
            zero_rows(Qs, 1)
            zero_rows(Ks, 1)
            zero_values(1)
            link(pool.iota(diff[:], pattern=[[1, 128]], base=0, channel_multiplier=-1,
                           allow_small_or_imprecise_dtypes=True))
            pool.tensor_scalar(diff[:], diff[:], 0.0, None, ALU.max).then_inc(diff_ready, 1)
            link(pool.memset(empty_row[:], 0.0))
            pool.iota(empty_row[:, TOKEN:TOKEN + 1].bitcast(I32), pattern=[[0, 1]], base=NT, channel_multiplier=1)\
                .then_inc(tile_zero, 1)
            link(pool.memset(wo_rp[:], 0.0))
            pool.wait_ge(ld_wb, 16 * 6)
            pool.tensor_copy(wo_rp[:, :, 0:DH], wo_raw[:].rearrange("p (h d) -> p h d", d=DH)).then_inc(wo_padded, 1)
            link(pool.memset(bandb[:], 0.0))
            link(pool.affine_select(bandb[:], bandb[:], pattern=[[1, 128]], compare_op=ALU.is_ge,
                                    fill=MASKED, base=-1, channel_multiplier=-1))
            pool.affine_select(bandb[:], bandb[:], pattern=[[-1, 128]], compare_op=ALU.is_ge,
                               fill=MASKED, base=WINDOW, channel_multiplier=1).then_inc(band_ready, 1)
            pool.wait_ge(ld_braw, 32)
            pool.tensor_copy(b_parts[:, 0, :], b_raw[:]).then_inc(b_split, 1)
            pool.wait_ge(b_split, 1)
            link(pool.tensor_tensor(b_rest[:], b_raw[:], b_parts[:, 0, :], ALU.subtract))
            pool.tensor_copy(b_parts[:, 1, :], b_rest[:]).then_inc(b_split, 1)
            pool.wait_ge(b_split, 2)
            pool.tensor_tensor(b_parts[:, 2, :], b_rest[:], b_parts[:, 1, :], ALU.subtract).then_inc(b_split, 1)
            pool.wait_ge(ema_exp, 1)
            pool.affine_select(ema[:], ema[:], pattern=[[0, ND + 1], [1, 128]], compare_op=ALU.is_ge,
                               fill=0.0, base=0, channel_multiplier=-1).then_inc(ema_ready, 1)
            pool.wait_ge(ld_g1, 32)
            job_wait_full(pool, "trX_1")
            pool.tensor_tensor(xb[:], x_tok[:], bc_mid(beta1[:], NB), ALU.add).then_inc(xb_ready, 1)
            link(pool.memset(onehotb[:, 0:NB], 0.0))
            link(pool.memset(onesb[:], 1.0))
            link(pool.affine_select(trib[:], onesb[:], pattern=[[1, 128]], compare_op=ALU.is_gt, fill=0.0,
                                    base=0, channel_multiplier=-1))
            link(pool.iota(em8[:], pattern=[[1, NE]], base=-NE, channel_multiplier=0,
                           allow_small_or_imprecise_dtypes=True))
            link(pool.iota(k128[:], pattern=[[128, NB]], base=0, channel_multiplier=0,
                           allow_small_or_imprecise_dtypes=True))
            link(pool.iota(tile_no[:], pattern=[[1, TILES]], base=0, channel_multiplier=0,
                           allow_small_or_imprecise_dtypes=True))
            link(pool.memset(tri8[:], 1.0))
            pool.affine_select(tri8[:], tri8[:], pattern=[[1, NE], [-1, NE]], compare_op=ALU.is_gt, fill=0.0,
                               base=0, channel_multiplier=0).then_inc(rank_consts, 1)
            link(pool.memset(mhalf[:], -0.5))
            pool.wait_ge(b_split, 3)
            job_wait_full(pool, "trS2_1")
            pool.iota(rows[:, :, TOKEN:TOKEN + 1].bitcast(I32), pattern=[[T, NB], [0, 1]], base=0, channel_multiplier=1)\
                .then_inc(token_no, 1)
            pool.wait_ge(attn_ready, NB)
            pool.memset(b_rows[:], 0.0).then_inc(brow_zero, 1)

            def inverse_std(n, bs):
                pool.wait_ge(mv_ready, HALF * (n + 1))
                link(pool.tensor_scalar(rstd[:, bs], mv[:, bs, 1], EPS, None, ALU.add))
                pool.tensor_tensor(rstd[:, bs], rstd[:, bs], mhalf[:, bs], ALU.pow).then_inc(rstd_ready, 1)

            inverse_std(0, slice(0, HALF))
            inverse_std(1, slice(HALF, NB))

            for b in range(NB):
                k = b % 2
                pool.wait_ge(gated_ready, half_of(b) + 1)
                pool.wait_ge(mod_ready, half_of(b) + 1)
                pool.wait_ge(blend_ready, 1)
                if b >= 2:
                    pool.wait_ge(G_used, b - 1)
                ds = slice(ND - PD, ND)
                link(pool.tensor_tensor(Gb[:, k, ds, :], bc_mid(wgate[:, b, :], PD), blend[:, ds, :], ALU.mult))
                pool.tensor_tensor(Gb[:, k, ds, :], Gb[:, k, ds, :], bc_last(mod[:, b, ds], D), ALU.mult)\
                    .then_inc(Gp_ready, 1)

            inverse_std(2, slice(0, HALF))
            inverse_std(3, slice(HALF, NB))

            pool.wait_ge(slot_ready, 1)
            pool.wait_ge(gate_ready, 1)
            pool.wait_ge(z_ready, 2)
            pool.wait_ge(token_no, 1)
            pool.wait_ge(z_zeroed, 16)
            for b in range(NB):
                pool.indirect_dma_start(out=z_dram, out_offset=bass.IndirectOffsetOnAxis(slot[:, b:b + 1], 0),
                                        in_=rows[:, b, :], in_offset=None).then_inc(z_out, 16)
            for i in range(TILES):
                pool.wait_ge(y_read, i + 1)
                pool.indirect_dma_start(
                    out=out.rearrange("b s c -> (b s) c"),
                    out_offset=bass.IndirectOffsetOnAxis(zs[:, i, TOKEN:TOKEN + 1].bitcast(U32), 0),
                    in_=ys[:, i, :], in_offset=None, bounds_check=NT - 1, oob_is_err=False).then_inc(y_out, 16)
            pool.wait_ge(y_out, 16 * TILES)

        @block.tensor
        def _(pe):
            def transposes(name, src, count, wait=None):
                job_wait_free(pe, name)
                for i in range(count):
                    m = pe.transpose(bank_of(name)[:, i * 128:(i + 1) * 128], src(i), ident[:])
                job_full(m, name)

            def dense(name, lhsT, rhs, cols_, start=True):
                job_wait_free(pe, name)
                m = pe.matmul(bank_of(name)[:, 0:cols_], lhsT, rhs, start=True, stop=True)
                job_full(m, name)

            def transpose_inputs(half):
                if half == 0:
                    pe.wait_ge(consts_ready, 1)
                    pe.wait_ge(ld_s2, 16)
                transposes(f"trS2_{half}", lambda i: s2_tok[:, half * HALF + i, :], 4)
                if half == 0:
                    pe.wait_ge(ld_x, 16)
                transposes(f"trX_{half}", lambda i: x_tok[:, half * HALF + i, :], 4)

            def project_qk(half):
                cs = slice(half * HT, half * HT + HT)
                job_wait_read(pe, f"trS2_{half}")
                dense(f"qT_{half}", w_dh[:, 0, :], s2T[:, cs], HT)
                job_wait_read(pe, f"trX_{half}")
                dense(f"kT_{half}", w_dh[:, 1, :], xT[:, cs], HT)

            def project_tok(b):
                dense(f"tok_{b}", s2T[:, b * T:(b + 1) * T], wqkv[:].rearrange("p a b -> p (a b)"), 3 * D)

            def four_batches(name, half, src, rhs):
                job_wait_free(pe, name)
                for i in range(HALF):
                    b = half * HALF + i
                    m = pe.matmul(bank_of(name)[:, i * D:(i + 1) * D], src[:, b * T:(b + 1) * T], rhs, start=True, stop=True)
                job_full(m, name)

            def stacked(stack, b, h):
                return stack[:, half_of(b), h, (b % HALF) * T:(b % HALF + 1) * T]

            def scores_max(b, g):
                u = b * G + g
                if u == 0:
                    job_wait_read(pe, "qT_1")
                    job_wait_read(pe, "kT_1")
                if b % HALF == 0 and g == 0:
                    pe.wait_ge(rows_in[half_of(b)], 32)
                    pe.wait_ge(stack_in[half_of(b)], 16 * 2 * NSLOT)
                if u >= 2:
                    pe.wait_ge(s1_read, u - 1)
                for j in range(4):
                    h = 4 * g + j
                    m = pe.matmul(S1B[u % 2][:, j * T:(j + 1) * T], stacked(Qs, b, h), stacked(Ks, b, h),
                                  start=True, stop=True)
                m.then_inc(s1_full, 1)

            def scores(b, g):
                u = b * G + g
                pe.wait_ge(negm_ready, b + 1)
                if u == 0:
                    job_wait_read(pe, "vp_0")
                    job_wait_read(pe, "kT_0")
                    job_wait_read(pe, "trX_1")
                if u >= 2:
                    pe.wait_ge(s2_read, u - 1)
                for j in range(4):
                    h = 4 * g + j
                    o = S2B[u % 2][:, j * T:(j + 1) * T]
                    pe.matmul(o, stacked(Ks, b, h), stacked(Qs, b, h), start=True, stop=False)
                    m = pe.matmul(o, negm[:, b, h:h + 1].broadcast_to([128, 128]), identb[:], start=False, stop=True)
                m.then_inc(s2_full, 1)

            def values(b, g):
                u = b * G + g
                pe.wait_ge(s2_read, u + 1)
                if g == 0:
                    job_wait_read(pe, f"vp_{half_of(b)}")
                    if b >= 2:
                        pe.wait_ge(pv_read, b - 1)
                for j in range(4):
                    m = pe.matmul(PVB[b % 2][32 * j:32 * j + 32, g * T:(g + 1) * T], v_pad[:, b, 4 * g + j, :],
                                  P[:, u % 3, j * T:(j + 1) * T], start=True, stop=True)
                m.then_inc(pv_done, 1)

            def wide(name, lhsT, rhs):
                dense(name, lhsT, rhs, HT)

            def project_window_y(half):
                job_wait_read(pe, f"attnT_{half * HALF + HALF - 1}")
                wide(f"y0T_{half}", wo[:], attnT[:, half * HT:half * HT + HT])

            def project_window_qk(half):
                job_wait_read(pe, "wB")
                job_wait_read(pe, f"y0T_{half}")
                wide(f"bq_{half}", wB[:, 0, :], y0T[:, half * HT:half * HT + HT])
                wide(f"bk_{half}", wB[:, 1, :], y0T[:, half * HT:half * HT + HT])

            def project_window_v(half):
                four_batches(f"bv_{half}", half, y0T, wB[:, 2, :])

            def weight_job(i):
                if i == 1:
                    pe.wait_ge(ld_wb, 16 * 6)
                    transposes("wB", lambda k: w_raw[:, k, :], 3)
                if i == 2:
                    pe.wait_ge(wo_padded, 1)
                    transposes("wO", lambda k: wo_rp[:, 4 * k:4 * k + 4, :].rearrange("p a b -> p (a b)"), 4)
                if i == 3:
                    pe.wait_ge(ld_wcr, 16 * 6)
                    transposes("wC1", lambda k: wc_raw[:, k, :], 4)
                if i == 4:
                    job_wait_free(pe, "wC2")
                    bank = bank_of("wC2")
                    pe.transpose(bank[:, 0:128], wc_raw[:, 4, :], ident[:])
                    pe.transpose(bank[:, 128:128 + NH1], wn1_raw[:], ident[0:NH1, 0:NH1])
                    job_full(pe.transpose(bank[0:NH1, 160:160 + ND], wn2_raw[:], ident[0:ND, 0:ND]), "wC2")

            transpose_inputs(0)
            pe.wait_ge(ld_wa, 16 * 6)
            pe.wait_ge(ld_cols, 16 * 2)
            job_wait_free(pe, "bcols")
            pe.wait_ge(wdh_ready, 4)
            for i, added in enumerate((BSELF, BPREV)):
                o = bank_of("bcols")[:, i:i + 1]
                pe.matmul(o, w_dh[:, i, :], cols[:, added:added + 1], start=True, stop=False)
                m = pe.matmul(o, b_dh[:, i, :], ident[0:1, 0:1], start=False, stop=True)
            job_full(m, "bcols")
            dense("bbc", cols[:, BSELF:BSELF + 1].broadcast_to([128, 128]),
                  wqkv[:, 0:2, :].rearrange("p a b -> p (a b)"), 2 * D)
            project_qk(0)
            transpose_inputs(1)
            project_qk(1)
            for b in range(HALF):
                project_tok(b)
            four_batches("vp_0", 0, xT, wqkv[:, 2, :])

            for t in range(UNITS + LAG_OUT + 1):
                if t < UNITS:
                    scores_max(t // G, t % G)
                if t in (1, 2, 3, 4):
                    project_tok(HALF + t - 1)
                if t == 5:
                    four_batches("vp_1", 1, xT, wqkv[:, 2, :])
                if t % G == 2:
                    weight_job(t // G)
                u = t - LAG_SCORES
                if 0 <= u < UNITS:
                    scores(u // G, u % G)
                u = t - LAG_VALUES
                if 0 <= u < UNITS:
                    values(u // G, u % G)
                if t == PROJECT_AT:
                    project_window_qk(0)
                if t == PROJECT_AT + 3:
                    project_window_v(0)
                u = t - LAG_PVTR
                if 0 <= u < UNITS and u % G == G - 1:
                    b = u // G
                    pe.wait_ge(pv_read, b + 1)
                    transposes(f"pvtr_{b}", lambda k: pv_sb[:, b % 2, k * 128:(k + 1) * 128], 4)
                u = t - LAG_OUT
                if 0 <= u < UNITS and u % G == G - 1:
                    b = u // G
                    pe.wait_ge(attn_ready, b + 1)
                    transposes(f"attnT_{b}", lambda k: attn[:, b % 2, :], 1)
                    if b == HALF - 1:
                        project_window_y(0)
            project_window_y(1)
            project_window_qk(1)
            project_window_v(1)

            def window_scores(b, g):
                u = b * G + g
                if u == 0:
                    pe.wait_ge(s1_read, G * NB)
                    pe.wait_ge(s2_read, G * NB)
                    pe.wait_ge(band_ready, 1)
                if b % HALF == 0 and g == 0:
                    pe.wait_ge(stack_in[half_of(b)], 16 * (4 * NSLOT + 1))
                if u >= 4:
                    pe.wait_ge(sb_read, u - 3)
                bank = ps[u % 4]
                for j in range(4):
                    h = 4 * g + j
                    pe.matmul(bank[:, j * T:(j + 1) * T], stacked(Ks, b, h), stacked(Qs, b, h), start=True, stop=False)
                    m = pe.matmul(bank[:, j * T:(j + 1) * T], identb[:], bandb[:], start=False, stop=True)
                m.then_inc(sb_full, 1)

            def window_values(b, g):
                u = b * G + g
                pe.wait_ge(sb_read, u + 1)
                if g == 0:
                    job_wait_read(pe, f"bv_{half_of(b)}")
                    pe.wait_ge(pv_read, NB + b - 1)
                for j in range(4):
                    m = pe.matmul(PVB[b % 2][32 * j:32 * j + 32, g * T:(g + 1) * T], v_pad[:, b, 4 * g + j, :],
                                  P[:, u % 3, j * T:(j + 1) * T], start=True, stop=True)
                m.then_inc(pv_done, 1)

            def window_out(b):
                pe.wait_ge(pv_read, NB + b + 1)
                if b == 0:
                    job_wait_read(pe, "wO")
                name = f"y_{b}"
                job_wait_free(pe, name)
                o = bank_of(name)[:, 0:D]
                pe.matmul(o, attnT[:, b * T:(b + 1) * T], wo[:], start=True, stop=False)
                for g in range(G):
                    m = pe.matmul(o, pv_sb[:, b % 2, g * T:(g + 1) * T], woT[:, g, :], start=False, stop=(g == G - 1))
                job_full(m, name)

            for u in range(G * NB + 2):
                if u < G * NB:
                    window_scores(u // G, u % G)
                if u >= 2:
                    window_values((u - 2) // G, (u - 2) % G)
                if u >= 8 and u % G == 0:
                    window_out(u // G - 2)
            window_out(NB - 1)

            def by_batch(name, half, lhsT, rhs, n):
                job_wait_free(pe, name)
                for i in range(HALF):
                    b = half * HALF + i
                    for k in range(len(lhsT)):
                        m = pe.matmul(bank_of(name)[:, i * n:(i + 1) * n], lhsT[k](b), rhs[k], start=(k == 0),
                                      stop=(k == len(lhsT) - 1))
                job_full(m, name)

            tok = lambda src: lambda b: src[:, b * T:(b + 1) * T]
            def ema_front(half):
                hs_ = slice(half * HT, half * HT + HT)
                pe.wait_ge(x1_ready, half + 1)
                transposes(f"x1T_{half}", lambda i: x1[:, half * HALF + i, :], 4)
                if half == 0:
                    pe.wait_ge(ema_ready, 1)
                by_batch(f"ctxT_{half}", half, [lambda b: x1[:, b, :]], [ema[:, 0, :]], T)
                if half == 0:
                    job_wait_read(pe, "wC1")
                    job_wait_read(pe, "wC2")
                job_wait_read(pe, f"x1T_{half}")
                name = f"h1_{half}"
                job_wait_free(pe, name)
                job_full(pe.matmul(bank_of(name)[0:NH1, :], wn1T[:], x1T[:, hs_], start=True, stop=True), name)
                job_wait_read(pe, f"ctxT_{half}")
                by_batch(f"gate_{half}", half, [tok(x1T), tok(ctxT)], [wC[:, 0, :], wC[:, 1, :]], D)
                wide(f"soma_{half}", wC[:, 2, :], x1T[:, hs_])
                job_wait_read(pe, f"h1_{half}")
                by_batch(f"mod_{half}", half, [tok(h1T)], [wn2T[:]], ND)

            def traces(b):
                pe.wait_ge(Gd_ready, b + 1)
                pe.wait_ge(Gp_ready, b + 1)
                if b == 0:
                    pe.wait_ge(sb_read, UNITS)
                for d in range(ND):
                    m = pe.matmul(ps[half_of(b)][:, (b % HALF) * T:(b % HALF + 1) * T], Gb[:, b % 2, d, :],
                                  ema[:, 1 + d, :], start=(d == 0), stop=(d == ND - 1))
                m.then_inc(G_used, 1)

            def gate_of(half):
                pe.wait_ge(ema_read, half + 1)
                wide(f"tg_{half}", wC[:, 3, :], tempT[:, half * HT:half * HT + HT])

            def output_of(half):
                pe.wait_ge(sg_ready, half + 1)
                by_batch(f"o_{half}", half, [tok(gateT)], [wC[:, 4, :]], D)

            ema_front(0)
            ema_front(1)
            for b in range(NB):
                traces(b)
                if b == HALF:
                    gate_of(0)
                if b == NB - 2:
                    output_of(0)
            gate_of(1)
            output_of(1)
            for half in range(2):
                pe.wait_ge(z_ready, half + 1)
                transposes(f"zT_{half}", lambda i: z[:, half * HALF + i, :], 4)
                job_wait_read(pe, f"zT_{half}")
                if half == 0:
                    pe.wait_ge(ld_c, 16 * 9)
                by_batch(f"lg_{half}", half, [tok(zT)], [wr[:]], NE)

            pe.wait_ge(onehot_ready, 1)
            pe.wait_ge(rank_consts, 1)
            job_wait_free(pe, "rank")
            bank = bank_of("rank")
            oh = onehotb[:].rearrange("p b e -> p (b e)")
            W = NB * NE
            pe.matmul(bank[:, 0:W], trib[:], oh[:, W:2 * W], start=True, stop=False)
            for k in range(1, NB):
                pe.matmul(bank[:, 0:W], onesb[:], oh[:, W - k * NE:2 * W - k * NE], start=False, stop=(k == NB - 1))
            for b in range(NB):
                m = pe.matmul(bank[:, W:W + NE], onesb[:], oh[:, W + b * NE:W + (b + 1) * NE], start=(b == 0),
                              stop=(b == NB - 1))
            job_full(m, "rank")

            pe.wait_ge(tmap_ready, 1)
            pe.wait_ge(ld_f, 32)
            pe.wait_ge(ld_brow, 16)
            pe.wait_ge(ema_read, 2)
            job_wait_read(pe, "rank")
            expert = {}
            for i in range(TILES + 3):
                if i < TILES:
                    pe.wait_ge(zs_in[i // (TILES // 3)], 16)
                    if i >= 2:
                        pe.wait_ge(a_read, i - 1)
                    pe.transpose(ps[4 + i % 2][:, 0:128], zs[:, i, 0:D], ident[:]).then_inc(a_full, 1)
                if 1 <= i <= TILES:
                    n = i - 1
                    e = pe.value_load(tmap[0:1, n:n + 1], min_val=0, max_val=NE - 1)
                    expert[n] = e
                    pe.wait_ge(a_read, n + 1)
                    if n >= 2:
                        pe.wait_ge(h_read, n - 1)
                    pe.matmul(ps[n % 2][:, :], zsT[:, n % 2, :], W1[:, bass.ds(e, 1), :].rearrange("p a f -> p (a f)"),
                              start=True, stop=False)
                    pe.matmul(ps[n % 2][:, :], onesb[0:KROWS, :], b_rows[:, bass.ds(e, 1), 0:FF].rearrange("p a f -> p (a f)"),
                              start=False, stop=True).then_inc(h_full, 1)
                if 2 <= i <= TILES + 1:
                    n = i - 2
                    pe.wait_ge(h_read, n + 1)
                    if n >= 2:
                        pe.wait_ge(t_read, n - 1)
                    for c in range(FC):
                        m = pe.transpose(ps[2 + n % 2][:, c * 128:(c + 1) * 128], hs[:, n % 2, c * 128:(c + 1) * 128],
                                         ident[:])
                    m.then_inc(t_full, 1)
                if i >= 3:
                    n = i - 3
                    e = expert[n]
                    pe.wait_ge(t_read, n + 1)
                    if n >= 2:
                        pe.wait_ge(y_read, n - 1)
                    o = ps[6 + n % 2][:, 0:D]
                    for c in range(FC):
                        pe.matmul(o, hsT[:, n % 2, c * 128:(c + 1) * 128],
                                  W2[:, bass.ds(e, 1), c, :].rearrange("p a f -> p (a f)"), start=(c == 0), stop=False)
                    pe.matmul(o, onesb[0:KROWS, :], b_rows[:, bass.ds(e, 1), FF:].rearrange("p a f -> p (a f)"),
                              start=False, stop=True).then_inc(y_full, 1)

        @block.scalar
        def _(act):
            def split_high(name, which, n, bias=None):
                job_wait_full(act, name)
                if n:
                    act.wait_ge(rest_ready, 2 * (n - 1) + which + 1)
                if n >= 2:
                    act.wait_ge(stack_in[n % 2], 16 * 2 * NSLOT)
                bank = bank_of(name)
                add = {} if bias is None else {"bias": bias}
                act.activation(parts[:, n % 2, which, 0, :], bank[:, 0:HT], ACT.Identity, **add).then_inc(high_ready, 1)
                job_read(act.activation(qf[:, which, :], bank[:, 0:HT], ACT.Identity, **add), name)

            def split_middle(which, n):
                act.wait_ge(rest_ready, 2 * n + which + 1)
                act.copy(parts[:, n % 2, which, 1, :], rest[:, which, :]).then_inc(mid_ready, 1)

            job_wait_read(act, "bcols")
            for half in range(2):
                split_high(f"qT_{half}", 0, half, ecols[:, 0:1])
                split_high(f"kT_{half}", 1, half, ecols[:, 1:2])
                split_middle(0, half)
                split_middle(1, half)

            def weights_of(u):
                act.wait_ge(s2_full, u + 1)
                if u >= 3:
                    act.wait_ge(pv_done, u - 2)
                act.activation(P[:, u % 3, :], S2B[u % 2][:, :], ACT.Exp, scale=SCALE).then_inc(s2_read, 1)

            def evac_y0T(half):
                name = f"y0T_{half}"
                job_wait_full(act, name)
                if half == 0:
                    act.wait_ge(ld_wb, 16 * 6)
                job_read(act.activation(y0T[:, half * HT:half * HT + HT], bank_of(name)[:, :], ACT.Identity,
                                        bias=cols[:, BO:BO + 1]), name)

            def split_window(half):
                split_high(f"bq_{half}", 0, 2 + half)
                split_high(f"bk_{half}", 1, 2 + half)
                split_middle(0, 2 + half)
                split_middle(1, 2 + half)

            def window_pv(b):
                act.wait_ge(pv_done, G * (NB + b + 1))
                if b >= 2:
                    job_wait_full(act, f"y_{b-2}")
                else:
                    job_wait_full(act, f"pvtr_{NB-2+b}")
                act.copy(pv_sb[:, b % 2, :], PVB[b % 2][:, :]).then_inc(pv_read, 1)

            act.wait_ge(tau_abs, 1)
            act.activation(tau2[:], tau2[:], ACT.Exp, scale=-1.0).then_inc(tau_exp, 1)
            act.wait_ge(tau_exp, 1)
            act.activation(tau2[:], tau2[:], ACT.Ln, bias=1.0).then_inc(tau_exp, 1)
            for t in range(UNITS + LAG_OUT + 1):
                if t >= G and t % G == 0 and t <= UNITS:
                    b = t // G - 1
                    act.wait_ge(sshift_ready, b + 1)
                    act.activation(w_self[:, b, :], sshift[:, b, :], ACT.Exp, scale=SCALE).then_inc(wself_ready, 1)
                u = t - LAG_SCORES
                if 0 <= u < UNITS:
                    weights_of(u)
                u = t - LAG_VALUES - 1
                if 0 <= u < UNITS and u % G == G - 1:
                    b = u // G
                    act.wait_ge(pv_done, G * (b + 1))
                    if b >= 2:
                        job_wait_full(act, f"pvtr_{b-2}")
                    act.copy(pv_sb[:, b % 2, :], PVB[b % 2][:, :]).then_inc(pv_read, 1)
                if t == 2 * G:
                    act.wait_ge(tau_ready, 1)
                    act.wait_ge(diff_ready, 1)
                d = t - 2 * G
                if 0 <= d <= ND:
                    m = act.activation(ema[:, d, :], diff[:], ACT.Exp, scale=tau2[:, d:d + 1])
                    if d == ND:
                        m.then_inc(ema_exp, 1)
                if t == G + 2:
                    act.wait_ge(blend_sub, 1)
                    act.activation(blend[:], blend[:], ACT.Exp).then_inc(blend_exp, 1)
                if t == PROJECT_AT:
                    split_window(0)
                u = t - LAG_OUT
                if 0 <= u < UNITS and u % G == G - 1:
                    b = u // G
                    job_wait_full(act, f"attnT_{b}")
                    job_read(act.copy(attnT[:, b * T:(b + 1) * T], bank_of(f"attnT_{b}")[:, 0:T]), f"attnT_{b}")
                    if b == HALF - 1:
                        evac_y0T(0)
            evac_y0T(1)
            split_window(1)

            for u in range(G * NB + 2):
                if u < G * NB:
                    act.wait_ge(sb_full, u + 1)
                    act.wait_ge(pv_done, G * NB + u - 2)
                    act.activation(P[:, u % 3, :], ps[u % 4][:, :], ACT.Sigmoid, scale=SCALE).then_inc(sb_read, 1)
                if u >= 5 and (u - 5) % G == 0:
                    window_pv((u - 5) // G)

            def evac(name, dst, rows=128):
                job_wait_full(act, name)
                job_read(act.copy(dst, bank_of(name)[0:rows, 0:HT]), name)

            cut = lambda buf, half: buf[:, half * HT:half * HT + HT]
            def front(half):
                evac(f"x1T_{half}", cut(x1T, half))
                evac(f"ctxT_{half}", cut(ctxT, half))
                if half == 0:
                    act.wait_ge(ld_c, 16 * 9)
                name = f"h1_{half}"
                job_wait_full(act, name)
                job_read(act.activation(cut(h1T, half), bank_of(name)[0:NH1, :], ACT.Gelu,
                                        bias=cols[0:NH1, BN1:BN1 + 1]), name)
                name = f"soma_{half}"
                job_wait_full(act, name)
                job_read(act.activation(cut(somaT, half), bank_of(name)[:, :], ACT.Gelu,
                                        bias=cols[:, BSOMA:BSOMA + 1]), name)
                bs = slice(half * HALF, half * HALF + HALF)
                job_wait_read(act, f"gate_{half}")
                act.activation(wgate[:, bs, :], wgate[:, bs, :], ACT.Sigmoid).then_inc(gate_sig, 1)
                job_wait_read(act, f"mod_{half}")
                act.activation(mod[:, bs, :], mod[:, bs, :], ACT.Sigmoid).then_inc(mod_sig, 1)

            def back(half):
                act.wait_ge(G_used, HALF * (half + 1))
                act.copy(cut(tempT, half), ps[half][:, :]).then_inc(ema_read, 1)
                name = f"tg_{half}"
                job_wait_full(act, name)
                job_read(act.activation(cut(gateT, half), bank_of(name)[:, :], ACT.Sigmoid,
                                        bias=cols[:, BTEMP:BTEMP + 1]), name)

            front(0)
            front(1)
            back(0)
            evac("o_0", o_sb[:, 0:HALF, :].rearrange("p b c -> p (b c)"))
            back(1)
            evac("o_1", o_sb[:, HALF:NB, :].rearrange("p b c -> p (b c)"))
            for half in range(2):
                evac(f"zT_{half}", cut(zT, half))
            act.wait_ge(lgm_sub, 1)
            act.activation(gexp[:], gexp[:], ACT.Exp).then_inc(gexp_ready, 1)

            for i in range(TILES + 1):
                if i < TILES:
                    act.wait_ge(a_full, i + 1)
                    if i >= 2:
                        act.wait_ge(h_full, i - 1)
                    act.copy(zsT[:, i % 2, :], ps[4 + i % 2][:, 0:128]).then_inc(a_read, 1)
                if i >= 1:
                    n = i - 1
                    act.wait_ge(h_full, n + 1)
                    if n >= 2:
                        act.wait_ge(t_full, n - 1)
                    act.activation(hs[:, n % 2, :], ps[n % 2][:, :], ACT.Gelu).then_inc(h_read, 1)

        @block.vector
        def _(dve):
            counts = {}

            def link(ins, s=dve_step):
                counts[id(s)] = counts.get(id(s), 0) + 1
                ins.then_inc(s, 1)
                dve.wait_ge(s, counts[id(s)])

            def link_job(ins, name):
                job_read(ins, name)
                job_wait_read(dve, name)

            def evac_transposes(name, dst):
                job_wait_full(dve, name)
                job_read(dve.tensor_copy(dst, bank_of(name)[:, 0:HT]), name)

            evac_transposes("trS2_0", s2T[:, 0:HT])
            evac_transposes("trX_0", xT[:, 0:HT])
            dve.wait_ge(ld_wa, 16 * 6)
            for i in range(2):
                link(dve.tensor_copy(w_dh[:, i, :].rearrange("p (d h) -> p d h", h=H),
                                     wqkv[:, i, :].rearrange("p (h d) -> p d h", d=DH)), wdh_ready)
                link(dve.tensor_copy(b_dh[:, i, :].rearrange("p (d h) -> p d h", h=H),
                                     bqkv_bc[0:1, i, :].rearrange("p (h d) -> p d h", d=DH)), wdh_ready)

            def token_major(b):
                name = f"tok_{b}"
                job_wait_full(dve, name)
                link_job(dve.tensor_tensor(tokA[:, b].rearrange("p a b -> p (a b)"), bank_of(name)[:, 0:3 * D],
                                           bqkv_bc[:].rearrange("p a b -> p (a b)"), ALU.add), name)

            def v_prev(half):
                name = f"vp_{half}"
                bs = slice(half * HALF, half * HALF + HALF)
                job_wait_full(dve, name)
                dve.wait_ge(vpad_zero, half + 1)
                for b in range(half * HALF, half * HALF + HALF):
                    m = dve.tensor_tensor(v_pad[:, b, :, 0:DH],
                                          bank_of(name)[:, (b % HALF) * D:(b % HALF + 1) * D].rearrange("p (h d) -> p h d", d=DH),
                                          bqkv_bc[:, 2, :].rearrange("p (h d) -> p h d", d=DH), ALU.add)
                job_read(m, name)

            def split_rest(name, which, n):
                dve.wait_ge(high_ready, 2 * n + which + 1)
                job_wait_read(dve, name)
                if n:
                    dve.wait_ge(mid_ready, 2 * (n - 1) + which + 1)
                link(dve.tensor_tensor(rest[:, which, :], qf[:, which, :], parts[:, n % 2, which, 0, :], ALU.subtract), rest_ready)

            def split_low(which, n):
                dve.wait_ge(mid_ready, 2 * n + which + 1)
                link(dve.tensor_tensor(parts[:, n % 2, which, 2, :], rest[:, which, :], parts[:, n % 2, which, 1, :], ALU.subtract),
                     split_ready)

            def split_both(names, n):
                split_rest(names[0], 0, n)
                split_rest(names[1], 1, n)
                split_low(0, n)
                split_low(1, n)

            job_wait_full(dve, "bcols")
            link_job(dve.tensor_copy(ecols[:], bank_of("bcols")[:, 0:2]), "bcols")
            job_wait_full(dve, "bbc")
            qk_bc = bqkv_bc[:, 0:2, :].rearrange("p a b -> p (a b)")
            link_job(dve.tensor_tensor(qk_bc, bank_of("bbc")[:, 0:2 * D], qk_bc, ALU.add), "bbc")
            evac_transposes("trS2_1", s2T[:, HT:2 * HT])
            evac_transposes("trX_1", xT[:, HT:2 * HT])
            split_both(("qT_0", "kT_0"), 0)
            dve.wait_ge(ld_len, 16)
            link(dve.tensor_copy(len_f[:], len_i[:]))
            dve.wait_ge(pool_pos, 1)
            link(dve.tensor_tensor(pos_row[:], pos_row[:], bc_last(len_f[:], T), ALU.is_ge))
            link(dve.tensor_scalar(mask_row[:], pos_row[:], MASKED, None, ALU.mult), mask_row_ready)

            split_both(("qT_1", "kT_1"), 1)

            def self_scores(half):
                bs = slice(half * HALF, half * HALF + HALF)
                link(dve.tensor_tensor(prod[:], tokA[:, bs, 0, :], tokA[:, bs, 1, :], ALU.mult))
                link(dve.tensor_reduce(s_self[:, bs, :], prod[:].rearrange("p b (h d) -> p b h d", d=DH), AX.X, ALU.add))

            for b in range(HALF):
                token_major(b)
            self_scores(0)
            v_prev(0)

            dve.wait_ge(ld_tau, 32)
            link(dve.scalar_tensor_tensor(tau2[:], tau[:], -1.0, tau[:], ALU.mult, ALU.max), tau_abs)
            link(dve.tensor_scalar(tau[:], tau[:], 0.0, None, ALU.max))

            def row_max(b, g):
                u = b * G + g
                dve.wait_ge(s1_full, u + 1)
                dve.tensor_reduce(mx[:, b, 4 * g:4 * g + 4], S1B[u % 2][:, :].rearrange("p (j t) -> p j t", j=4),
                                  AX.X, ALU.max).then_inc(s1_read, 1)

            def shift(b):
                dve.wait_ge(s1_read, G * (b + 1))
                link(dve.tensor_tensor(mx[:, b, :], mx[:, b, :], s_self[:, b, :], ALU.max))
                link(dve.tensor_scalar(negm[:, b, :], mx[:, b, :], -1.0, None, ALU.mult), negm_ready)
                dve.tensor_tensor(sshift[:, b, :], s_self[:, b, :], negm[:, b, :], ALU.add).then_inc(sshift_ready, 1)

            def normalise(b, step):
                name = f"pvtr_{b}"
                k = b % 2
                pvt = bank_of(name)[:, :].rearrange("p (h e) -> p h e", e=32)
                hd = lambda ap: ap.rearrange("p (h d) -> p h d", d=DH)
                if step == 0:
                    dve.wait_ge(wself_ready, b + 1)
                    dve.tensor_tensor(hd(wv[:, k, :]), hd(tokA[:, b, 2, :]), bc_last(w_self[:, b, :], DH), ALU.mult)\
                        .then_inc(norm_step, 1)
                    job_wait_full(dve, name)
                    dve.tensor_tensor(den[:, k, :], pvt[:, :, DH], w_self[:, b, :], ALU.add).then_inc(norm_step, 1)
                if step == 1:
                    dve.wait_ge(norm_step, 3 * b + 2)
                    dve.reciprocal(rden[:, k, :], den[:, k, :]).then_inc(norm_step, 1)
                    job_read(dve.tensor_tensor(hd(wv[:, k, :]), pvt[:, :, 0:DH], hd(wv[:, k, :]), ALU.add), name)
                if step == 2:
                    dve.wait_ge(norm_step, 3 * b + 3)
                    job_wait_read(dve, name)
                    dve.tensor_tensor(hd(attn[:, k, :]), hd(wv[:, k, :]), bc_last(rden[:, k, :], DH), ALU.mult)\
                        .then_inc(attn_ready, 1)

            by_c = blend[:].rearrange("p d c -> p c d")

            def weight_copies(i):
                if i == 0:
                    dve.wait_ge(tau_exp, 2)
                    link(dve.scalar_tensor_tensor(tau2[:], tau[:], -1.0, tau2[:], ALU.mult, ALU.subtract), tau_ready)
                    dve.wait_ge(ld_blend, 16)
                    link(dve.tensor_reduce(bl_small[:, 0, :], by_c, AX.X, ALU.max))
                    link(dve.tensor_tensor(blend[:], blend[:], bc_mid(bl_small[:, 0, :], ND), ALU.subtract), blend_sub)
                if i == 1:
                    job_wait_full(dve, "wB")
                    bank = bank_of("wB")
                    hd, dh = "p (h d) -> p h d", "p (d h) -> p h d"
                    kv = bank[:, 128:384].rearrange("p (h e) -> p h e", e=2 * DH)
                    link(dve.tensor_copy(wB[:, 0, :].rearrange(dh, d=DH), bank[:, 0:128].rearrange(hd, d=DH)))
                    link(dve.tensor_copy(wB[:, 1, :].rearrange(dh, d=DH), kv[:, :, 0:DH]))
                    link_job(dve.tensor_copy(wB[:, 2, :].rearrange(hd, d=DH), kv[:, :, DH:]), "wB")
                if i == 2:
                    job_wait_full(dve, "wO")
                    link_job(dve.tensor_copy(woT[:].rearrange("p g c -> p (g c)"), bank_of("wO")[:, :]), "wO")
                    dve.wait_ge(blend_exp, 1)
                    link(dve.tensor_reduce(bl_small[:, 0, :], by_c, AX.X, ALU.add))
                    link(dve.reciprocal(bl_small[:, 1, :], bl_small[:, 0, :]))
                    link(dve.tensor_tensor(blend[:], blend[:], bc_mid(bl_small[:, 1, :], ND), ALU.mult), blend_ready)
                if i == 3:
                    job_wait_full(dve, "wC1")
                    link_job(dve.tensor_copy(wC[:, 0:4, :].rearrange("p g c -> p (g c)"), bank_of("wC1")[:, :]), "wC1")
                if i == 4:
                    job_wait_full(dve, "wC2")
                    bank = bank_of("wC2")
                    link(dve.tensor_copy(wC[:, 4, :], bank[:, 0:128]))
                    link(dve.tensor_copy(wn1T[:], bank[:, 128:128 + NH1]))
                    link_job(dve.tensor_copy(wn2T[:], bank[0:NH1, 160:160 + ND]), "wC2")

            def window_v(half):
                name = f"bv_{half}"
                job_wait_full(dve, name)
                dve.wait_ge(pv_done, G * HALF * (half + 1))
                for i in range(HALF):
                    m = dve.tensor_copy(v_pad[:, half * HALF + i, :, 0:DH],
                                        bank_of(name)[:, i * D:(i + 1) * D].rearrange("p (h d) -> p h d", d=DH))
                job_read(m, name)

            for t in range(UNITS + LAG_OUT + 1):
                if t < UNITS:
                    row_max(t // G, t % G)
                    if t % G == G - 1:
                        shift(t // G)
                if t in (2, 3, 4, 5):
                    token_major(HALF + t - 2)
                if t == 6:
                    self_scores(1)
                    v_prev(1)
                if t % G == 3:
                    weight_copies(t // G)
                if t == PROJECT_AT + 1:
                    split_both(("bq_0", "bk_0"), 2)
                if t == PROJECT_AT + 5:
                    window_v(0)
                for step in range(3):
                    u = t - LAG_PVTR - step
                    if 0 <= u < UNITS and u % G == G - 1:
                        normalise(u // G, step)
            split_both(("bq_1", "bk_1"), 3)
            window_v(1)

            def statistics(src, b, n):
                dve.bn_stats(stats[:, b, :], src).then_inc(stats_ready, 1)
                dve.wait_ge(stats_ready, n + 1)
                dve.bn_aggr(mv[:, b, :], stats[:, b, :]).then_inc(mv_ready, 1)

            dve.wait_ge(ld_g1, 32)
            dve.wait_ge(xb_ready, 1)

            def norm_half(n, buf, half, gamma, into, addend, done):
                bs = slice(half * HALF, half * HALF + HALF)
                dve.wait_ge(rstd_ready, n + 1)
                for b in range(half * HALF, half * HALF + HALF):
                    m = dve.tensor_scalar(buf[:, b, :], buf[:, b, :], mv[:, b, 0:1], rstd[:, b:b + 1],
                                          ALU.subtract, ALU.mult)
                link(m)
                link(dve.tensor_tensor(buf[:, bs, :], buf[:, bs, :], bc_mid(gamma[:], HALF), ALU.mult))
                link(dve.tensor_tensor(into[:, bs, :], buf[:, bs, :], addend, ALU.add), done)

            for b in range(NB):
                name = f"y_{b}"
                job_wait_full(dve, name)
                link_job(dve.tensor_tensor(x1[:, b, :], bank_of(name)[:, 0:D], bo_bc[:], ALU.add), name)
                statistics(x1[:, b, :], b, b)
                if b == HALF - 1 or b == NB - 1:
                    half = half_of(b)
                    norm_half(half, x1, half, gamma1, x1, xb[:, half * HALF:half * HALF + HALF, :], x1_ready)

            def gate_sums(half):
                name = f"gate_{half}"
                bs = slice(half * HALF, half * HALF + HALF)
                job_wait_full(dve, name)
                job_read(dve.tensor_tensor(wgate[:, bs, :], bank_of(name)[:, :].rearrange("p (b c) -> p b c", b=HALF),
                                           bc_mid(bg_bc[:], HALF), ALU.add), name)
                name = f"mod_{half}"
                job_wait_full(dve, name)
                job_read(dve.tensor_tensor(mod[:, bs, :], bank_of(name)[:, 0:HALF * ND].rearrange("p (b c) -> p b c", b=HALF),
                                           bc_mid(bn2_bc[:], HALF), ALU.add), name)

            def gated_inputs(half):
                bs = slice(half * HALF, half * HALF + HALF)
                dve.wait_ge(gate_sig, half + 1)
                dve.tensor_tensor(wgate[:, bs, :], wgate[:, bs, :], x1[:, bs, :], ALU.mult).then_inc(gated_ready, 1)
                dve.wait_ge(mod_sig, half + 1)
                dve.tensor_scalar(mod[:, bs, :], mod[:, bs, :], 0.5, None, ALU.add).then_inc(mod_ready, 1)

            def blended(b):
                if b % HALF == 0:
                    dve.wait_ge(gated_ready, half_of(b) + 1)
                    dve.wait_ge(mod_ready, half_of(b) + 1)
                if b >= 2:
                    dve.wait_ge(G_used, b - 1)
                for d in range(ND - PD):
                    m = dve.scalar_tensor_tensor(Gb[:, b % 2, d, :], wgate[:, b, :], mod[:, b, d:d + 1],
                                                 blend[:, d, :], ALU.mult, ALU.mult)
                m.then_inc(Gd_ready, 1)

            def gated_soma(half):
                cs = slice(half * HT, half * HT + HT)
                job_wait_read(dve, f"tg_{half}")
                job_wait_read(dve, f"soma_{half}")
                dve.tensor_tensor(gateT[:, cs], gateT[:, cs], somaT[:, cs], ALU.mult).then_inc(sg_ready, 1)

            dve.wait_ge(ld_c, 16 * 9)
            gate_sums(0)
            gated_inputs(0)
            for b in range(NB):
                blended(b)
                if b == 1:
                    gate_sums(1)
                if b == 2:
                    gated_inputs(1)
                if b == HALF + 1:
                    gated_soma(0)

            def statistics_z(half):
                job_wait_read(dve, f"o_{half}")
                for b in range(half * HALF, half * HALF + HALF):
                    statistics(o_sb[:, b, :], b, NB + b)

            def norm_z(half):
                norm_half(2 + half, o_sb, half, gamma2, z, bc_mid(beta2[:], HALF), z_ready)

            statistics_z(0)
            gated_soma(1)
            norm_z(0)
            statistics_z(1)
            norm_z(1)

            for half in range(2):
                name = f"lg_{half}"
                bs = slice(half * HALF, half * HALF + HALF)
                job_wait_full(dve, name)
                link_job(dve.tensor_tensor(lg[:, bs, :], bank_of(name)[:, 0:HALF * NE].rearrange("p (b c) -> p b c", b=HALF),
                                           bc_mid(br_bc[:], HALF), ALU.add), name)
            dve.wait_ge(rank_consts, 1)
            link(dve.tensor_reduce(lgm[:], lg[:], AX.X, ALU.max))
            dve.tensor_tensor(gexp[:], lg[:], bc_last(lgm[:], NE), ALU.subtract).then_inc(lgm_sub, 1)
            link(dve.tensor_tensor(cand[:], lg[:], bc_last(lgm[:], NE), ALU.is_equal))
            link(dve.tensor_tensor(cand[:], cand[:], bc_mid(em8[:], NB), ALU.mult))
            link(dve.tensor_reduce(emin[:], cand[:], AX.X, ALU.min))
            onehot = onehotb[:, NB:]
            dve.tensor_tensor(onehot, cand[:], bc_last(emin[:], NE), ALU.is_equal).then_inc(onehot_ready, 1)
            dve.wait_ge(gexp_ready, 1)
            link(dve.tensor_reduce(gsum[:], gexp[:], AX.X, ALU.add))
            dve.reciprocal(rows[:, :, GATE], gsum[:]).then_inc(gate_ready, 1)
            job_wait_full(dve, "rank")
            bank = bank_of("rank")
            W = NB * NE
            link(dve.tensor_tensor(cmp[:], bc_last(bank[:, W:W + NE], NB), bc_mid(k128[:], NE), ALU.is_gt))
            link(dve.tensor_reduce(tiles_e[:], cmp[:], AX.X, ALU.add))
            link(dve.tensor_tensor(cmp[:], tri8[:], bc_mid(tiles_e[:], NE), ALU.mult))
            link(dve.tensor_reduce(excl[:], cmp[:], AX.X, ALU.add))
            link_job(dve.scalar_tensor_tensor(cand[:], bc_mid(excl[:], NB), 128.0,
                                              bank[:, 0:W].rearrange("p (b e) -> p b e", e=NE), ALU.mult, ALU.add), "rank")
            link(dve.tensor_tensor(cand[:], cand[:], onehot, ALU.mult))
            link(dve.tensor_reduce(slotf[:], cand[:], AX.X, ALU.add))
            dve.tensor_copy(slot[:], slotf[:]).then_inc(slot_ready, 1)
            link(dve.tensor_tensor(incl[:], excl[:], tiles_e[:], ALU.add))
            link(dve.tensor_tensor(tmap_c[:], bc_mid(incl[0:1, :], TILES), bc_last(tile_no[:], NE), ALU.is_le))
            link(dve.tensor_reduce(tmap_f[:], tmap_c[:], AX.X, ALU.add))
            dve.tensor_scalar(tmap[:], tmap_f[:], float(NE - 1), None, ALU.min).then_inc(tmap_ready, 1)

            for i in range(2, TILES + 3):
                if i < TILES + 2:
                    n = i - 2
                    dve.wait_ge(t_full, n + 1)
                    if n >= 2:
                        dve.wait_ge(y_full, n - 1)
                    dve.tensor_copy(hsT[:, n % 2, :], ps[2 + n % 2][:, :]).then_inc(t_read, 1)
                if i >= 3:
                    n = i - 3
                    dve.wait_ge(y_full, n + 1)
                    dve.scalar_tensor_tensor(ys[:, n, :], ps[6 + n % 2][:, 0:D], zs[:, n, GATE:GATE + 1],
                                             zs[:, n, D:2 * D], ALU.mult, ALU.add).then_inc(y_read, 1)


_OUTS = [((8, 128, 128), "float32")]


def kernel(**inputs):
    import numpy as _np
    import concourse.bacc as _bacc
    from concourse import mybir as _mybir
    from concourse.bass_utils import run_bass_kernel_spmd as _run

    nc = _bacc.Bacc("TRN2", target_bir_lowering=False, num_devices=1)
    arrays, args = {}, {}
    for name, a in inputs.items():
        a = _np.ascontiguousarray(a)
        if a.ndim == 0:
            a = a.reshape(1)
        arrays[f"in_{name}_dram"] = a
        args[name] = nc.dram_tensor(f"in_{name}_dram", a.shape, _mybir.dt.from_np(a.dtype), kind="ExternalInput").ap()
    shape, dtype = _OUTS[0]
    o = nc.dram_tensor("out_0_dram", shape, _mybir.dt.from_np(_np.dtype(dtype)), kind="ExternalOutput").ap()
    fused_layer(nc, args, o)
    r = _run(nc, [arrays], core_ids=[0])
    return r.results[0]["out_0_dram"]
```

```python
from contextlib import ExitStack

import concourse.bass as bass
from concourse import mybir

ALU = mybir.AluOpType
ACT = mybir.ActivationFunctionType
AX = mybir.AxisListType
F32 = mybir.dt.float32
BF16 = mybir.dt.bfloat16
I32 = mybir.dt.int32
U32 = mybir.dt.uint32


def fused_layer(nc, A, out):
    NB, T, D = A["x"].shape
    H = 16
    DH = D // H
    G = H // 4
    HALF = NB // 2
    HT = HALF * T
    NT = NB * T
    WINDOW = 16
    NE, _, FF = A["L0_ffn_W1"].shape
    FC = FF // 128
    ND = A["cond_1024"].shape[0]
    NH1 = A["cond_256"].shape[1]
    TILES = NT // 128 + NE - 1
    SCALE = float(DH) ** -0.5
    MASKED = -1.0e30
    EPS = 1e-5
    PRODUCTS = ((0, 1, 2, 0, 1, 0), (0, 0, 0, 1, 1, 2))
    NSLOT = len(PRODUCTS[0])
    NPROD = NSLOT * DH
    KROWS = 96
    R0 = KROWS - NPROD
    RMASK = R0 - 1

    ctx = ExitStack()
    with ctx:
        sb = lambda name, shape, dt=F32: ctx.enter_context(nc.sbuf_tensor("t_" + name, shape, dt))
        sem = lambda name: ctx.enter_context(nc.semaphore(name))
        dram = lambda name, shape, dt=F32: nc.dram_tensor(name, shape, dt).ap()

        ident = sb("ident", [128, 128])
        identb = sb("identb", [128, 128], BF16)
        bandb = sb("bandb", [128, 128], BF16)
        onesb = sb("onesb", [128, 128], BF16)
        ones_row = sb("ones_row", [1, NT], BF16)
        mask_row = sb("mask_row", [1, NB, T], BF16)
        pos_row = sb("pos_row", [1, NB, T])
        len_i = sb("len_i", [1, NB], I32)
        len_f = sb("len_f", [1, NB])
        wqkv = sb("wqkv", [128, 3, D])
        wo = sb("wo", [128, D])
        bqkv_bc = sb("bqkv_bc", [128, 3, D])
        bo_bc = sb("bo_bc", [128, D])
        cols = sb("cols", [128, 12])
        BQ, BK, BPREV, BSELF, BO, BSOMA, BTEMP, BN1 = range(8)
        ecols = sb("ecols", [128, 2])

        x_tok = sb("x_tok", [128, NB, D])
        ROW = 2 * D + 2
        GATE, TOKEN = 2 * D, 2 * D + 1
        rows = sb("rows", [128, NB, ROW])
        z, x1 = rows[:, :, 0:D], rows[:, :, D:2 * D]
        s2_tok = rows[:].rearrange("p b c -> p (b c)")[:, 0:NB * D].rearrange("p (b c) -> p b c", b=NB)
        xT = sb("xT", [128, NT])
        s2T = sb("s2T", [128, NT])
        qf = sb("qf", [128, 2, HT])
        parts = sb("parts", [128, 2, 2, 3, HT], BF16)
        rest = sb("rest", [128, 2, HT])
        Qs_all = sb("Qs", [128, 2, H, HT], BF16)
        Ks_all = sb("Ks", [128, 2, H, HT], BF16)
        Qs, Ks = Qs_all[0:KROWS], Ks_all[0:KROWS]
        w_dh = sb("w_dh", [128, 2, D])
        b_dh = sb("b_dh", [1, 2, D])
        tokA = sb("tokA", [128, NB, 3, D])
        v_pad = sb("v_pad", [128, NB, H, 32])
        prod = sb("prod", [128, HALF, D])
        s_self = sb("s_self", [128, NB, H])
        mx = sb("mx", [128, NB, H])
        negm = sb("negm", [128, NB, H], BF16)
        sshift = sb("sshift", [128, NB, H])
        w_self = sb("w_self", [128, NB, H])
        P = sb("P", [128, 3, 512])
        pv_sb = sb("pv_sb", [128, 2, 256])
        den = sb("den", [128, 2, H])
        rden = sb("rden", [128, 2, H])
        wv = sb("wv", [128, 2, D])
        attn = sb("attn", [128, 2, D])
        attnT = sb("attnT", [128, NT])

        w_raw = sb("w_raw", [128, 3, D])
        wo_raw = sb("wo_raw", [128, D])
        wB = sb("wB", [128, 3, D])
        woT = sb("woT", [128, D])
        y0T = sb("y0T", [128, NT])
        stats = sb("stats", [128, NB, 6])
        mv = sb("mv", [128, NB, 2])
        rstd = sb("rstd", [128, NB])
        zshift = sb("zshift", [128, NB])
        mhalf = sb("mhalf", [128, NB])
        gamma1 = sb("gamma1", [128, D])
        beta1 = sb("beta1", [128, D])
        wc_raw = sb("wc_raw", [128, 5, D])
        wn1_raw = sb("wn1_raw", [NH1, D])
        wn2_raw = sb("wn2_raw", [ND, NH1])
        wC = sb("wC", [128, 6, D])
        wn1T = sb("wn1T", [128, NH1])
        wn2T = sb("wn2T", [NH1, ND])
        bg_bc = sb("bg_bc", [128, D])
        bn2_bc = sb("bn2_bc", [128, ND])
        blend = sb("blend", [128, ND, D])
        bl_small = sb("bl_small", [128, D])
        tau = sb("tau", [128, ND + 1])
        tau2 = sb("tau2", [128, ND + 1])
        diff = sb("diff", [128, 128])
        ema = sb("ema", [128, ND + 1, 128])
        gamma2 = sb("gamma2", [128, D])
        beta2 = sb("beta2", [128, D])
        x1T = xT
        ctxT = s2T
        mod = sb("mod", [128, NB, ND])
        tempT = attnT
        somaT = y0T
        wr = sb("wr", [128, NE])
        wr_g = sb("wr_g", [128, NE])
        gb2 = sb("gb2", [128, 2])
        mean_mat = sb("mean_mat", [128, 128])
        b1_raw = sb("b1_raw", [NE * FC, 128])
        b1T = sb("b1T", [128, NE, FC])
        b1_tile = sb("b1_tile", [128, 2, FC])
        br_bc = sb("br_bc", [128, NE])
        b_parts = sb("b_parts", [NE, 3, D], BF16)
        lg = sb("lg", [128, NB, NE])
        lgm = sb("lgm", [128, NB])
        em8 = sb("em8", [128, NE])
        cand = sb("cand", [128, NB, NE])
        emin = sb("emin", [128, NB])
        onehotb = sb("onehotb", [128, 2 * NB, NE], BF16)
        gexp = sb("gexp", [128, NB, NE])
        gsum = sb("gsum", [128, NB])
        trib = sb("trib", [128, 128], BF16)
        k128 = sb("k128", [128, NB])
        cmp = sb("cmp", [128, NE, NB])
        tiles_e = sb("tiles_e", [128, NE])
        tri8 = sb("tri8", [128, NE, NE])
        incl = sb("incl", [128, NE])
        excl = sb("excl", [128, NE])
        slotf = sb("slotf", [128, NB])
        slot = sb("slot", [128, NB], U32)
        tile_no = sb("tile_no", [1, TILES])
        tmap_c = sb("tmap_c", [1, TILES, NE])
        tmap_f = sb("tmap_f", [1, TILES])
        tmap = sb("tmap", [1, TILES], I32)
        zsT = sb("zsT", [128, 2, 128])
        empty_row = sb("empty_row", [128, ROW])

        flat = lambda buf, pattern: buf[:].rearrange(pattern)
        q_room = flat(Qs_all, "p a h t -> p (a h t)").bitcast(F32)
        k_room = flat(Ks_all, "p a h t -> p (a h t)").bitcast(F32)
        v_room = flat(v_pad, "p b h e -> p (b h e)")
        t_room = flat(tokA, "p b a c -> p (b a c)")
        cut3 = lambda room, at, n, m: room[:, at:at + n * m].rearrange("p (n m) -> p n m", n=n)
        NG = 4
        Gb = q_room[:, 0:NG * ND * D].rearrange("p (k d c) -> p k d c", k=NG, d=ND)
        at = NG * ND * D
        gateT, h1T, oT = (q_room[:, at + i * NT:at + (i + 1) * NT] for i in range(3))
        h1T = h1T[0:NH1]
        at += 3 * NT
        o_raw = cut3(q_room, at, NB, D)
        zs = cut3(q_room, 0, TILES, ROW)
        W1 = cut3(k_room, 0, NE, FF)
        W2 = k_room[:, NE * FF:NE * (FF + FC * D)].rearrange("p (e k d) -> p e k d", e=NE, k=FC)
        wgate = cut3(v_room, 0, NB, D)
        hsT = cut3(v_room, NB * D, 2, FF)
        ys = cut3(v_room, NB * D + 2 * FF, TILES, D)
        b_rows = t_room.bitcast(BF16)[0:KROWS, 0:NE * D].rearrange("p (e f) -> p e f", e=NE)
        W1_tile = cut3(t_room, NE * D // 2, 2, FF)
        b_raw = flat(rows, "p b c -> p (b c)")[0:NE, 0:D]
        b_rest = flat(rows, "p b c -> p (b c)")[0:NE, D:2 * D]
        xb = x_tok

        b_dram = dram("b_dram", (3, NE, D), BF16)
        z_dram = dram("z_dram", (TILES * 128, ROW))

        ps = [ctx.enter_context(nc.psum_tensor(f"ps{i}", [128, 512], F32)) for i in range(8)]
        MAX_BANKS, SCORE_BANKS, VALUE_BANKS = ps[0:2], ps[2:4], ps[4:6]

        ZS_CUTS = (0, 2, 7, TILES)
        zs_part = lambda i: sum(i >= c for c in ZS_CUTS[1:])
        UNITS = G * NB
        PD = 2
        GROUPS = (range(0, HALF), range(HALF, NB - 1), range(NB - 1, NB))
        LAG_SCORES, LAG_VALUES = 5, 7
        LAG_PVTR, LAG_OUT = 9, 12
        EMA_AT = 3 * G
        TOK_AT, VP_AT = {HALF - 2 + i: HALF + i for i in range(HALF)}, 2 * HALF - 1
        Y0, QK, VW = 1, 2, 5
        HANDOFF = [half * HALF * G + HALF * G - 1 + LAG_OUT for half in range(2)]
        WINDOW_AT = UNITS + LAG_VALUES
        LAG_WVALUES, LAG_WOUT = 2, 5
        TURNS = WINDOW_AT + UNITS + LAG_WOUT
        FRONT_AT = WINDOW_AT + HALF * G - 1 + LAG_WOUT + 6
        HIDDEN_AT = WINDOW_AT + UNITS + 1
        def handoff(t, step):
            return [half for half in range(2) if t == HANDOFF[half] + step]

        order = [("trS2_0", 6), ("trX_0", 7), ("bcols", 0), ("bbc", 1), ("qT_0", 2), ("kT_0", 3), ("trS2_1", 4),
                 ("trX_1", 5), ("qT_1", 0), ("kT_1", 1)]
        order += [("tok_0", 6), ("tok_1", 7), ("tok_2", 4), ("tok_3", 5), ("vp_0", 2)]
        alternating = []
        for t in range(TURNS):
            if t in TOK_AT:
                alternating += [f"tok_{TOK_AT[t]}"]
            if t == VP_AT:
                alternating += ["vp_1"]
            if t % G == 2:
                alternating += {1: ["wB"], 2: ["wO"], 3: ["wC1"], 4: ["wC2"], 6: ["wR"]}.get(t // G, [])
            alternating += [f"{name}_{half}" for half in handoff(t, QK) for name in ("bq", "bk")]
            alternating += [f"bv_{half}" for half in handoff(t, VW)]
            for lag, name in ((LAG_PVTR, "pvtr"), (LAG_OUT, "attnT")):
                u = t - lag
                if 0 <= u < UNITS and u % G == G - 1:
                    alternating += [f"{name}_{u // G}"]
            alternating += [f"y0T_{half}" for half in handoff(t, Y0)]
            u = t - WINDOW_AT - LAG_WOUT
            if 0 <= u < UNITS and u % G == G - 1:
                alternating += [f"y_{u // G}"]
            alternating += {FRONT_AT: ["x1T_0"], FRONT_AT + 1: ["ctxT_0"], FRONT_AT + 2: ["gate_0"],
                            HIDDEN_AT: ["h1_0"]}.get(t, [])
        alternating += ["mod_0", "x1T_1", "ctxT_1", "h1_1", "mod_1", "gate_1",
                        "tg_0", "o_0", "tg_1", "o_1", "tg_2", "oT_0", "o_2", "oT_1", "lg_0", "lg_1", "rank"]
        order += [(name, 6 + n % 2) for n, name in enumerate(alternating)]
        order += [("soma_0", 4), ("soma_1", 5)]
        job = {}
        served = [0] * 8
        for name, bank in order:
            job[name] = (bank, served[bank])
            served[bank] += 1
        bank_full = [sem(f"bank_full{i}") for i in range(8)]
        bank_read = [sem(f"bank_read{i}") for i in range(8)]
        bank_of = lambda name: ps[job[name][0]]

        def job_wait_free(eng, name):
            bank, n = job[name]
            if n:
                eng.wait_ge(bank_read[bank], n)

        def job_full(ins, name):
            ins.then_inc(bank_full[job[name][0]], 1)

        def job_wait_full(eng, name):
            eng.wait_ge(bank_full[job[name][0]], job[name][1] + 1)

        def job_read(ins, name):
            ins.then_inc(bank_read[job[name][0]], 1)

        def job_wait_read(eng, name):
            eng.wait_ge(bank_read[job[name][0]], job[name][1] + 1)

        ld_wv = sem("ld_wv")
        ld_s2, ld_x, ld_wa, ld_cols, ld_len = sem("ld_s2"), sem("ld_x"), sem("ld_wa"), sem("ld_cols"), sem("ld_len")
        consts_ready = sem("consts_ready")
        vpad_zero = sem("vpad_zero")
        row_ready = sem("row_ready")
        split_ready = sem("split_ready")
        high_ready = sem("high_ready")
        stack_in = [sem(f"stack_in{i}") for i in range(2)]
        rows_in = [sem("rows_in0"), sem("rows_in1")]
        max_scores_full, max_scores_read = sem("max_scores_full"), sem("max_scores_read")
        scores_full, scores_read = sem("scores_full"), sem("scores_read")
        pv_read = sem("pv_read")
        pv_done = sem("pv_done")
        negm_ready = sem("negm_ready")
        wself_ready = sem("wself_ready")
        sshift_ready = sem("sshift_ready")
        attn_ready = sem("attn_ready")
        tok_biased, prod_ready, self_ready = sem("tok_biased"), sem("prod_ready"), sem("self_ready")
        norm_step = sem("norm_step")
        dve_step = sem("dve_step")
        pool_step = sem("pool_step")
        stack_zero = sem("stack_zero")
        wdh_ready = sem("wdh_ready")
        pool_pos = sem("pool_pos")
        rest_ready = sem("rest_ready")
        mid_ready = sem("mid_ready")
        mask_row_ready = sem("mask_row_ready")

        ld_wb, ld_wcr, ld_c, ld_f, ld_brow = sem("ld_wb"), sem("ld_wcr"), sem("ld_c"), sem("ld_f"), sem("ld_brow")
        ld_tau, ld_braw, ld_g1, ld_blend = sem("ld_tau"), sem("ld_braw"), sem("ld_g1"), sem("ld_blend")
        window_scores_full, window_scores_read = sem("window_scores_full"), sem("window_scores_read")
        vpad_clear = sem("vpad_clear")
        shift_ready, z_scaled = sem("shift_ready"), sem("z_scaled")
        stats_ready = sem("stats_ready")
        mv_ready, rstd_ready = sem("mv_ready"), sem("rstd_ready")
        x1_ready, xb_ready = sem("x1_ready"), sem("xb_ready")
        band_ready = sem("band_ready")
        ema_ready, tau_ready, diff_ready, ema_exp = sem("ema_ready"), sem("tau_ready"), sem("diff_ready"), sem("ema_exp")
        tau_abs, tau_exp = sem("tau_abs"), sem("tau_exp")
        wrg_ready, mean_ready = sem("wrg_ready"), sem("mean_ready")
        blend_max, blend_sum, blend_inv = sem("blend_max"), sem("blend_sum"), sem("blend_inv")
        blend_sub, blend_exp, blend_ready = sem("blend_sub"), sem("blend_exp"), sem("blend_ready")
        gate_sig, gated_ready = sem("gate_sig"), sem("gated_ready")
        mod_sig, mod_ready = sem("mod_sig"), sem("mod_ready")
        blend_vector, blend_pool, blend_used, traces_read = sem("blend_vector"), sem("blend_pool"), sem("blend_used"), sem("traces_read")
        gated_soma_ready, z_ready = sem("gated_soma_ready"), sem("z_ready")
        lgm_sub, gexp_ready, onehot_ready, slot_ready, tmap_ready = sem("lgm_sub"), sem("gexp_ready"), sem("onehot_ready"), sem("slot_ready"), sem("tmap_ready")
        b_split, b_out = sem("b_split"), sem("b_out")
        z_zeroed, z_out = sem("z_zeroed"), sem("z_out")
        zs_in = [sem(f"zs_in{i}") for i in range(3)]
        brow_zero, tile_zero = sem("brow_zero"), sem("tile_zero")
        zT_full, zT_read = sem("zT_full"), sem("zT_read")
        h_full, h_read = sem("h_full"), sem("h_read")
        w1_ready = sem("w1_ready")
        y_full, y_read = sem("y_full"), sem("y_read")
        y_out, gate_ready, token_no = sem("y_out"), sem("gate_ready"), sem("token_no")
        rank_consts = sem("rank_consts")

        half_of = lambda b: b // HALF
        tokens_of = lambda batches: slice(batches[0] * T, (batches[-1] + 1) * T)
        pair_head = lambda g, j: 8 * (g // 2) + 2 * j + g % 2
        quad_head = lambda g, j: 4 * j + g
        bc_mid = lambda ap, n: ap.unsqueeze(1).broadcast_to([ap.shape[0], n, ap.shape[1]])
        bc_last = lambda ap, n: ap.unsqueeze(2).broadcast_to([ap.shape[0], ap.shape[1], n])

        block = ctx.enter_context(nc.Block())

        @block.sync
        def _(sp):
            col = lambda a: a.rearrange("(p o) -> p o", o=1)
            sp.dma_start(s2_tok[:], A["fside_BxSxS_0"].rearrange("b s c -> s b c")).then_inc(ld_s2, 16)
            sp.dma_start(x_tok[:], A["x"].rearrange("b s c -> s b c")).then_inc(ld_x, 16)
            for i, n in enumerate(("q", "k")):
                sp.dma_start(wqkv[:, i, :], A[f"L0_cond_W{n}"]).then_inc(ld_wa, 16)
                sp.dma_start(bqkv_bc[:, i, :], A[f"L0_cond_b{n}"].partition_broadcast(128)).then_inc(ld_wa, 16)
            sp.dma_start(cols[:, BPREV:BPREV + 1], A["L0_cond_b_prev"].rearrange("a b c -> c (a b)")).then_inc(ld_cols, 16)
            sp.dma_start(cols[:, BSELF:BSELF + 1], A["L0_cond_b_self"].rearrange("a b c -> c (a b)")).then_inc(ld_cols, 16)
            sp.dma_start(len_i[:], A["itok_B_18_1004"].rearrange("(o b) -> o b", o=1)).then_inc(ld_len, 16)
            sp.dma_start(wqkv[:, 2, :], A["L0_cond_Wv"]).then_inc(ld_wv, 16)
            sp.dma_start(bqkv_bc[:, 2, :], A["L0_cond_bv"].partition_broadcast(128)).then_inc(ld_wv, 16)
            sp.dma_start(wo[:], A["L0_cond_Wo"]).then_inc(ld_wb, 16)
            sp.dma_start(w_raw[:, 0, :], A["L0_attn_wq"]).then_inc(ld_wb, 16)
            sp.dma_start(w_raw[:, 1:3, :], A["L0_attn_wkv"].rearrange("(a p) c -> p a c", a=2)).then_inc(ld_wb, 16)
            sp.dma_start(wo_raw[:], A["L0_attn_wo"]).then_inc(ld_wb, 16)
            sp.dma_start(bo_bc[:], A["L0_cond_bo"].partition_broadcast(128)).then_inc(ld_wb, 16)
            sp.dma_start(cols[:, BO:BO + 1], col(A["L0_cond_bo"])).then_inc(ld_wb, 16)
            sp.dma_start(tau[:, 0:1], A["L0_cond2_tau_ctx"].partition_broadcast(128)).then_inc(ld_tau, 16)
            sp.dma_start(tau[:, 1:], A["condB_tauraws"].partition_broadcast(128)).then_inc(ld_tau, 16)
            sp.dma_start(blend[:], A["cond_1024"].partition_broadcast(128)).then_inc(ld_blend, 16)
            def constant_rows(half):
                row = mask_row[:, half * HALF:half * HALF + HALF, :].rearrange("o b t -> o (b t)")
                sp.dma_start(Ks[RMASK:R0, half], bc_mid(row, H)).then_inc(rows_in[half], 16)
                sp.dma_start(Qs[RMASK:R0, half], bc_mid(ones_row[:, 0:HT], H)).then_inc(rows_in[half], 16)

            def stack_up(att, half):
                n = 2 * att + half
                for part in range(3):
                    for which, stack in enumerate((Qs, Ks)):
                        sp.wait_ge((high_ready, mid_ready, split_ready)[part], 2 * n + which + 1)
                        for slot in range(NSLOT):
                            if PRODUCTS[which][slot] == part:
                                r0 = R0 + slot * DH
                                sp.dma_start(stack[r0:r0 + DH, half], parts[:, half, which, part, :])\
                                    .then_inc(stack_in[half], 16)

            sp.wait_ge(stack_zero, 2)
            sp.wait_ge(row_ready, 1)
            sp.wait_ge(mask_row_ready, 1)
            constant_rows(0)
            stack_up(0, 0)
            sp.wait_ge(stack_zero, 4)
            constant_rows(1)
            stack_up(0, 1)
            job_wait_read(sp, "trS2_1")
            sp.dma_start(b_raw, A["L0_ffn_b2"]).then_inc(ld_braw, 16)
            sp.dma_start(gamma1[:], A["L0_attn_gamma"].partition_broadcast(128)).then_inc(ld_g1, 16)
            sp.dma_start(beta1[:], A["L0_attn_beta"].partition_broadcast(128)).then_inc(ld_g1, 16)
            sp.dma_start(wc_raw[:, 0:2, :], A["L0_cond2_Wg"].rearrange("e (a c) -> e a c", a=2)).then_inc(ld_wcr, 16)
            for i, n in enumerate(("Wsoma", "Wtemp", "Wout")):
                sp.dma_start(wc_raw[:, 2 + i, :], A[f"L0_cond2_{n}"]).then_inc(ld_wcr, 16)
            sp.dma_start(wn1_raw[:], A["L0_cond2_Wn1"]).then_inc(ld_wcr, 16)
            sp.dma_start(wn2_raw[:], A["cond_256"]).then_inc(ld_wcr, 16)
            sp.dma_start(b1_raw[:], A["L0_ffn_b1"].rearrange("e (c p) -> (e c) p", p=128)).then_inc(ld_wcr, 16)
            for dst, n in ((bg_bc, "L0_cond2_bg"), (bn2_bc, "condB_bn2"), (gamma2, "L0_cond2_gamma"),
                           (beta2, "L0_cond2_beta"), (br_bc, "L0_ffn_br")):
                sp.dma_start(dst[:], A[n].partition_broadcast(128)).then_inc(ld_c, 16)
            sp.dma_start(cols[:, BSOMA:BSOMA + 1], col(A["L0_cond2_bsoma"])).then_inc(ld_c, 16)
            sp.dma_start(cols[:, BTEMP:BTEMP + 1], col(A["L0_cond2_btemp"])).then_inc(ld_c, 16)
            sp.dma_start(cols[0:NH1, BN1:BN1 + 1], col(A["L0_cond2_bn1"])).then_inc(ld_c, 16)
            sp.dma_start(wr[:], A["L0_ffn_Wr"]).then_inc(ld_c, 16)
            sp.dma_start(gb2[:, 0:1], col(A["L0_cond2_gamma"])).then_inc(ld_c, 16)
            sp.dma_start(gb2[:, 1:2], col(A["L0_cond2_beta"])).then_inc(ld_c, 16)
            sp.wait_ge(tile_zero, 1)
            sp.dma_start(z_dram.rearrange("(i p) c -> p i c", p=128), bc_mid(empty_row[:], TILES)).then_inc(z_zeroed, 16)
            sp.wait_ge(b_split, 3)
            sp.dma_start(b_dram.rearrange("q e f -> e q f"), b_parts[:]).then_inc(b_out, 16)
            for half in range(2):
                sp.wait_ge(scores_full, G * HALF * (half + 1))
                sp.dma_start(Qs[RMASK:R0, half], bc_mid(ones_row[:, HT:2 * HT], H)).then_inc(stack_in[half], 16)
                stack_up(1, half)
            sp.wait_ge(b_out, 16)
            sp.wait_ge(brow_zero, 1)
            sp.dma_start(b_rows[0:3], b_dram).then_inc(ld_brow, 16)
            sp.wait_ge(window_scores_full, G * NB)
            sp.dma_start(W1[:], A["L0_ffn_W1"].rearrange("e d f -> d e f")).then_inc(ld_f, 16)
            sp.dma_start(W2[:], A["L0_ffn_W2"].rearrange("e (k p) d -> p e k d", p=128)).then_inc(ld_f, 16)
            sp.wait_ge(z_out, 16 * NB)
            for k in range(3):
                a, z_ = ZS_CUTS[k], ZS_CUTS[k + 1]
                sp.dma_start(zs[:, a:z_, :], z_dram[a * 128:z_ * 128].rearrange("(i p) c -> p i c", p=128))\
                    .then_inc(zs_in[k], 16)

        @block.gpsimd
        def _(pool):
            steps = [0]

            def link(ins):
                steps[0] += 1
                ins.then_inc(pool_step, 1)
                pool.wait_ge(pool_step, steps[0])

            link(pool.memset(ident[:], 1.0))
            zero_rows = lambda stack, half: pool.memset(stack[0:64, half].bitcast(F32), 0.0).then_inc(stack_zero, 1)
            pool.affine_select(ident[:], ident[:], pattern=[[1, 128]], compare_op=ALU.is_equal, fill=0.0,
                               base=0, channel_multiplier=-1).then_inc(consts_ready, 1)
            link(pool.memset(ones_row[:, HT:2 * HT], 0.0))
            pool.memset(ones_row[:, 0:HT], 1.0).then_inc(row_ready, 1)
            pool.iota(pos_row[:], pattern=[[0, NB], [1, T]], base=0, channel_multiplier=0,
                      allow_small_or_imprecise_dtypes=True).then_inc(pool_pos, 1)
            pool.wait_ge(consts_ready, 1)
            pool.tensor_copy(identb[:], ident[:]).then_inc(consts_ready, 1)
            zero_rows(Qs, 0)
            zero_rows(Ks, 0)
            def zero_values(half):
                bs = slice(half * HALF, half * HALF + HALF)
                link(pool.memset(v_pad[:, bs], 0.0))
                link(pool.memset(v_pad[:, bs, 0:H:2, DH:DH + 1], 1.0))
                pool.memset(v_pad[:, bs, 1:H:2, 16 + DH:17 + DH], 1.0).then_inc(vpad_zero, 1)

            zero_values(0)
            zero_rows(Qs, 1)
            zero_rows(Ks, 1)
            zero_values(1)

            def add_token_bias(half):
                bs = slice(half * HALF, half * HALF + HALF)
                if half == 0:
                    pool.wait_ge(ld_wv, 32)
                    job_wait_read(pool, "bbc")
                for b in range(half * HALF, half * HALF + HALF):
                    job_wait_read(pool, f"tok_{b}")
                    m = pool.tensor_tensor(tokA[:, b, 0:2], tokA[:, b, 0:2], bqkv_bc[:, 0:2], ALU.add)
                link(m)
                if half == 1:
                    pool.wait_ge(self_ready, 1)
                pool.tensor_tensor(prod[:], tokA[:, bs, 0, :], tokA[:, bs, 1, :], ALU.mult).then_inc(prod_ready, 1)
                pool.tensor_tensor(tokA[:, bs, 2], tokA[:, bs, 2], bc_mid(bqkv_bc[:, 2], HALF), ALU.add)\
                    .then_inc(tok_biased, 1)

            add_token_bias(0)
            link(pool.iota(diff[:], pattern=[[1, 128]], base=0, channel_multiplier=-1,
                           allow_small_or_imprecise_dtypes=True))
            pool.tensor_scalar(diff[:], diff[:], 0.0, None, ALU.max).then_inc(diff_ready, 1)
            pool.memset(mean_mat[:], 1.0 / D).then_inc(mean_ready, 1)
            link(pool.memset(empty_row[:], 0.0))
            pool.iota(empty_row[:, TOKEN:TOKEN + 1].bitcast(I32), pattern=[[0, 1]], base=NT, channel_multiplier=1)\
                .then_inc(tile_zero, 1)
            link(pool.memset(bandb[:], 0.0))
            link(pool.affine_select(bandb[:], bandb[:], pattern=[[1, 128]], compare_op=ALU.is_ge,
                                    fill=MASKED, base=-1, channel_multiplier=-1))
            pool.affine_select(bandb[:], bandb[:], pattern=[[-1, 128]], compare_op=ALU.is_ge,
                               fill=MASKED, base=WINDOW, channel_multiplier=1).then_inc(band_ready, 1)
            add_token_bias(1)
            pool.wait_ge(blend_max, 1)
            pool.tensor_tensor(blend[:], blend[:], bc_mid(bl_small[:], ND), ALU.subtract).then_inc(blend_sub, 1)
            pool.wait_ge(blend_exp, 1)
            link(pool.tensor_tensor(bl_small[:], blend[:, 0, :], blend[:, 1, :], ALU.add))
            for d in range(2, ND - 1):
                link(pool.tensor_tensor(bl_small[:], bl_small[:], blend[:, d, :], ALU.add))
            pool.tensor_tensor(bl_small[:], bl_small[:], blend[:, ND - 1, :], ALU.add).then_inc(blend_sum, 1)
            pool.wait_ge(blend_inv, 1)
            pool.tensor_tensor(blend[:], blend[:], bc_mid(bl_small[:], ND), ALU.mult).then_inc(blend_ready, 1)
            pool.wait_ge(ld_braw, 16)
            pool.tensor_copy(b_parts[:, 0, :], b_raw[:]).then_inc(b_split, 1)
            pool.wait_ge(b_split, 1)
            link(pool.tensor_tensor(b_rest[:], b_raw[:], b_parts[:, 0, :], ALU.subtract))
            pool.tensor_copy(b_parts[:, 1, :], b_rest[:]).then_inc(b_split, 1)
            pool.wait_ge(b_split, 2)
            pool.tensor_tensor(b_parts[:, 2, :], b_rest[:], b_parts[:, 1, :], ALU.subtract).then_inc(b_split, 1)
            pool.wait_ge(ema_exp, 1)
            pool.affine_select(ema[:], ema[:], pattern=[[0, ND + 1], [1, 128]], compare_op=ALU.is_ge,
                               fill=0.0, base=0, channel_multiplier=-1).then_inc(ema_ready, 1)
            pool.wait_ge(ld_g1, 32)
            job_wait_full(pool, "trX_1")
            pool.tensor_tensor(xb[:], x_tok[:], bc_mid(beta1[:], NB), ALU.add).then_inc(xb_ready, 1)
            link(pool.memset(onehotb[:, 0:NB], 0.0))
            link(pool.memset(onesb[:], 1.0))
            link(pool.affine_select(trib[:], onesb[:], pattern=[[1, 128]], compare_op=ALU.is_gt, fill=0.0,
                                    base=0, channel_multiplier=-1))
            link(pool.iota(em8[:], pattern=[[1, NE]], base=-NE, channel_multiplier=0,
                           allow_small_or_imprecise_dtypes=True))
            link(pool.iota(k128[:], pattern=[[128, NB]], base=0, channel_multiplier=0,
                           allow_small_or_imprecise_dtypes=True))
            link(pool.iota(tile_no[:], pattern=[[1, TILES]], base=0, channel_multiplier=0,
                           allow_small_or_imprecise_dtypes=True))
            link(pool.memset(tri8[:], 1.0))
            pool.affine_select(tri8[:], tri8[:], pattern=[[1, NE], [-1, NE]], compare_op=ALU.is_gt, fill=0.0,
                               base=0, channel_multiplier=0).then_inc(rank_consts, 1)
            link(pool.memset(mhalf[:], -0.5))
            pool.wait_ge(b_split, 3)
            job_wait_full(pool, "trS2_1")
            pool.iota(rows[:, :, TOKEN:TOKEN + 1].bitcast(I32), pattern=[[T, NB], [0, 1]], base=0, channel_multiplier=1)\
                .then_inc(token_no, 1)
            def clear_values(half):
                pool.wait_ge(pv_done, G * HALF * (half + 1))
                pool.memset(v_pad[:, half * HALF:half * HALF + HALF], 0.0).then_inc(vpad_clear, 1)

            clear_values(0)
            clear_values(1)
            pool.wait_ge(attn_ready, NB)
            pool.memset(b_rows[:], 0.0).then_inc(brow_zero, 1)

            def inverse_std(norm, batches):
                pool.wait_ge(mv_ready, norm * NB + batches[-1] + 1)
                bs = slice(batches[0], batches[-1] + 1)
                link(pool.tensor_scalar(rstd[:, bs], mv[:, bs, 1], EPS, None, ALU.add))
                pool.tensor_tensor(rstd[:, bs], rstd[:, bs], mhalf[:, bs], ALU.pow).then_inc(rstd_ready, 1)

            inverse_std(0, range(0, HALF))
            inverse_std(0, range(HALF, NB))

            for b in range(NB):
                k = b % NG
                pool.wait_ge(gated_ready, half_of(b) + 1)
                pool.wait_ge(mod_ready, half_of(b) + 1)
                if b >= NG:
                    pool.wait_ge(blend_used, b - NG + 1)
                ds = slice(ND - PD, ND)
                link(pool.tensor_tensor(Gb[:, k, ds, :], bc_mid(wgate[:, b, :], PD), blend[:, ds, :], ALU.mult))
                pool.tensor_tensor(Gb[:, k, ds, :], Gb[:, k, ds, :], bc_last(mod[:, b, ds], D), ALU.mult)\
                    .then_inc(blend_pool, 1)

            def norm_z(half):
                bs = slice(half * HALF, half * HALF + HALF)
                pool.wait_ge(z_scaled, half + 1)
                link(pool.tensor_tensor(z[:, bs, :], z[:, bs, :], bc_mid(gamma2[:], HALF), ALU.mult))
                pool.tensor_tensor(z[:, bs, :], z[:, bs, :], bc_mid(beta2[:], HALF), ALU.add).then_inc(z_ready, 1)

            inverse_std(1, GROUPS[0])
            job_wait_read(pool, "tg_2")
            job_wait_read(pool, "soma_1")
            cs = tokens_of(GROUPS[2])
            pool.tensor_tensor(gateT[:, cs], gateT[:, cs], somaT[:, cs], ALU.mult).then_inc(gated_soma_ready, 1)
            inverse_std(1, GROUPS[1])
            inverse_std(1, GROUPS[2])
            norm_z(0)
            norm_z(1)

            pool.wait_ge(slot_ready, 1)
            pool.wait_ge(gate_ready, 1)
            pool.wait_ge(z_ready, 2)
            pool.wait_ge(token_no, 1)
            pool.wait_ge(z_zeroed, 16)
            for b in range(NB):
                pool.indirect_dma_start(out=z_dram, out_offset=bass.IndirectOffsetOnAxis(slot[:, b:b + 1], 0),
                                        in_=rows[:, b, :], in_offset=None).then_inc(z_out, 16)
            for i in range(TILES):
                pool.wait_ge(y_read, i + 1)
                pool.indirect_dma_start(
                    out=out.rearrange("b s c -> (b s) c"),
                    out_offset=bass.IndirectOffsetOnAxis(zs[:, i, TOKEN:TOKEN + 1].bitcast(U32), 0),
                    in_=ys[:, i, :], in_offset=None, bounds_check=NT - 1, oob_is_err=False).then_inc(y_out, 16)
            pool.wait_ge(y_out, 16 * TILES)

        @block.tensor
        def _(pe):
            def transposes(name, src, count, wait=None):
                job_wait_free(pe, name)
                for i in range(count):
                    m = pe.transpose(bank_of(name)[:, i * 128:(i + 1) * 128], src(i), ident[:])
                job_full(m, name)

            def dense(name, lhsT, rhs, cols_, start=True):
                job_wait_free(pe, name)
                m = pe.matmul(bank_of(name)[:, 0:cols_], lhsT, rhs, start=True, stop=True)
                job_full(m, name)

            def transpose_inputs(half):
                if half == 0:
                    pe.wait_ge(consts_ready, 1)
                    pe.wait_ge(ld_s2, 16)
                transposes(f"trS2_{half}", lambda i: s2_tok[:, half * HALF + i, :], 4)
                if half == 0:
                    pe.wait_ge(ld_x, 16)
                transposes(f"trX_{half}", lambda i: x_tok[:, half * HALF + i, :], 4)

            def project_q(half):
                cs = slice(half * HT, half * HT + HT)
                job_wait_read(pe, f"trS2_{half}")
                dense(f"qT_{half}", w_dh[:, 0, :], s2T[:, cs], HT)

            def project_k(half):
                cs = slice(half * HT, half * HT + HT)
                job_wait_read(pe, f"trX_{half}")
                dense(f"kT_{half}", w_dh[:, 1, :], xT[:, cs], HT)

            def project_tok(b):
                dense(f"tok_{b}", s2T[:, b * T:(b + 1) * T], wqkv[:].rearrange("p a b -> p (a b)"), 3 * D)

            def four_batches(name, half, src, rhs):
                job_wait_free(pe, name)
                for i in range(HALF):
                    b = half * HALF + i
                    m = pe.matmul(bank_of(name)[:, i * D:(i + 1) * D], src[:, b * T:(b + 1) * T], rhs, start=True, stop=True)
                job_full(m, name)

            def router_job():
                pe.wait_ge(wrg_ready, 1)
                pe.wait_ge(mean_ready, 1)
                job_wait_free(pe, "wR")
                bank = bank_of("wR")
                pe.matmul(bank[:, 0:NE], mean_mat[:], wr_g[:], start=True, stop=True)
                m = pe.matmul(bank[:, NE:2 * NE], gb2[:, 1:2].broadcast_to([128, 128]), wr[:], start=True, stop=True)
                job_full(m, "wR")

            def stacked(stack, b, h):
                return stack[:, half_of(b), h, (b % HALF) * T:(b % HALF + 1) * T]

            def scores_max(b, g):
                u = b * G + g
                if u == 0:
                    job_wait_read(pe, "qT_1")
                    job_wait_read(pe, "kT_1")
                if b % HALF == 0 and g == 0:
                    pe.wait_ge(rows_in[half_of(b)], 32)
                    pe.wait_ge(stack_in[half_of(b)], 16 * 2 * NSLOT)
                if u >= 2:
                    pe.wait_ge(max_scores_read, u - 1)
                for j in range(4):
                    h = 4 * g + j
                    m = pe.matmul(MAX_BANKS[u % 2][:, j * T:(j + 1) * T], stacked(Qs, b, h), stacked(Ks, b, h),
                                  start=True, stop=True)
                m.then_inc(max_scores_full, 1)

            def scores(b, g):
                u = b * G + g
                pe.wait_ge(negm_ready, b + 1)
                if u == 0:
                    job_wait_read(pe, "vp_0")
                    job_wait_read(pe, "kT_0")
                    job_wait_read(pe, "trX_1")
                if u >= 2:
                    pe.wait_ge(scores_read, u - 1)
                for j in range(4):
                    h = pair_head(g, j)
                    o = SCORE_BANKS[u % 2][:, j * T:(j + 1) * T]
                    pe.matmul(o, stacked(Ks, b, h), stacked(Qs, b, h), start=True, stop=False)
                    m = pe.matmul(o, negm[:, b, h:h + 1].broadcast_to([128, 128]), identb[:], start=False, stop=True)
                m.then_inc(scores_full, 1)

            def values(b, g):
                u = b * G + g
                pe.wait_ge(scores_read, u + 1)
                if u == 0:
                    job_wait_read(pe, "tok_2")
                    job_wait_read(pe, "tok_3")
                if g == 0:
                    job_wait_read(pe, f"vp_{half_of(b)}")
                    if b >= 2:
                        pe.wait_ge(pv_read, b - 1)
                for j in range(4):
                    m = pe.matmul(VALUE_BANKS[b % 2][32 * j:32 * j + 32, g // 2 * T:(g // 2 + 1) * T],
                                  v_pad[:, b, pair_head(g, j), :], P[:, u % 3, j * T:(j + 1) * T],
                                  start=(g % 2 == 0), stop=(g % 2 == 1))
                m.then_inc(pv_done, 1)

            def wide(name, lhsT, rhs):
                dense(name, lhsT, rhs, HT)

            def project_window_y(half):
                job_wait_read(pe, f"attnT_{half * HALF + HALF - 1}")
                wide(f"y0T_{half}", wo[:], attnT[:, half * HT:half * HT + HT])

            def project_window_qk(half):
                job_wait_read(pe, "wB")
                job_wait_read(pe, f"y0T_{half}")
                wide(f"bq_{half}", wB[:, 0, :], y0T[:, half * HT:half * HT + HT])
                wide(f"bk_{half}", wB[:, 1, :], y0T[:, half * HT:half * HT + HT])

            def project_window_v(half):
                four_batches(f"bv_{half}", half, y0T, wB[:, 2, :])

            def weight_job(i):
                if i == 1:
                    pe.wait_ge(ld_wb, 16 * 6)
                    transposes("wB", lambda k: w_raw[:, k, :], 3)
                if i == 2:
                    transposes("wO", lambda k: wo_raw[:], 1)
                if i == 3:
                    pe.wait_ge(ld_wcr, 16 * 7)
                    transposes("wC1", lambda k: wc_raw[:, k, :], 4)
                if i == 6:
                    router_job()
                if i == 4:
                    job_wait_free(pe, "wC2")
                    bank = bank_of("wC2")
                    pe.transpose(bank[:, 0:128], wc_raw[:, 4, :], ident[:])
                    pe.transpose(bank[:, 128:128 + NH1], wn1_raw[:], ident[0:NH1, 0:NH1])
                    pe.transpose(bank[0:NH1, 160:160 + ND], wn2_raw[:], ident[0:ND, 0:ND])
                    job_full(pe.transpose(bank[:, 256:256 + NE * FC], b1_raw[:], ident[0:NE * FC, 0:NE * FC]), "wC2")

            transpose_inputs(0)
            pe.wait_ge(wdh_ready, 4)
            project_q(0)
            pe.wait_ge(ld_wa, 16 * 4)
            pe.wait_ge(ld_cols, 16 * 2)
            job_wait_free(pe, "bcols")
            for i, added in enumerate((BSELF, BPREV)):
                o = bank_of("bcols")[:, i:i + 1]
                pe.matmul(o, w_dh[:, i, :], cols[:, added:added + 1], start=True, stop=False)
                m = pe.matmul(o, b_dh[:, i, :], ident[0:1, 0:1], start=False, stop=True)
            job_full(m, "bcols")
            project_k(0)
            dense("bbc", cols[:, BSELF:BSELF + 1].broadcast_to([128, 128]),
                  wqkv[:, 0:2, :].rearrange("p a b -> p (a b)"), 2 * D)
            transpose_inputs(1)
            project_q(1)
            project_k(1)
            pe.wait_ge(ld_wv, 32)
            for b in range(HALF):
                project_tok(b)
            four_batches("vp_0", 0, xT, wqkv[:, 2, :])

            def window_scores(b, g):
                u = b * G + g
                if u == 0:
                    pe.wait_ge(max_scores_read, G * NB)
                    pe.wait_ge(scores_read, G * NB)
                    pe.wait_ge(band_ready, 1)
                if b % HALF == 0 and g == 0:
                    pe.wait_ge(stack_in[half_of(b)], 16 * (4 * NSLOT + 1))
                if u >= 4:
                    pe.wait_ge(window_scores_read, u - 3)
                bank = ps[u % 4]
                pe.matmul(bank[:, :], identb[:], bc_mid(bandb[:], 4), start=True, stop=False)
                for j in range(4):
                    h = quad_head(g, j)
                    m = pe.matmul(bank[:, j * T:(j + 1) * T], stacked(Ks, b, h), stacked(Qs, b, h), start=False,
                                  stop=(j == 3))
                m.then_inc(window_scores_full, 1)

            def window_values(b, g):
                u = b * G + g
                pe.wait_ge(window_scores_read, u + 1)
                if g == 0:
                    job_wait_read(pe, f"bv_{half_of(b)}")
                    pe.wait_ge(pv_read, NB + b - 1)
                for j in range(4):
                    m = pe.matmul(VALUE_BANKS[b % 2][32 * j:32 * j + 32, 0:T], v_pad[:, b, quad_head(g, j), :],
                                  P[:, (UNITS + u) % 3, j * T:(j + 1) * T], start=(g == 0), stop=(g == G - 1))
                m.then_inc(pv_done, 1)

            def window_out(b):
                pe.wait_ge(pv_read, NB + b + 1)
                if b == 0:
                    job_wait_read(pe, "wO")
                name = f"y_{b}"
                job_wait_free(pe, name)
                o = bank_of(name)[:, 0:D]
                pe.matmul(o, attnT[:, b * T:(b + 1) * T], wo[:], start=True, stop=False)
                job_full(pe.matmul(o, pv_sb[:, b % 2, 0:T], woT[:], start=False, stop=True), name)

            def by_batch(name, half, lhsT, rhs, n, batches=None):
                job_wait_free(pe, name)
                for i, b in enumerate(batches or range(half * HALF, half * HALF + HALF)):
                    for k in range(len(lhsT)):
                        m = pe.matmul(bank_of(name)[:, i * n:(i + 1) * n], lhsT[k](b), rhs[k], start=(k == 0),
                                      stop=(k == len(lhsT) - 1))
                job_full(m, name)

            tok = lambda src: lambda b: src[:, b * T:(b + 1) * T]
            def transpose_x1(half):
                pe.wait_ge(x1_ready, half + 1)
                transposes(f"x1T_{half}", lambda i: x1[:, half * HALF + i, :], 4)

            def context(half):
                if half == 0:
                    pe.wait_ge(ema_ready, 1)
                by_batch(f"ctxT_{half}", half, [lambda b: x1[:, b, :]], [ema[:, 0, :]], T)

            def hidden(half):
                if half == 0:
                    job_wait_read(pe, "wC1")
                    job_wait_read(pe, "wC2")
                job_wait_read(pe, f"x1T_{half}")
                name = f"h1_{half}"
                job_wait_free(pe, name)
                job_full(pe.matmul(bank_of(name)[0:NH1, :], wn1T[:], x1T[:, half * HT:half * HT + HT],
                                   start=True, stop=True), name)

            def input_gate(half):
                job_wait_read(pe, f"ctxT_{half}")
                by_batch(f"gate_{half}", half, [tok(x1T), tok(ctxT)], [wC[:, 0, :], wC[:, 1, :]], D)

            def modulation(half):
                job_wait_read(pe, f"h1_{half}")
                by_batch(f"mod_{half}", half, [tok(h1T)], [wn2T[:]], ND)

            def soma(half):
                wide(f"soma_{half}", wC[:, 2, :], x1T[:, half * HT:half * HT + HT])

            def traces(b):
                pe.wait_ge(blend_vector, b + 1)
                pe.wait_ge(blend_pool, b + 1)
                if b == 0:
                    pe.wait_ge(window_scores_read, UNITS)
                group = [b in batches for batches in GROUPS].index(True)
                i = b - GROUPS[group][0]
                for d in range(ND):
                    m = pe.matmul(ps[group][:, i * T:(i + 1) * T], Gb[:, b % NG, d, :],
                                  ema[:, 1 + d, :], start=(d == 0), stop=(d == ND - 1))
                m.then_inc(blend_used, 1)

            def gate_of(group):
                pe.wait_ge(traces_read, group + 1)
                cs = tokens_of(GROUPS[group])
                dense(f"tg_{group}", wC[:, 3, :], tempT[:, cs], cs.stop - cs.start)

            def output_of(group):
                pe.wait_ge(gated_soma_ready, group + 1)
                by_batch(f"o_{group}", None, [tok(gateT)], [wC[:, 4, :]], D, GROUPS[group])

            for t in range(TURNS):
                if t < UNITS:
                    scores_max(t // G, t % G)
                if t in TOK_AT:
                    project_tok(TOK_AT[t])
                if t == VP_AT:
                    four_batches("vp_1", 1, xT, wqkv[:, 2, :])
                if t % G == 2:
                    weight_job(t // G)
                u = t - LAG_SCORES
                if 0 <= u < UNITS:
                    scores(u // G, u % G)
                u = t - LAG_VALUES
                if 0 <= u < UNITS:
                    values(u // G, u % G)
                u = t - WINDOW_AT
                if 0 <= u < UNITS:
                    window_scores(u // G, u % G)
                u = t - WINDOW_AT - LAG_WVALUES
                if 0 <= u < UNITS:
                    window_values(u // G, u % G)
                for half in handoff(t, QK):
                    project_window_qk(half)
                for half in handoff(t, VW):
                    project_window_v(half)
                u = t - LAG_PVTR
                if 0 <= u < UNITS and u % G == G - 1:
                    b = u // G
                    pe.wait_ge(pv_read, b + 1)
                    transposes(f"pvtr_{b}", lambda k: pv_sb[:, b % 2, k * 128:(k + 1) * 128], 2)
                u = t - LAG_OUT
                if 0 <= u < UNITS and u % G == G - 1:
                    b = u // G
                    pe.wait_ge(attn_ready, b + 1)
                    transposes(f"attnT_{b}", lambda k: attn[:, b % 2, :], 1)
                for half in handoff(t, Y0):
                    project_window_y(half)
                u = t - WINDOW_AT - LAG_WOUT
                if 0 <= u < UNITS and u % G == G - 1:
                    window_out(u // G)
                if t == FRONT_AT:
                    transpose_x1(0)
                if t == FRONT_AT + 1:
                    context(0)
                if t == FRONT_AT + 2:
                    input_gate(0)
                if t == HIDDEN_AT:
                    hidden(0)

            soma(0)
            modulation(0)
            traces(0)
            transpose_x1(1)
            context(1)
            hidden(1)
            soma(1)
            traces(1)
            modulation(1)
            input_gate(1)
            traces(2)
            for b in range(3, NB):
                traces(b)
                if b == HALF:
                    gate_of(0)
                if b == NB - 2:
                    output_of(0)
                    gate_of(1)

            def transpose_output(half):
                job_wait_read(pe, ("o_0", "o_2")[half])
                transposes(f"oT_{half}", lambda i: o_raw[:, half * HALF + i, :], 4)

            def router_logits(half):
                job_wait_read(pe, f"oT_{half}")
                by_batch(f"lg_{half}", half, [tok(oT)], [wr_g[:]], NE)

            output_of(1)
            gate_of(2)
            transpose_output(0)
            output_of(2)
            transpose_output(1)
            router_logits(0)
            router_logits(1)

            pe.wait_ge(onehot_ready, 1)
            pe.wait_ge(rank_consts, 1)
            job_wait_free(pe, "rank")
            bank = bank_of("rank")
            oh = onehotb[:].rearrange("p b e -> p (b e)")
            W = NB * NE
            pe.matmul(bank[:, 0:W], trib[:], oh[:, W:2 * W], start=True, stop=False)
            for k in range(1, NB):
                pe.matmul(bank[:, 0:W], onesb[:], oh[:, W - k * NE:2 * W - k * NE], start=False, stop=(k == NB - 1))
            for b in range(NB):
                m = pe.matmul(bank[:, W:W + NE], onesb[:], oh[:, W + b * NE:W + (b + 1) * NE], start=(b == 0),
                              stop=(b == NB - 1))
            job_full(m, "rank")

            pe.wait_ge(tmap_ready, 1)
            pe.wait_ge(ld_brow, 16)
            pe.wait_ge(traces_read, 3)
            job_wait_read(pe, "rank")
            for i in range(TILES + 2):
                if i < TILES:
                    pe.wait_ge(zs_in[zs_part(i)], 16)
                    if i >= 2:
                        pe.wait_ge(zT_read, i - 1)
                    pe.transpose(ps[4 + i % 2][:, 0:128], zs[:, i, 0:D], ident[:]).then_inc(zT_full, 1)
                if 1 <= i <= TILES:
                    n = i - 1
                    pe.wait_ge(zT_read, n + 1)
                    pe.wait_ge(w1_ready, n + 1)
                    if n >= 2:
                        pe.wait_ge(h_read, n - 1)
                    for c in range(FC):
                        m = pe.matmul(ps[n % 2][:, c * 128:(c + 1) * 128], W1_tile[:, n % 2, c * 128:(c + 1) * 128],
                                      zsT[:, n % 2, :], start=True, stop=True)
                    m.then_inc(h_full, 1)
                if i >= 2:
                    n = i - 2
                    e = pe.value_load(tmap[0:1, n:n + 1], min_val=0, max_val=NE - 1)
                    pe.wait_ge(h_read, n + 1)
                    if n >= 2:
                        pe.wait_ge(y_read, n - 1)
                    o = ps[6 + n % 2][:, 0:D]
                    pe.matmul(o, onesb[0:KROWS, :], b_rows[:, bass.ds(e, 1), :].rearrange("p a f -> p (a f)"),
                              start=True, stop=False)
                    for c in range(FC):
                        m = pe.matmul(o, hsT[:, n % 2, c * 128:(c + 1) * 128],
                                      W2[:, bass.ds(e, 1), c, :].rearrange("p a f -> p (a f)"), start=False,
                                      stop=(c == FC - 1))
                    m.then_inc(y_full, 1)

        @block.scalar
        def _(act):
            def split_high(name, which, n, bias=None):
                job_wait_full(act, name)
                if n:
                    act.wait_ge(rest_ready, 2 * (n - 1) + which + 1)
                if n >= 2:
                    act.wait_ge(stack_in[n % 2], 16 * 2 * NSLOT)
                bank = bank_of(name)
                add = {} if bias is None else {"bias": bias}
                act.activation(parts[:, n % 2, which, 0, :], bank[:, 0:HT], ACT.Identity, **add).then_inc(high_ready, 1)
                job_read(act.activation(qf[:, which, :], bank[:, 0:HT], ACT.Identity, **add), name)

            def split_middle(which, n):
                act.wait_ge(rest_ready, 2 * n + which + 1)
                act.copy(parts[:, n % 2, which, 1, :], rest[:, which, :]).then_inc(mid_ready, 1)

            job_wait_read(act, "bcols")
            for half in range(2):
                split_high(f"qT_{half}", 0, half, ecols[:, 0:1])
                split_high(f"kT_{half}", 1, half, ecols[:, 1:2])
                split_middle(0, half)
                split_middle(1, half)

            def weights_of(u):
                act.wait_ge(scores_full, u + 1)
                if u >= 3:
                    act.wait_ge(pv_done, u - 2)
                act.activation(P[:, u % 3, :], SCORE_BANKS[u % 2][:, :], ACT.Exp, scale=SCALE).then_inc(scores_read, 1)

            def evac_y0T(half):
                name = f"y0T_{half}"
                job_wait_full(act, name)
                if half == 0:
                    act.wait_ge(ld_wb, 16 * 6)
                job_read(act.activation(y0T[:, half * HT:half * HT + HT], bank_of(name)[:, :], ACT.Identity,
                                        bias=cols[:, BO:BO + 1]), name)

            def split_window_high(half):
                split_high(f"bq_{half}", 0, 2 + half)
                split_high(f"bk_{half}", 1, 2 + half)

            def split_window_middle(half):
                split_middle(0, 2 + half)
                split_middle(1, 2 + half)

            def window_weights(u):
                act.wait_ge(window_scores_full, u + 1)
                act.wait_ge(pv_done, UNITS + u - 2)
                act.activation(P[:, (UNITS + u) % 3, :], ps[u % 4][:, :], ACT.Sigmoid, scale=SCALE).then_inc(window_scores_read, 1)

            def window_pv(b):
                act.wait_ge(pv_done, G * (NB + b + 1))
                if b >= 2:
                    job_wait_full(act, f"y_{b-2}")
                else:
                    job_wait_full(act, f"pvtr_{NB-2+b}")
                act.copy(pv_sb[:, b % 2, 0:T], VALUE_BANKS[b % 2][:, 0:T]).then_inc(pv_read, 1)

            def evac(name, dst, rows=128):
                job_wait_full(act, name)
                job_read(act.copy(dst, bank_of(name)[0:rows, 0:HT]), name)

            cut = lambda buf, half: buf[:, half * HT:half * HT + HT]

            def gelu(name, buf, rows, bias, half):
                job_wait_full(act, name)
                job_read(act.activation(cut(buf, half), bank_of(name)[0:rows, :], ACT.Gelu,
                                        bias=cols[0:rows, bias:bias + 1]), name)

            def gate_sigmoid(half):
                bs = slice(half * HALF, half * HALF + HALF)
                job_wait_read(act, f"gate_{half}")
                act.activation(wgate[:, bs, :], wgate[:, bs, :], ACT.Sigmoid).then_inc(gate_sig, 1)

            def mod_sigmoid(half):
                bs = slice(half * HALF, half * HALF + HALF)
                job_wait_read(act, f"mod_{half}")
                act.activation(mod[:, bs, :], mod[:, bs, :], ACT.Sigmoid).then_inc(mod_sig, 1)

            def token_major(b):
                name = f"tok_{b}"
                job_wait_full(act, name)
                job_read(act.copy(tokA[:, b].rearrange("p a b -> p (a b)"), bank_of(name)[:, 0:3 * D]), name)

            for b in range(HALF):
                token_major(b)
            act.wait_ge(tau_abs, 1)
            act.activation(tau2[:], tau2[:], ACT.Exp, scale=-1.0).then_inc(tau_exp, 1)
            act.wait_ge(tau_exp, 1)
            act.activation(tau2[:], tau2[:], ACT.Ln, bias=1.0).then_inc(tau_exp, 1)
            for t in range(TURNS):
                if t in TOK_AT:
                    token_major(TOK_AT[t])
                if t >= G and t % G == 0 and t <= UNITS:
                    b = t // G - 1
                    act.wait_ge(sshift_ready, b + 1)
                    act.activation(w_self[:, b, :], sshift[:, b, :], ACT.Exp, scale=SCALE).then_inc(wself_ready, 1)
                u = t - LAG_SCORES
                if 0 <= u < UNITS:
                    weights_of(u)
                u = t - LAG_VALUES - 1
                if 0 <= u < UNITS and u % G == G - 1:
                    b = u // G
                    act.wait_ge(pv_done, G * (b + 1))
                    if b >= 2:
                        job_wait_full(act, f"pvtr_{b-2}")
                    act.copy(pv_sb[:, b % 2, :], VALUE_BANKS[b % 2][:, 0:2 * T]).then_inc(pv_read, 1)
                if t == EMA_AT:
                    act.wait_ge(tau_ready, 1)
                    act.wait_ge(diff_ready, 1)
                d = t - EMA_AT
                if 0 <= d <= ND:
                    m = act.activation(ema[:, d, :], diff[:], ACT.Exp, scale=tau2[:, d:d + 1])
                    if d == ND:
                        m.then_inc(ema_exp, 1)
                if t == EMA_AT + 2:
                    act.wait_ge(blend_sub, 1)
                    act.activation(blend[:], blend[:], ACT.Exp).then_inc(blend_exp, 1)
                u = t - WINDOW_AT
                if 0 <= u < UNITS:
                    window_weights(u)
                for half in handoff(t, QK):
                    split_window_high(half)
                for half in handoff(t, QK + 2):
                    split_window_middle(half)
                u = t - LAG_OUT
                if 0 <= u < UNITS and u % G == G - 1:
                    b = u // G
                    job_wait_full(act, f"attnT_{b}")
                    job_read(act.copy(attnT[:, b * T:(b + 1) * T], bank_of(f"attnT_{b}")[:, 0:T]), f"attnT_{b}")
                for half in handoff(t, Y0):
                    evac_y0T(half)
                u = t - WINDOW_AT - LAG_WVALUES - 1
                if 0 <= u < UNITS - 1 and u % G == G - 1:
                    window_pv(u // G)
                if t == FRONT_AT:
                    act.wait_ge(ld_c, 16 * 11)
                    evac("x1T_0", cut(x1T, 0))
                if t == FRONT_AT + 1:
                    evac("ctxT_0", cut(ctxT, 0))
                if t == FRONT_AT + 3:
                    gate_sigmoid(0)
                if t == HIDDEN_AT:
                    gelu("h1_0", h1T, NH1, BN1, 0)

            mod_sigmoid(0)
            evac("x1T_1", cut(x1T, 1))
            evac("ctxT_1", cut(ctxT, 1))
            gelu("h1_1", h1T, NH1, BN1, 1)
            gelu("soma_0", somaT, 128, BSOMA, 0)
            gelu("soma_1", somaT, 128, BSOMA, 1)
            mod_sigmoid(1)
            gate_sigmoid(1)

            def evac_traces(group):
                act.wait_ge(blend_used, GROUPS[group][-1] + 1)
                cs = tokens_of(GROUPS[group])
                act.copy(tempT[:, cs], ps[group][:, 0:cs.stop - cs.start]).then_inc(traces_read, 1)

            def output_gate(group):
                name = f"tg_{group}"
                cs = tokens_of(GROUPS[group])
                job_wait_full(act, name)
                job_read(act.activation(gateT[:, cs], bank_of(name)[:, 0:cs.stop - cs.start], ACT.Sigmoid,
                                        bias=cols[:, BTEMP:BTEMP + 1]), name)

            def evac_output(group):
                name = f"o_{group}"
                batches = GROUPS[group]
                job_wait_full(act, name)
                job_read(act.copy(o_raw[:, batches[0]:batches[-1] + 1, :].rearrange("p b c -> p (b c)"),
                                  bank_of(name)[:, 0:len(batches) * D]), name)

            evac_traces(0)
            output_gate(0)
            evac_traces(1)
            evac_output(0)
            output_gate(1)
            evac_traces(2)
            evac_output(1)
            output_gate(2)
            evac("oT_0", cut(oT, 0))
            evac_output(2)

            def scale_z(half):
                act.wait_ge(shift_ready, half + 1)
                for b in range(half * HALF, half * HALF + HALF):
                    m = act.activation(z[:, b, :], o_raw[:, b, :], ACT.Identity, scale=rstd[:, b:b + 1],
                                       bias=zshift[:, b:b + 1])
                m.then_inc(z_scaled, 1)

            evac("oT_1", cut(oT, 1))
            scale_z(0)
            scale_z(1)
            act.wait_ge(lgm_sub, 1)
            act.activation(gexp[:], gexp[:], ACT.Exp).then_inc(gexp_ready, 1)

            for n in range(TILES):
                act.wait_ge(h_full, n + 1)
                if n >= 2:
                    act.wait_ge(y_full, n - 1)
                for c in range(FC):
                    cs = slice(c * 128, (c + 1) * 128)
                    m = act.activation(hsT[:, n % 2, cs], ps[n % 2][:, cs], ACT.Gelu, bias=b1_tile[:, n % 2, c:c + 1])
                m.then_inc(h_read, 1)

        @block.vector
        def _(dve):
            counts = {}

            def link(ins, s=dve_step):
                counts[id(s)] = counts.get(id(s), 0) + 1
                ins.then_inc(s, 1)
                dve.wait_ge(s, counts[id(s)])

            def link_job(ins, name):
                job_read(ins, name)
                job_wait_read(dve, name)

            def evac_transposes(name, dst):
                job_wait_full(dve, name)
                job_read(dve.tensor_copy(dst, bank_of(name)[:, 0:HT]), name)

            evac_transposes("trS2_0", s2T[:, 0:HT])
            evac_transposes("trX_0", xT[:, 0:HT])
            dve.wait_ge(ld_wa, 16 * 4)
            for i in range(2):
                link(dve.tensor_copy(w_dh[:, i, :].rearrange("p (d h) -> p d h", h=H),
                                     wqkv[:, i, :].rearrange("p (h d) -> p d h", d=DH)), wdh_ready)
                link(dve.tensor_copy(b_dh[:, i, :].rearrange("p (d h) -> p d h", h=H),
                                     bqkv_bc[0:1, i, :].rearrange("p (h d) -> p d h", d=DH)), wdh_ready)

            def v_prev(half):
                name = f"vp_{half}"
                bs = slice(half * HALF, half * HALF + HALF)
                job_wait_full(dve, name)
                dve.wait_ge(vpad_zero, half + 1)
                for b in range(half * HALF, half * HALF + HALF):
                    by_head = lambda ap: ap.rearrange("p (h d) -> p h d", d=DH)
                    src, bias = by_head(bank_of(name)[:, (b % HALF) * D:(b % HALF + 1) * D]), by_head(bqkv_bc[:, 2, :])
                    for odd in range(2):
                        m = dve.tensor_tensor(v_pad[:, b, odd:H:2, 16 * odd:16 * odd + DH], src[:, odd:H:2, :],
                                              bias[:, odd:H:2, :], ALU.add)
                job_read(m, name)

            def split_rest(name, which, n):
                dve.wait_ge(high_ready, 2 * n + which + 1)
                job_wait_read(dve, name)
                if n:
                    dve.wait_ge(mid_ready, 2 * (n - 1) + which + 1)
                link(dve.tensor_tensor(rest[:, which, :], qf[:, which, :], parts[:, n % 2, which, 0, :], ALU.subtract), rest_ready)

            def split_low(which, n):
                dve.wait_ge(mid_ready, 2 * n + which + 1)
                link(dve.tensor_tensor(parts[:, n % 2, which, 2, :], rest[:, which, :], parts[:, n % 2, which, 1, :], ALU.subtract),
                     split_ready)

            def split_both(names, n):
                split_rest(names[0], 0, n)
                split_rest(names[1], 1, n)
                split_low(0, n)
                split_low(1, n)

            dve.wait_ge(ld_wv, 32)
            dve.wait_ge(ld_len, 16)
            link(dve.tensor_copy(len_f[:], len_i[:]))
            dve.wait_ge(pool_pos, 1)
            link(dve.tensor_tensor(pos_row[:], pos_row[:], bc_last(len_f[:], T), ALU.is_ge))
            link(dve.tensor_scalar(mask_row[:], pos_row[:], MASKED, None, ALU.mult), mask_row_ready)

            job_wait_full(dve, "bcols")
            link_job(dve.tensor_copy(ecols[:], bank_of("bcols")[:, 0:2]), "bcols")
            job_wait_full(dve, "bbc")
            qk_bc = bqkv_bc[:, 0:2, :].rearrange("p a b -> p (a b)")
            link_job(dve.tensor_tensor(qk_bc, bank_of("bbc")[:, 0:2 * D], qk_bc, ALU.add), "bbc")
            evac_transposes("trS2_1", s2T[:, HT:2 * HT])
            evac_transposes("trX_1", xT[:, HT:2 * HT])
            split_both(("qT_0", "kT_0"), 0)
            split_both(("qT_1", "kT_1"), 1)

            def self_scores(half):
                bs = slice(half * HALF, half * HALF + HALF)
                dve.wait_ge(prod_ready, half + 1)
                link(dve.tensor_reduce(s_self[:, bs, :], prod[:].rearrange("p b (h d) -> p b h d", d=DH), AX.X, ALU.add), self_ready)

            dve.wait_ge(ld_tau, 32)
            link(dve.scalar_tensor_tensor(tau2[:], tau[:], -1.0, tau[:], ALU.mult, ALU.max), tau_abs)
            link(dve.tensor_scalar(tau[:], tau[:], 0.0, None, ALU.max))

            def row_max(b, g):
                u = b * G + g
                dve.wait_ge(max_scores_full, u + 1)
                dve.tensor_reduce(mx[:, b, 4 * g:4 * g + 4], MAX_BANKS[u % 2][:, :].rearrange("p (j t) -> p j t", j=4),
                                  AX.X, ALU.max).then_inc(max_scores_read, 1)

            def shift(b):
                dve.wait_ge(max_scores_read, G * (b + 1))
                link(dve.tensor_tensor(mx[:, b, :], mx[:, b, :], s_self[:, b, :], ALU.max))
                link(dve.tensor_scalar(negm[:, b, :], mx[:, b, :], -1.0, None, ALU.mult), negm_ready)
                dve.tensor_tensor(sshift[:, b, :], s_self[:, b, :], negm[:, b, :], ALU.add).then_inc(sshift_ready, 1)

            def normalise(b, step):
                name = f"pvtr_{b}"
                k = b % 2
                pvt = bank_of(name)[:, 0:H * 16].rearrange("p (h e) -> p h e", e=16)
                hd = lambda ap: ap.rearrange("p (h d) -> p h d", d=DH)
                if step == 0:
                    dve.wait_ge(wself_ready, b + 1)
                    if b % HALF == 0:
                        dve.wait_ge(tok_biased, half_of(b) + 1)
                    dve.tensor_tensor(hd(wv[:, k, :]), hd(tokA[:, b, 2, :]), bc_last(w_self[:, b, :], DH), ALU.mult)\
                        .then_inc(norm_step, 1)
                    job_wait_full(dve, name)
                    dve.tensor_tensor(den[:, k, :], pvt[:, :, DH], w_self[:, b, :], ALU.add).then_inc(norm_step, 1)
                if step == 1:
                    dve.wait_ge(norm_step, 3 * b + 2)
                    dve.reciprocal(rden[:, k, :], den[:, k, :]).then_inc(norm_step, 1)
                    job_read(dve.tensor_tensor(hd(wv[:, k, :]), pvt[:, :, 0:DH], hd(wv[:, k, :]), ALU.add), name)
                if step == 2:
                    dve.wait_ge(norm_step, 3 * b + 3)
                    job_wait_read(dve, name)
                    dve.tensor_tensor(hd(attn[:, k, :]), hd(wv[:, k, :]), bc_last(rden[:, k, :], DH), ALU.mult)\
                        .then_inc(attn_ready, 1)

            def weight_copies(i):
                if i == 1:
                    job_wait_full(dve, "wB")
                    bank = bank_of("wB")
                    hd, dh = "p (h d) -> p h d", "p (d h) -> p h d"
                    kv = bank[:, 128:384].rearrange("p (h e) -> p h e", e=2 * DH)
                    dve.tensor_copy(wB[:, 0, :].rearrange(dh, d=DH), bank[:, 0:128].rearrange(hd, d=DH))
                    dve.tensor_copy(wB[:, 1, :].rearrange(dh, d=DH), kv[:, :, 0:DH])
                    link_job(dve.tensor_copy(wB[:, 2, :].rearrange(hd, d=DH), kv[:, :, DH:]), "wB")
                if i == 2:
                    job_wait_full(dve, "wO")
                    link_job(dve.tensor_copy(woT[:], bank_of("wO")[:, 0:D]), "wO")
                if i == 2:
                    dve.wait_ge(tau_exp, 2)
                    link(dve.scalar_tensor_tensor(tau2[:], tau[:], -1.0, tau2[:], ALU.mult, ALU.subtract), tau_ready)
                    dve.wait_ge(ld_blend, 16)
                    dve.tensor_reduce(bl_small[:], blend[:].rearrange("p d c -> p c d"), AX.X, ALU.max).then_inc(blend_max, 1)
                if i == 3:
                    job_wait_full(dve, "wC1")
                    link_job(dve.tensor_copy(wC[:, 0:4, :].rearrange("p g c -> p (g c)"), bank_of("wC1")[:, :]), "wC1")
                if i == 6:
                    job_wait_full(dve, "wR")
                    dve.tensor_tensor(br_bc[:], bank_of("wR")[:, NE:2 * NE], br_bc[:], ALU.add)
                    job_read(dve.tensor_tensor(wr_g[:], wr_g[:], bank_of("wR")[:, 0:NE], ALU.subtract), "wR")
                if i == 5:
                    dve.wait_ge(ld_c, 16 * 11)
                    dve.tensor_scalar(wr_g[:], wr[:], gb2[:, 0:1], None, ALU.mult).then_inc(wrg_ready, 1)
                    dve.wait_ge(blend_sum, 1)
                    dve.reciprocal(bl_small[:], bl_small[:]).then_inc(blend_inv, 1)
                if i == 4:
                    job_wait_full(dve, "wC2")
                    bank = bank_of("wC2")
                    dve.tensor_copy(wC[:, 4, :], bank[:, 0:128])
                    dve.tensor_copy(wn1T[:], bank[:, 128:128 + NH1])
                    dve.tensor_copy(wn2T[:], bank[0:NH1, 160:160 + ND])
                    job_read(dve.tensor_copy(b1T[:].rearrange("p e c -> p (e c)"), bank[:, 256:256 + NE * FC]), "wC2")

            def window_v(half):
                name = f"bv_{half}"
                job_wait_full(dve, name)
                dve.wait_ge(vpad_clear, half + 1)
                src = bank_of(name)[:, :].rearrange("p (b h d) -> p b h d", b=HALF, d=DH)
                for g in range(G):
                    m = dve.tensor_copy(v_pad[:, half * HALF:half * HALF + HALF, g:H:G, g * DH:(g + 1) * DH],
                                        src[:, :, g:H:G, :])
                job_read(m, name)

            def statistics(src, b, n):
                dve.bn_stats(stats[:, b, :], src).then_inc(stats_ready, 1)
                dve.wait_ge(stats_ready, n + 1)
                dve.bn_aggr(mv[:, b, :], stats[:, b, :]).then_inc(mv_ready, 1)

            def norm_half(n, buf, half, gamma, into, addend, done):
                bs = slice(half * HALF, half * HALF + HALF)
                dve.wait_ge(rstd_ready, n + 1)
                for b in range(half * HALF, half * HALF + HALF):
                    m = dve.tensor_scalar(buf[:, b, :], buf[:, b, :], mv[:, b, 0:1], rstd[:, b:b + 1],
                                          ALU.subtract, ALU.mult)
                link(m)
                link(dve.tensor_tensor(buf[:, bs, :], buf[:, bs, :], bc_mid(gamma[:], HALF), ALU.mult))
                link(dve.tensor_tensor(into[:, bs, :], buf[:, bs, :], addend, ALU.add), done)

            def residual(b):
                if b == 0:
                    dve.wait_ge(ld_g1, 32)
                    dve.wait_ge(xb_ready, 1)
                name = f"y_{b}"
                job_wait_full(dve, name)
                link_job(dve.tensor_tensor(x1[:, b, :], bank_of(name)[:, 0:D], bo_bc[:], ALU.add), name)
                statistics(x1[:, b, :], b, b)

            def add_norm(half):
                norm_half(half, x1, half, gamma1, x1, xb[:, half * HALF:half * HALF + HALF, :], x1_ready)

            def gate_sums(half):
                name = f"gate_{half}"
                bs = slice(half * HALF, half * HALF + HALF)
                job_wait_full(dve, name)
                job_read(dve.tensor_tensor(wgate[:, bs, :], bank_of(name)[:, :].rearrange("p (b c) -> p b c", b=HALF),
                                           bc_mid(bg_bc[:], HALF), ALU.add), name)

            def mod_sums(half):
                bs = slice(half * HALF, half * HALF + HALF)
                name = f"mod_{half}"
                job_wait_full(dve, name)
                job_read(dve.tensor_tensor(mod[:, bs, :], bank_of(name)[:, 0:HALF * ND].rearrange("p (b c) -> p b c", b=HALF),
                                           bc_mid(bn2_bc[:], HALF), ALU.add), name)

            def gated_inputs(half):
                bs = slice(half * HALF, half * HALF + HALF)
                dve.wait_ge(gate_sig, half + 1)
                dve.tensor_tensor(wgate[:, bs, :], wgate[:, bs, :], x1[:, bs, :], ALU.mult).then_inc(gated_ready, 1)

            def modulate(half):
                bs = slice(half * HALF, half * HALF + HALF)
                dve.wait_ge(mod_sig, half + 1)
                dve.tensor_scalar(mod[:, bs, :], mod[:, bs, :], 0.5, None, ALU.add).then_inc(mod_ready, 1)

            def blended(b):
                if b % HALF == 0:
                    dve.wait_ge(gated_ready, half_of(b) + 1)
                    dve.wait_ge(mod_ready, half_of(b) + 1)
                if b >= NG:
                    dve.wait_ge(blend_used, b - NG + 1)
                for d in range(ND - PD):
                    m = dve.scalar_tensor_tensor(Gb[:, b % NG, d, :], wgate[:, b, :], mod[:, b, d:d + 1],
                                                 blend[:, d, :], ALU.mult, ALU.mult)
                m.then_inc(blend_vector, 1)

            def gated_soma(group):
                cs = tokens_of(GROUPS[group])
                job_wait_read(dve, f"tg_{group}")
                job_wait_read(dve, f"soma_{half_of(GROUPS[group][0])}")
                dve.tensor_tensor(gateT[:, cs], gateT[:, cs], somaT[:, cs], ALU.mult).then_inc(gated_soma_ready, 1)

            for t in range(TURNS + 1):
                if t < UNITS:
                    row_max(t // G, t % G)
                    if t % G == G - 1 and t >= G:
                        shift(t // G)
                if t == 3:
                    self_scores(0)
                if t == G - 1:
                    shift(0)
                if t == G:
                    v_prev(0)
                if t == VP_AT + 1:
                    self_scores(1)
                    v_prev(1)
                if t % G == 3:
                    weight_copies(t // G)
                for half in handoff(t, QK + 1):
                    split_rest(f"bq_{half}", 0, 2 + half)
                    split_rest(f"bk_{half}", 1, 2 + half)
                for half in handoff(t, QK + 2):
                    split_low(0, 2 + half)
                    split_low(1, 2 + half)
                for half in handoff(t, VW + 1):
                    window_v(half)
                for step in range(3):
                    u = t - LAG_PVTR - step
                    if 0 <= u < UNITS and u % G == G - 1:
                        normalise(u // G, step)
                if t == WINDOW_AT + LAG_WVALUES + UNITS:
                    dve.wait_ge(pv_done, G * 2 * NB)
                    dve.wait_ge(pv_read, 2 * NB - 1)
                    job_wait_full(dve, f"y_{NB-3}")
                    dve.tensor_copy(pv_sb[:, (NB - 1) % 2, 0:T], VALUE_BANKS[(NB - 1) % 2][:, 0:T]).then_inc(pv_read, 1)
                u = t - WINDOW_AT - LAG_WOUT - 1
                if 0 <= u < UNITS and u % G == G - 1:
                    residual(u // G)
                    if u // G == HALF - 1:
                        add_norm(0)
                if t == FRONT_AT + 3:
                    dve.wait_ge(ld_c, 16 * 11)
                    gate_sums(0)
                if t == FRONT_AT + 5:
                    gated_inputs(0)

            mod_sums(0)
            modulate(0)
            dve.wait_ge(blend_ready, 1)
            blended(0)
            add_norm(1)
            for b in range(1, NB):
                blended(b)
                if b == 3:
                    mod_sums(1)
                    gate_sums(1)
                    modulate(1)
                    gated_inputs(1)
                if b == HALF + 2:
                    gated_soma(0)

            def statistics_z(group):
                job_wait_read(dve, f"o_{group}")
                for b in GROUPS[group]:
                    statistics(o_raw[:, b, :], b, NB + b)

            statistics_z(0)
            gated_soma(1)
            statistics_z(1)
            statistics_z(2)

            for half in range(2):
                name = f"lg_{half}"
                bs = slice(half * HALF, half * HALF + HALF)
                dve.wait_ge(rstd_ready, (3, 5)[half])
                dve.scalar_tensor_tensor(zshift[:, bs], mv[:, bs, 0], -1.0, rstd[:, bs], ALU.mult, ALU.mult)\
                    .then_inc(shift_ready, 1)
                job_wait_full(dve, name)
                link_job(dve.tensor_tensor(lg[:, bs, :], bank_of(name)[:, 0:HALF * NE].rearrange("p (b c) -> p b c", b=HALF),
                                           bc_last(rstd[:, bs], NE), ALU.mult), name)
            link(dve.tensor_tensor(lg[:], lg[:], bc_mid(br_bc[:], NB), ALU.add))
            dve.wait_ge(rank_consts, 1)
            link(dve.tensor_reduce(lgm[:], lg[:], AX.X, ALU.max))
            dve.tensor_tensor(gexp[:], lg[:], bc_last(lgm[:], NE), ALU.subtract).then_inc(lgm_sub, 1)
            link(dve.tensor_tensor(cand[:], lg[:], bc_last(lgm[:], NE), ALU.is_equal))
            link(dve.tensor_tensor(cand[:], cand[:], bc_mid(em8[:], NB), ALU.mult))
            link(dve.tensor_reduce(emin[:], cand[:], AX.X, ALU.min))
            onehot = onehotb[:, NB:]
            dve.tensor_tensor(onehot, cand[:], bc_last(emin[:], NE), ALU.is_equal).then_inc(onehot_ready, 1)
            job_wait_full(dve, "rank")
            bank = bank_of("rank")
            W = NB * NE
            link(dve.tensor_tensor(cmp[:], bc_last(bank[:, W:W + NE], NB), bc_mid(k128[:], NE), ALU.is_gt))
            link(dve.tensor_reduce(tiles_e[:], cmp[:], AX.X, ALU.add))
            link(dve.tensor_tensor(cmp[:], tri8[:], bc_mid(tiles_e[:], NE), ALU.mult))
            link(dve.tensor_reduce(excl[:], cmp[:], AX.X, ALU.add))
            dve.wait_ge(gexp_ready, 1)
            link(dve.tensor_reduce(gsum[:], gexp[:], AX.X, ALU.add))
            dve.reciprocal(rows[:, :, GATE], gsum[:]).then_inc(gate_ready, 1)
            link_job(dve.scalar_tensor_tensor(cand[:], bc_mid(excl[:], NB), 128.0,
                                              bank[:, 0:W].rearrange("p (b e) -> p b e", e=NE), ALU.mult, ALU.add), "rank")
            link(dve.tensor_tensor(cand[:], cand[:], onehot, ALU.mult))
            link(dve.tensor_reduce(slotf[:], cand[:], AX.X, ALU.add))
            dve.tensor_copy(slot[:], slotf[:]).then_inc(slot_ready, 1)
            link(dve.tensor_tensor(incl[:], excl[:], tiles_e[:], ALU.add))
            link(dve.tensor_tensor(tmap_c[:], bc_mid(incl[0:1, :], TILES), bc_last(tile_no[:], NE), ALU.is_le))
            link(dve.tensor_reduce(tmap_f[:], tmap_c[:], AX.X, ALU.add))
            dve.tensor_scalar(tmap[:], tmap_f[:], float(NE - 1), None, ALU.min).then_inc(tmap_ready, 1)

            dve.wait_ge(ld_f, 32)
            dve.wait_ge(tmap_ready, 1)
            for i in range(TILES + 2):
                if i < TILES:
                    e = dve.value_load(tmap[0:1, i:i + 1], min_val=0, max_val=NE - 1)
                    if i >= 2:
                        dve.wait_ge(h_read, i - 1)
                    dve.tensor_copy(b1_tile[:, i % 2, :], b1T[:, bass.ds(e, 1), :].rearrange("p a f -> p (a f)"))
                    dve.tensor_copy(W1_tile[:, i % 2, :], W1[:, bass.ds(e, 1), :].rearrange("p a f -> p (a f)"))\
                        .then_inc(w1_ready, 1)
                    dve.wait_ge(zT_full, i + 1)
                    dve.tensor_copy(zsT[:, i % 2, :], ps[4 + i % 2][:, 0:128]).then_inc(zT_read, 1)
                if i >= 2:
                    n = i - 2
                    dve.wait_ge(y_full, n + 1)
                    dve.scalar_tensor_tensor(ys[:, n, :], ps[6 + n % 2][:, 0:D], zs[:, n, GATE:GATE + 1],
                                             zs[:, n, D:2 * D], ALU.mult, ALU.add).then_inc(y_read, 1)


_OUTS = [((8, 128, 128), "float32")]


def kernel(**inputs):
    import numpy as _np
    import concourse.bacc as _bacc
    from concourse import mybir as _mybir
    from concourse.bass_utils import run_bass_kernel_spmd as _run

    nc = _bacc.Bacc("TRN2", target_bir_lowering=False, num_devices=1)
    arrays, args = {}, {}
    for name, a in inputs.items():
        a = _np.ascontiguousarray(a)
        if a.ndim == 0:
            a = a.reshape(1)
        arrays[f"in_{name}_dram"] = a
        args[name] = nc.dram_tensor(f"in_{name}_dram", a.shape, _mybir.dt.from_np(a.dtype), kind="ExternalInput").ap()
    shape, dtype = _OUTS[0]
    o = nc.dram_tensor("out_0_dram", shape, _mybir.dt.from_np(_np.dtype(dtype)), kind="ExternalOutput").ap()
    fused_layer(nc, args, o)
    r = _run(nc, [arrays], core_ids=[0])
    return r.results[0]["out_0_dram"]
```
